# Optimizing a Trainium2 kernel written in Bass

```python
import numpy as np
import jax
import jax.numpy as jnp

def _softmax(x, axis=-1):
    return jax.nn.softmax(x, axis=axis)

def _gelu(x):
    return jax.nn.gelu(x, approximate=True)

def _silu(x):
    return jax.nn.silu(x)

def _sigmoid(x):
    return jax.nn.sigmoid(x)

def _layernorm(x, axis=-1, eps=1e-05):
    m = jnp.mean(x, axis=axis, keepdims=True)
    v = jnp.var(x, axis=axis, keepdims=True)
    return (x - m) / jnp.sqrt(v + eps)

def _scatter_add(tgt, idx, src, axis=0):
    return tgt.at[idx].add(src)

def _segment_sum(src, seg, n):
    return jax.ops.segment_sum(src, seg, n)
kernel_name = 'mk_gnn_preln_d4_gnn_r8_cff2d5'

def setup_inputs(seed: int=0):
    np.random.seed(seed)
    _w = jnp.asarray

    def _rec_inputs():
        import jax
        import jax.numpy as jnp
        _gk = jax.random.key(seed)
        x = -0.001003 + 1 * jax.random.normal(jax.random.fold_in(_gk, 1), (256, 768), jnp.float32)
        _s = jax.random.randint(jax.random.fold_in(_gk, 2), (4096,), 0, 256, jnp.int32)
        _d = jax.random.randint(jax.random.fold_in(_gk, 3), (4096,), 0, 256, jnp.int32)
        _loop = jnp.arange(256, dtype=jnp.int32)
        src = jnp.concatenate([_s, _d, _loop])
        dst = jnp.concatenate([_d, _s, _loop])
        _o = jnp.argsort(dst, stable=True)
        src = src[_o]
        dst = dst[_o]
        edge_attr_32 = 0.000376506 + 0.999991 * jax.random.normal(jax.random.fold_in(_gk, 11), (8448, 32), jnp.float32)
        edge_type_3 = jax.random.randint(jax.random.fold_in(_gk, 13), (8448,), 0, 3, jnp.int32)
        node_type_6 = jax.random.randint(jax.random.fold_in(_gk, 14), (256,), 0, 6, jnp.int32)
        return (x, src, dst, edge_attr_32, edge_type_3, node_type_6)
    x, src, dst, edge_attr_32, edge_type_3, node_type_6 = _rec_inputs()

    def _L0_gnn_setup():
        import jax, jax.numpy as jnp
        import numpy as np
        NUM_RELATIONS = 3

        def _rgcn(x, W_rel, W_root, bias, src, dst, etype):
            n = x.shape[0]
            xr = jnp.einsum('ni,rio->rno', x, W_rel)
            msg = xr[etype, src]
            out = x @ W_root + bias
            for r in range(NUM_RELATIONS):
                m = etype == r
                s = jax.ops.segment_sum(jnp.where(m[:, None], msg, 0.0), dst, num_segments=n)
                c = jax.ops.segment_sum(m.astype(x.dtype), dst, num_segments=n)
                out = out + s / jnp.maximum(c, 1.0)[:, None]
            return out

        def _gate(h, q, Wg, bg, Wq, bq):
            B, L, F = q.shape
            N = h.shape[0] // B
            h3 = h.reshape(B, N, F)
            hg = jnp.einsum('bnf,gf->bng', h3, Wg[:, :F])
            qg = jnp.einsum('blf,gf->blg', q, Wg[:, F:]) + bg
            attn = jax.nn.sigmoid(hg[:, :, None, :] + qg[:, None, :, :])
            qi = jnp.einsum('bnlf,blf->bnf', attn, q)
            alpha = jax.nn.sigmoid(jnp.einsum('bnf,gf->bng', h3, Wq[:, :F]) + jnp.einsum('bnf,gf->bng', qi, Wq[:, F:]) + bq)
            hn = alpha * jnp.tanh(qi) + (1.0 - alpha) * h3
            return hn.reshape(B * N, F)
        key = jax.random.key(seed)
        ks = jax.random.split(key, 16)
        F = 768
        BN, E, B, L = (256, 8192, 8, 64)
        s = 0.02
        return {'x': jax.random.normal(ks[0], (BN, F), jnp.float32), 'edge_index': jax.random.randint(ks[1], (2, E), 0, BN), 'edge_type': jax.random.randint(ks[2], (E,), 0, NUM_RELATIONS), 'query_embs': jax.random.normal(ks[3], (B, L, F), jnp.float32), 'W_rel1': jax.random.normal(ks[4], (NUM_RELATIONS, F, F), jnp.float32) * s, 'W_root1': jax.random.normal(ks[5], (F, F), jnp.float32) * s, 'b1': jnp.zeros((F,), jnp.float32), 'W_rel2': jax.random.normal(ks[6], (NUM_RELATIONS, F, F), jnp.float32) * s, 'W_root2': jax.random.normal(ks[7], (F, F), jnp.float32) * s, 'b2': jnp.zeros((F,), jnp.float32), 'Wg': jax.random.normal(ks[8], (F, 2 * F), jnp.float32) * s, 'bg': jnp.zeros((F,), jnp.float32), 'Wq': jax.random.normal(ks[9], (F, 2 * F), jnp.float32) * s, 'bq': jnp.zeros((F,), jnp.float32)}
    _L0_gnn_all = _L0_gnn_setup()
    _L0_gnn_in = {k: v for k, v in _L0_gnn_all.items() if k in ('query_embs', 'W_rel1', 'W_root1', 'b1', 'W_rel2', 'W_root2', 'b2', 'Wg', 'bg', 'Wq', 'bq')}
    del _L0_gnn_all

    def _L1_gnn_setup():
        import jax, jax.numpy as jnp
        import numpy as np
        N_NODES = 1250
        N_EDGES = 12500
        DIM = 768
        NEG_SLOPE = 0.2

        def gat_conv(x, src, dst, W, att_src, att_dst, bias, num_nodes):
            h = x @ W
            a_s = h @ att_src
            a_d = h @ att_dst
            e = jax.nn.leaky_relu(a_s[src] + a_d[dst], NEG_SLOPE)
            m = jax.ops.segment_max(e, dst, num_segments=num_nodes)
            e = jnp.exp(e - m[dst])
            denom = jax.ops.segment_sum(e, dst, num_segments=num_nodes)
            alpha = e / denom[dst]
            msg = alpha[:, None] * h[src]
            out = jax.ops.segment_sum(msg, dst, num_segments=num_nodes)
            return out + bias
        key = jax.random.key(seed)
        ks = jax.random.split(key, 12)
        s = 1.0 / np.sqrt(DIM)
        inp = {'x': jax.random.normal(ks[0], (N_NODES, DIM), dtype=jnp.float32), 'edge_index': jax.random.randint(ks[1], (2, N_EDGES), 0, N_NODES, dtype=jnp.int64), 'W1': jax.random.normal(ks[2], (DIM, DIM), dtype=jnp.float32) * s, 'att_src1': jax.random.normal(ks[3], (DIM,), dtype=jnp.float32) * s, 'att_dst1': jax.random.normal(ks[4], (DIM,), dtype=jnp.float32) * s, 'b1': jnp.zeros((DIM,), dtype=jnp.float32), 'W2': jax.random.normal(ks[5], (DIM, DIM), dtype=jnp.float32) * s, 'att_src2': jax.random.normal(ks[6], (DIM,), dtype=jnp.float32) * s, 'att_dst2': jax.random.normal(ks[7], (DIM,), dtype=jnp.float32) * s, 'b2': jnp.zeros((DIM,), dtype=jnp.float32)}
        return inp
    _L1_gnn_all = _L1_gnn_setup()
    _L1_gnn_in = {k: v for k, v in _L1_gnn_all.items() if k in ('W1', 'att_src1', 'att_dst1', 'b1', 'W2', 'att_src2', 'att_dst2', 'b2')}
    del _L1_gnn_all

    def _L2_gnn_setup():
        import jax, jax.numpy as jnp
        import numpy as np
        NEG_SLOPE = 0.2
        EPS = 1e-16
        N_NODES = 4096
        N_EDGES = 20000
        DIM = 768
        HEADS1 = 4
        OUT1 = DIM // HEADS1
        HEADS2 = 1
        OUT2 = DIM
        N_REL = 3

        def rgat_conv(x, W, q, k, b, src, dst, etype, heads, out_ch, n_nodes):
            xr = jnp.einsum('nd,rdf->rnf', x, W)
            oi = xr[etype, dst]
            oj = xr[etype, src]
            qi = oi @ q
            kj = oj @ k
            alpha = jax.nn.leaky_relu(qi + kj, NEG_SLOPE)
            m = jax.ops.segment_max(alpha, dst, num_segments=n_nodes)
            e = jnp.exp(alpha - m[dst])
            z = jax.ops.segment_sum(e, dst, num_segments=n_nodes)
            a = e / (z[dst] + EPS)
            msg = (a[:, :, None] * oj.reshape(-1, heads, out_ch)).reshape(-1, heads * out_ch)
            out = jax.ops.segment_sum(msg, dst, num_segments=n_nodes)
            return out + b
        key = jax.random.key(seed)
        ks = jax.random.split(key, 12)
        s = 0.02
        return {'x': jax.random.normal(ks[0], (N_NODES, DIM), dtype=jnp.float32), 'edge_index': jax.random.randint(ks[1], (2, N_EDGES), 0, N_NODES, dtype=jnp.int64), 'edge_type': jax.random.randint(ks[2], (N_EDGES,), 0, N_REL, dtype=jnp.int64), 'W1': jax.random.normal(ks[3], (N_REL, DIM, HEADS1 * OUT1), dtype=jnp.float32) * s, 'q1': jax.random.normal(ks[4], (HEADS1 * OUT1, HEADS1), dtype=jnp.float32) * s, 'k1': jax.random.normal(ks[5], (HEADS1 * OUT1, HEADS1), dtype=jnp.float32) * s, 'b1': jnp.zeros((HEADS1 * OUT1,), dtype=jnp.float32), 'W2': jax.random.normal(ks[6], (N_REL, DIM, HEADS2 * OUT2), dtype=jnp.float32) * s, 'q2': jax.random.normal(ks[7], (HEADS2 * OUT2, HEADS2), dtype=jnp.float32) * s, 'k2': jax.random.normal(ks[8], (HEADS2 * OUT2, HEADS2), dtype=jnp.float32) * s, 'b2': jnp.zeros((HEADS2 * OUT2,), dtype=jnp.float32)}
    _L2_gnn_all = _L2_gnn_setup()
    _L2_gnn_in = {k: v for k, v in _L2_gnn_all.items() if k in ('W1', 'q1', 'k1', 'b1', 'W2', 'q2', 'k2', 'b2')}
    del _L2_gnn_all

    def _L3_gnn_setup():
        import jax, jax.numpy as jnp
        import numpy as np
        N, E, D, T, EA = (6250, 16384, 768, 6, 32)
        H4 = D // 4
        EPS = 1e-05
        key = jax.random.key(seed)
        ks = jax.random.split(key, 24)

        def init(k, shape, fan_in):
            return (jax.random.normal(k, shape, jnp.float32) / np.sqrt(fan_in)).astype(jnp.float32)
        inp = {'x': jax.random.normal(ks[0], (N, D), jnp.float32), 'edge_index': jax.random.randint(ks[1], (2, E), 0, N, jnp.int64), 'edge_attr': jax.random.normal(ks[2], (E, EA), jnp.float32), 'node_types': jax.random.randint(ks[3], (N,), 0, T, jnp.int64), 'W_type': init(ks[4], (T, D, D), D), 'b_type': jnp.zeros((T, D), jnp.float32), 'msg_W1': init(ks[5], (2 * D, D), 2 * D), 'msg_b1': jnp.zeros((D,), jnp.float32), 'msg_W2': init(ks[6], (D, D), D), 'msg_b2': jnp.zeros((D,), jnp.float32), 'edge_W1': init(ks[7], (EA, H4), EA), 'edge_b1': jnp.zeros((H4,), jnp.float32), 'edge_W2': init(ks[8], (H4, 1), H4), 'edge_b2': jnp.zeros((1,), jnp.float32), 'agg_W1': init(ks[9], (D, D), D), 'agg_b1': jnp.zeros((D,), jnp.float32), 'agg_W2': init(ks[10], (D, D), D), 'agg_b2': jnp.zeros((D,), jnp.float32), 'out_W': init(ks[11], (D, D), D), 'out_b': jnp.zeros((D,), jnp.float32), 'ln_g': jnp.ones((D,), jnp.float32), 'ln_b': jnp.zeros((D,), jnp.float32)}
        return inp
    _L3_gnn_all = _L3_gnn_setup()
    _L3_gnn_in = {k: v for k, v in _L3_gnn_all.items() if k in ('W_type', 'b_type', 'msg_W1', 'msg_b1', 'msg_W2', 'msg_b2', 'edge_W1', 'edge_b1', 'edge_W2', 'edge_b2', 'agg_W1', 'agg_b1', 'agg_W2', 'agg_b2', 'out_W', 'out_b', 'ln_g', 'ln_b')}
    del _L3_gnn_all
    return {'x': x, 'src': src, 'dst': dst, 'edge_attr_32': edge_attr_32, 'edge_type_3': edge_type_3, 'node_type_6': node_type_6, 'L0_gnn_query_embs': _L0_gnn_in['query_embs'], 'L0_gnn_W_rel1': _L0_gnn_in['W_rel1'], 'L0_gnn_W_root1': _L0_gnn_in['W_root1'], 'L0_gnn_b1': _L0_gnn_in['b1'], 'L0_gnn_W_rel2': _L0_gnn_in['W_rel2'], 'L0_gnn_W_root2': _L0_gnn_in['W_root2'], 'L0_gnn_b2': _L0_gnn_in['b2'], 'L0_gnn_Wg': _L0_gnn_in['Wg'], 'L0_gnn_bg': _L0_gnn_in['bg'], 'L0_gnn_Wq': _L0_gnn_in['Wq'], 'L0_gnn_bq': _L0_gnn_in['bq'], 'L1_gnn_W1': _L1_gnn_in['W1'], 'L1_gnn_att_src1': _L1_gnn_in['att_src1'], 'L1_gnn_att_dst1': _L1_gnn_in['att_dst1'], 'L1_gnn_b1': _L1_gnn_in['b1'], 'L1_gnn_W2': _L1_gnn_in['W2'], 'L1_gnn_att_src2': _L1_gnn_in['att_src2'], 'L1_gnn_att_dst2': _L1_gnn_in['att_dst2'], 'L1_gnn_b2': _L1_gnn_in['b2'], 'L2_gnn_W1': _L2_gnn_in['W1'], 'L2_gnn_q1': _L2_gnn_in['q1'], 'L2_gnn_k1': _L2_gnn_in['k1'], 'L2_gnn_b1': _L2_gnn_in['b1'], 'L2_gnn_W2': _L2_gnn_in['W2'], 'L2_gnn_q2': _L2_gnn_in['q2'], 'L2_gnn_k2': _L2_gnn_in['k2'], 'L2_gnn_b2': _L2_gnn_in['b2'], 'L3_gnn_W_type': _L3_gnn_in['W_type'], 'L3_gnn_b_type': _L3_gnn_in['b_type'], 'L3_gnn_msg_W1': _L3_gnn_in['msg_W1'], 'L3_gnn_msg_b1': _L3_gnn_in['msg_b1'], 'L3_gnn_msg_W2': _L3_gnn_in['msg_W2'], 'L3_gnn_msg_b2': _L3_gnn_in['msg_b2'], 'L3_gnn_edge_W1': _L3_gnn_in['edge_W1'], 'L3_gnn_edge_b1': _L3_gnn_in['edge_b1'], 'L3_gnn_edge_W2': _L3_gnn_in['edge_W2'], 'L3_gnn_edge_b2': _L3_gnn_in['edge_b2'], 'L3_gnn_agg_W1': _L3_gnn_in['agg_W1'], 'L3_gnn_agg_b1': _L3_gnn_in['agg_b1'], 'L3_gnn_agg_W2': _L3_gnn_in['agg_W2'], 'L3_gnn_agg_b2': _L3_gnn_in['agg_b2'], 'L3_gnn_out_W': _L3_gnn_in['out_W'], 'L3_gnn_out_b': _L3_gnn_in['out_b'], 'L3_gnn_ln_g': _L3_gnn_in['ln_g'], 'L3_gnn_ln_b': _L3_gnn_in['ln_b']}

def reference(x, src, dst, edge_attr_32, edge_type_3, node_type_6, L0_gnn_query_embs, L0_gnn_W_rel1, L0_gnn_W_root1, L0_gnn_b1, L0_gnn_W_rel2, L0_gnn_W_root2, L0_gnn_b2, L0_gnn_Wg, L0_gnn_bg, L0_gnn_Wq, L0_gnn_bq, L1_gnn_W1, L1_gnn_att_src1, L1_gnn_att_dst1, L1_gnn_b1, L1_gnn_W2, L1_gnn_att_src2, L1_gnn_att_dst2, L1_gnn_b2, L2_gnn_W1, L2_gnn_q1, L2_gnn_k1, L2_gnn_b1, L2_gnn_W2, L2_gnn_q2, L2_gnn_k2, L2_gnn_b2, L3_gnn_W_type, L3_gnn_b_type, L3_gnn_msg_W1, L3_gnn_msg_b1, L3_gnn_msg_W2, L3_gnn_msg_b2, L3_gnn_edge_W1, L3_gnn_edge_b1, L3_gnn_edge_W2, L3_gnn_edge_b2, L3_gnn_agg_W1, L3_gnn_agg_b1, L3_gnn_agg_W2, L3_gnn_agg_b2, L3_gnn_out_W, L3_gnn_out_b, L3_gnn_ln_g, L3_gnn_ln_b):
    import jax
    import jax.numpy as jnp

    def _L0_gnn_ref(x, edge_index, edge_type, query_embs, W_rel1, W_root1, b1, W_rel2, W_root2, b2, Wg, bg, Wq, bq):
        import jax, jax.numpy as jnp
        import numpy as np
        NUM_RELATIONS = 3

        def _rgcn(x, W_rel, W_root, bias, src, dst, etype):
            n = x.shape[0]
            xr = jnp.einsum('ni,rio->rno', x, W_rel)
            msg = xr[etype, src]
            out = x @ W_root + bias
            for r in range(NUM_RELATIONS):
                m = etype == r
                s = jax.ops.segment_sum(jnp.where(m[:, None], msg, 0.0), dst, num_segments=n)
                c = jax.ops.segment_sum(m.astype(x.dtype), dst, num_segments=n)
                out = out + s / jnp.maximum(c, 1.0)[:, None]
            return out

        def _gate(h, q, Wg, bg, Wq, bq):
            B, L, F = q.shape
            N = h.shape[0] // B
            h3 = h.reshape(B, N, F)
            hg = jnp.einsum('bnf,gf->bng', h3, Wg[:, :F])
            qg = jnp.einsum('blf,gf->blg', q, Wg[:, F:]) + bg
            attn = jax.nn.sigmoid(hg[:, :, None, :] + qg[:, None, :, :])
            qi = jnp.einsum('bnlf,blf->bnf', attn, q)
            alpha = jax.nn.sigmoid(jnp.einsum('bnf,gf->bng', h3, Wq[:, :F]) + jnp.einsum('bnf,gf->bng', qi, Wq[:, F:]) + bq)
            hn = alpha * jnp.tanh(qi) + (1.0 - alpha) * h3
            return hn.reshape(B * N, F)
        src, dst = (edge_index[0], edge_index[1])
        h = jax.nn.relu(_rgcn(x, W_rel1, W_root1, b1, src, dst, edge_type))
        h = _gate(h, query_embs, Wg, bg, Wq, bq)
        h = jax.nn.relu(_rgcn(h, W_rel2, W_root2, b2, src, dst, edge_type))
        h = _gate(h, query_embs, Wg, bg, Wq, bq)
        return h

    def _L1_gnn_ref(x, edge_index, W1, att_src1, att_dst1, b1, W2, att_src2, att_dst2, b2):
        import jax, jax.numpy as jnp
        import numpy as np
        N_NODES = 1250
        N_EDGES = 12500
        DIM = 768
        NEG_SLOPE = 0.2

        def gat_conv(x, src, dst, W, att_src, att_dst, bias, num_nodes):
            h = x @ W
            a_s = h @ att_src
            a_d = h @ att_dst
            e = jax.nn.leaky_relu(a_s[src] + a_d[dst], NEG_SLOPE)
            m = jax.ops.segment_max(e, dst, num_segments=num_nodes)
            e = jnp.exp(e - m[dst])
            denom = jax.ops.segment_sum(e, dst, num_segments=num_nodes)
            alpha = e / denom[dst]
            msg = alpha[:, None] * h[src]
            out = jax.ops.segment_sum(msg, dst, num_segments=num_nodes)
            return out + bias
        n = x.shape[0]
        loops = jnp.arange(n, dtype=edge_index.dtype)
        src = jnp.concatenate([edge_index[0], loops])
        dst = jnp.concatenate([edge_index[1], loops])
        h = gat_conv(x, src, dst, W1, att_src1, att_dst1, b1, n)
        h = jax.nn.relu(h)
        out = gat_conv(h, src, dst, W2, att_src2, att_dst2, b2, n)
        return out

    def _L2_gnn_ref(x, edge_index, edge_type, W1, q1, k1, b1, W2, q2, k2, b2):
        import jax, jax.numpy as jnp
        import numpy as np
        NEG_SLOPE = 0.2
        EPS = 1e-16
        N_NODES = 4096
        N_EDGES = 20000
        DIM = 768
        HEADS1 = 4
        OUT1 = DIM // HEADS1
        HEADS2 = 1
        OUT2 = DIM
        N_REL = 3

        def rgat_conv(x, W, q, k, b, src, dst, etype, heads, out_ch, n_nodes):
            xr = jnp.einsum('nd,rdf->rnf', x, W)
            oi = xr[etype, dst]
            oj = xr[etype, src]
            qi = oi @ q
            kj = oj @ k
            alpha = jax.nn.leaky_relu(qi + kj, NEG_SLOPE)
            m = jax.ops.segment_max(alpha, dst, num_segments=n_nodes)
            e = jnp.exp(alpha - m[dst])
            z = jax.ops.segment_sum(e, dst, num_segments=n_nodes)
            a = e / (z[dst] + EPS)
            msg = (a[:, :, None] * oj.reshape(-1, heads, out_ch)).reshape(-1, heads * out_ch)
            out = jax.ops.segment_sum(msg, dst, num_segments=n_nodes)
            return out + b
        src, dst = (edge_index[0], edge_index[1])
        n = x.shape[0]
        h = rgat_conv(x, W1, q1, k1, b1, src, dst, edge_type, HEADS1, OUT1, n)
        h = jax.nn.elu(h)
        out = rgat_conv(h, W2, q2, k2, b2, src, dst, edge_type, HEADS2, OUT2, n)
        return out

    def _L3_gnn_ref(x, edge_index, edge_attr, node_types, W_type, b_type, msg_W1, msg_b1, msg_W2, msg_b2, edge_W1, edge_b1, edge_W2, edge_b2, agg_W1, agg_b1, agg_W2, agg_b2, out_W, out_b, ln_g, ln_b):
        import jax, jax.numpy as jnp
        import numpy as np
        N, E, D, T, EA = (6250, 16384, 768, 6, 32)
        H4 = D // 4
        EPS = 1e-05
        n = x.shape[0]
        all_h = jnp.einsum('ni,tio->tno', x, W_type)
        h = jnp.take_along_axis(all_h, node_types[None, :, None], axis=0)[0]
        h = h + b_type[node_types]
        row, col = (edge_index[0], edge_index[1])
        m_in = jnp.concatenate([h[row], h[col]], axis=1)
        m = jax.nn.relu(m_in @ msg_W1 + msg_b1) @ msg_W2 + msg_b2
        ew = jax.nn.sigmoid(jax.nn.relu(edge_attr @ edge_W1 + edge_b1) @ edge_W2 + edge_b2)
        m = m * ew
        agg = jax.ops.segment_sum(m, col, num_segments=n)
        agg = jax.nn.relu(agg @ agg_W1 + agg_b1) @ agg_W2 + agg_b2
        h = h + agg
        h = h @ out_W + out_b
        h = h + x
        mu = jnp.mean(h, axis=-1, keepdims=True)
        var = jnp.mean(jnp.square(h - mu), axis=-1, keepdims=True)
        h = (h - mu) * jax.lax.rsqrt(var + EPS) * ln_g + ln_b
        return h
    edge_index = jnp.stack([src, dst])
    h = jnp.maximum(_layernorm(x, axis=-1), 0.0)
    x = x + _L0_gnn_ref(h, edge_index, edge_type_3, L0_gnn_query_embs, L0_gnn_W_rel1, L0_gnn_W_root1, L0_gnn_b1, L0_gnn_W_rel2, L0_gnn_W_root2, L0_gnn_b2, L0_gnn_Wg, L0_gnn_bg, L0_gnn_Wq, L0_gnn_bq)
    h = jnp.maximum(_layernorm(x, axis=-1), 0.0)
    x = x + _L1_gnn_ref(h, edge_index, L1_gnn_W1, L1_gnn_att_src1, L1_gnn_att_dst1, L1_gnn_b1, L1_gnn_W2, L1_gnn_att_src2, L1_gnn_att_dst2, L1_gnn_b2)
    h = jnp.maximum(_layernorm(x, axis=-1), 0.0)
    x = x + _L2_gnn_ref(h, edge_index, edge_type_3, L2_gnn_W1, L2_gnn_q1, L2_gnn_k1, L2_gnn_b1, L2_gnn_W2, L2_gnn_q2, L2_gnn_k2, L2_gnn_b2)
    h = jnp.maximum(_layernorm(x, axis=-1), 0.0)
    x = x + _L3_gnn_ref(h, edge_index, edge_attr_32, node_type_6, L3_gnn_W_type, L3_gnn_b_type, L3_gnn_msg_W1, L3_gnn_msg_b1, L3_gnn_msg_W2, L3_gnn_msg_b2, L3_gnn_edge_W1, L3_gnn_edge_b1, L3_gnn_edge_W2, L3_gnn_edge_b2, L3_gnn_agg_W1, L3_gnn_agg_b1, L3_gnn_agg_W2, L3_gnn_agg_b2, L3_gnn_out_W, L3_gnn_out_b, L3_gnn_ln_g, L3_gnn_ln_b)
    return x

_drawn_inputs = setup_inputs


def setup_inputs(seed=0):
    import zlib

    import numpy as np

    out = dict(_drawn_inputs(seed))
    spreads = {'L0_gnn_b1': (0.0, 0.636),
     'L0_gnn_b2': (0.0, 0.1),
     'L0_gnn_bg': (0.0, 0.527),
     'L0_gnn_bq': (0.0, 0.669),
     'L1_gnn_b1': (0.0, 0.1),
     'L1_gnn_b2': (0.0, 0.1),
     'L2_gnn_b1': (0.0, 0.352),
     'L2_gnn_b2': (0.0, 0.1),
     'L3_gnn_b_type': (0.0, 0.1),
     'L3_gnn_msg_b1': (0.0, 0.1),
     'L3_gnn_msg_b2': (0.0, 0.1),
     'L3_gnn_edge_b1': (0.0, 2.0),
     'L3_gnn_agg_b1': (0.0, 0.8),
     'L3_gnn_agg_b2': (0.0, 0.652),
     'L3_gnn_out_b': (0.0, 0.618),
     'L3_gnn_ln_g': (1.0, 0.2),
     'L3_gnn_ln_b': (0.0, 0.1)}
    factors = {'L1_gnn_att_src1': 3.783,
     'L1_gnn_att_dst1': 24.355,
     'L1_gnn_att_src2': 8.0,
     'L1_gnn_att_dst2': 64.0,
     'L2_gnn_q1': 29.927,
     'L2_gnn_k1': 29.033,
     'L2_gnn_q2': 24.98,
     'L2_gnn_k2': 64.0,
     'L3_gnn_edge_W1': 2.685}
    for name, (base, spread) in spreads.items():
        noise = np.random.default_rng([zlib.crc32(name.encode()), seed]).standard_normal(out[name].shape)
        drawn = base * np.exp(spread * noise) if base else spread * noise
        out[name] = jnp.asarray(drawn.astype(out[name].dtype))
    for name, factor in factors.items():
        out[name] = (out[name] * factor).astype(out[name].dtype)
    return out
```

```python
from contextlib import ExitStack

import numpy as np
import concourse.bass as bass
from concourse import mybir

F32 = mybir.dt.float32
F32R = mybir.dt.float32r
BF16 = mybir.dt.bfloat16
I32 = mybir.dt.int32
ALU = mybir.AluOpType
ACT = mybir.ActivationFunctionType

N, D, E, EA, H4, NREL, NTYPE = 256, 768, 8448, 32, 192, 3, 6
P = 128
NT = N // P
KB = D // P
HALF = D // 2
B, L, NB = 8, 64, N // 8
PAIRS = NB // 4
HL = L // 2
PIECES = 3
TILES = E // P
GROUP = 3
STEPS = TILES // (2 * GROUP)
HEADS1 = 4
SLOPE = 0.2
LN_EPS = 1e-5
Z_EPS = 1e-16
NO_EDGE = -1e30

UNITS = (["qg0", "qg1"]
         + [f"{l}.{w}" for l in "ab" for w in ("rel0", "rel1", "rel2", "root", "hg", "al1", "al2")]
         + ["gat1.0", "gat2.0", "rgat1.0", "rgat1.1", "rgat1.2", "rgat2.0", "rgat2.1", "rgat2.2"]
         + [f"ty{t}" for t in range(NTYPE)] + ["msgA", "msgB", "msg2", "agg1", "agg2", "out"])


def attention_jobs(name, rels, heads):
    jobs = [f"T.{name}"] + [f"{name}.{r}" for r in range(rels)] + [f"{name}.row0"]
    for h in range(heads):
        jobs += [f"{name}.row{h + 1}"] * (h + 1 < heads) + [f"{name}.pt{h}", f"{name}.sum{h}"]
    return jobs


ATT = {"gat1": (1, 1), "gat2": (1, 1), "rgat1": (NREL, HEADS1), "rgat2": (NREL, 1)}
JOBS = (["T.a", "counts", "countT", "countrow", "qg0", "qg1"]
        + ["a.rel0", "a.rel1", "a.rel2", "a.root", "T.a.h", "a.hg", "T.a.qi", "a.al"]
        + ["T.b", "b.rel0", "b.rel1", "b.rel2", "b.root", "T.b.h", "b.hg", "T.b.qi", "b.al"]
        + [j for n, (r, h) in ATT.items() for j in attention_jobs(n, r, h)]
        + ["T.m", "m.h", "T.m.h", "msgA", "msgB", "edges",
           "T.agg", "msg2", "T.msg2", "agg1", "T.agg1", "agg2", "T.agg2", "out"])


def unit(name):
    return UNITS.index(name)


def job(name):
    return JOBS.index(name)


def ends_with(name):
    if name.endswith(".al"):
        return name + "2"
    return {"m.h": f"ty{NTYPE - 1}"}.get(name, name if name in UNITS and not name.endswith("root") else None)


def readers(name):
    if ".row" in name and name != "countrow" or ".pt" in name:
        return (True, False)
    if ".sum" in name or name in ("countrow", "msg2", "agg2", "out"):
        return (False, True)
    return (True, True)


def taken(name, who):
    return sum(readers(n)[who] for n in JOBS[:job(name) + 1])


BIASES = ["b1", "b2", "bg", "bq", "msg_b1", "agg_b1", "agg_b2", "out_b"]
TYPE_ROW = 32
ATTVEC = 2 * HEADS1
C_PAT, C_SEL = 0, PAIRS * P
C_ID = C_SEL + len(BIASES) * P
C_RED = C_ID + P
C_IOTA = C_RED + PAIRS * 32
C_NODE = C_IOTA + NREL * N
C_TYPE = C_NODE + NT
C_END = C_TYPE + 1


def constants():
    c = np.zeros((P, C_END), np.float32)
    p = np.arange(P)
    col = np.arange(P)
    for j in range(PAIRS):
        node = (p[:, None] < 64) & (p[:, None] % 32 == 4 * j + col[None] // 32)
        query = (p[:, None] >= 64) & (p[:, None] % 32 == col[None] % 32)
        c[:, C_PAT + j * P:C_PAT + (j + 1) * P] = node | query
        c[:, C_RED + j * 32:C_RED + (j + 1) * 32] = np.arange(32)[None] == 4 * j + p[:, None] // 32
    for i in range(len(BIASES)):
        c[:, C_SEL + i * P:C_SEL + (i + 1) * P] = (p % 64 == i)[:, None]
    c[:, C_ID:C_ID + P] = np.eye(P)
    c[:, C_IOTA:C_IOTA + NREL * N] = np.arange(NREL * N)[None]
    for t in range(NT):
        c[:, C_NODE + t] = p + t * P
    c[:, C_TYPE] = p % 64 - TYPE_ROW
    return c


def build(nc, d):
    with ExitStack() as ctx:
        def sb(name, shape, dt=F32):
            return ctx.enter_context(nc.sbuf_tensor(name, shape, dt))

        def sem(name):
            return ctx.enter_context(nc.semaphore(name))

        raw = sb("raw", [P, PIECES, 2, D])
        whi = sb("whi", [P, PIECES, 2, D], F32R)
        wlo = sb("wlo", [P, PIECES, 2, D], F32R)
        thi = sb("thi", [P, 2, KB, N], F32R)
        tlo = sb("tlo", [P, 2, KB, N], F32R)
        x = sb("x", [P, NT, D])
        nat = sb("nat", [P, NT, D])
        tmp = sb("tmp", [P, NT, D])
        cnt = sb("cnt", [P, NT, NREL * N])
        sel = sb("sel", [P, len(BIASES), P], F32R)
        bias = sb("bias", [P, D], F32R)
        cst = sb("cst", [P, C_END - C_ID])
        ident = cst[:, 0:P]
        red = cst[:, C_RED - C_ID:C_IOTA - C_ID].rearrange("p (j c) -> p j c", c=32)
        iota = cst[:, C_IOTA - C_ID:C_NODE - C_ID]
        node_id = cst[:, C_NODE - C_ID:C_TYPE - C_ID]
        type_id = cst[:, C_TYPE - C_ID:C_END - C_ID]
        idx = sb("idx", [P, 3, TILES], I32)
        idf = sb("idf", [P, 2, TILES])
        ew = sb("ew", [P, TILES])
        st6 = sb("st6", [P, NT, 2, 6])
        mv = sb("mv", [P, NT, 2])
        rstd = sb("rstd", [P, NT, 2])
        sc = sb("sc", [P, NT, NREL, ATTVEC])
        mx = sb("mx", [P, NT, 4])
        b2e = sb("b2e", [P, 1])
        w2e = sb("w2e", [P, H4])
        w1e = sb("w1e", [EA + 1, H4])
        onec = sb("onec", [P, P])
        types = sb("types", [P, N], I32)
        tyhot = sb("tyhot", [P, N], F32R)
        sew = sb("sew", [P, NT])

        R = sb("R", [P, 11528], F32R)
        G = sb("G", [P, 10752])

        def r(a, *dims):
            return cut(R, a, dims)

        def g(a, *dims):
            return cut(G, a, dims)

        def cut(t, a, dims):
            n = int(np.prod(dims))
            v = t[:, a:a + n]
            if len(dims) == 1:
                return v
            names = "abcd"[:len(dims)]
            kw = {c: dims[i] for i, c in enumerate(names) if i}
            return v.rearrange(f"p ({' '.join(names)}) -> p {' '.join(names)}", **kw)

        pat = r(0, PAIRS, P)
        qhi, qlo = r(1024, KB, B * L), r(4096, KB, B * L)
        stack = r(1024, 2, 2, D)
        ghi, glo = r(7168, NT, D), r(8704, NT, D)
        mhi, mlo = r(0, 2, KB, N), r(3072, 2, KB, N)
        AB = r(0, 2, NT, 2, D)
        ohg = r(6144, GROUP, 4, P)
        ohs = r(7680, GROUP, N)
        msg = r(8448, 2, 2, D + 2)
        half_bias = r(7168, D)

        qraw = g(0, KB, B * L)
        cT = g(4608, NT, NREL * N)
        inv = g(6144, NREL * N)
        oh = G[:, 6912:8448].bitcast(BF16).rearrange("p (s c) -> p s c", s=GROUP)
        ea = g(8448, 2, GROUP * P)
        z1 = g(3072, GROUP, H4)
        craw = g(4608, C_ID)
        braw = g(6912, D)
        norm = g(9216, NT, NREL * N)
        xr = g(0, NREL, NT, D)
        qrep = g(0, 2, 2, D)
        prod = g(3072, 2, 2, D)
        psumm = g(6144, 2, D)
        qis = g(7680, 2, D)
        alpha = g(3072, NT, D)
        vec = g(4608, ATTVEC, D)
        esc = g(4608, 2, NREL * N)
        pt = g(6144, 2, 2 * NREL, N)
        brow = g(9216, D)
        m32 = g(0, 2, D + 2)
        ixe = G[:, 1540:1540 + 4 * GROUP * P].bitcast(I32).rearrange("p (s a e) -> p s a e", s=2, a=2)
        xin = g(4608, NT, D)
        b2row = g(6144, D)
        lng, lnb = g(6912, D), g(7680, D)

        ps = ctx.enter_context(nc.psum_tensor("ps", [P, 8, 512], F32))

        def flat(j, n):
            s = 4 * (j % 2)
            return ps[:, s:s + 4, :].rearrange("p b c -> p (b c)")[:, 0:n]

        def rows(j, t, w=HALF):
            s = 4 * (j % 2) + 2 * t
            return ps[:, s:s + 2, 0:w]

        def two(ap):
            return ap.rearrange("p (h c) -> p h c", h=2)

        raw_here = [sem(f"raw_here{s}") for s in range(PIECES)]
        w_hi = sem("w_hi")
        w_lo = sem("w_lo")
        w_used = sem("w_used")
        aux_done = sem("aux_done")
        act_took = sem("act_took")
        dve_took = sem("dve_took")
        t_hi = sem("t_hi")
        t_lo = sem("t_lo")
        rows_here = sem("rows_here")
        act_step = sem("act_step")
        dve_step = sem("dve_step")
        x_here = sem("x_here")
        cst_here = sem("cst_here")
        idx_here = sem("idx_here")
        edge_cst_here = sem("edge_cst_here")
        q_here = sem("q_here")
        set_up = sem("set_up")
        ones_set = sem("ones_set")
        ea_here = [sem(f"ea_here{s}") for s in range(2)]
        oh_here = sem("oh_here")
        oh_used = sem("oh_used")
        z_here = sem("z_here")
        z_read = sem("z_read")
        q_split = sem("q_split")
        parts_here = sem("parts_here")
        parts_stored = sem("parts_stored")
        stack_here = [sem(f"stack_here{s}") for s in range(2)]
        qrep_here = [sem(f"qrep_here{s}") for s in range(2)]
        add_done = [sem(f"add_done{s}") for s in range(2)]
        sig_done = [sem(f"sig_done{s}") for s in range(2)]
        mul_done = [sem(f"mul_done{s}") for s in range(2)]
        sum_done = [sem(f"sum_done{s}") for s in range(2)]
        sum_used = [sem(f"sum_used{s}") for s in range(2)]
        red_done = sem("red_done")
        red_took = sem("red_took")
        qi_stored = [sem(f"qi_stored{s}") for s in range(2)]
        qi_here = sem("qi_here")
        al_here = sem("al_here")
        std_here = sem("std_here")
        var_here = sem("var_here")
        vec_here = sem("vec_here")
        brow_here = sem("brow_here")
        sc_here = sem("sc_here")
        e_here = sem("e_here")
        max_here = sem("max_here")
        p_here = sem("p_here")
        pw_here = sem("pw_here")
        pt_here = sem("pt_here")
        elu_in = sem("elu_in")
        elu_exp = sem("elu_exp")
        ty_here = sem("ty_here")
        tyhot_here = sem("tyhot_here")
        m_here = sem("m_here")
        AB_here = sem("AB_here")
        ixe_here = [sem(f"ixe_here{s}") for s in range(2)]
        ohg_here = sem("ohg_here")
        gat_done = sem("gat_done")
        m32_here = sem("m32_here")
        sew_here = sem("sew_here")
        msg_here = sem("msg_here")
        scat_done = sem("scat_done")
        late_here = sem("late_here")
        out_stored = sem("out_stored")

        block = ctx.enter_context(nc.Block())

        def reached(eng, s, i, per, more):
            if not isinstance(i, int):
                eng.wait_ge(s, i * per + more)
            elif i * per + more > 0:
                eng.wait_ge(s, i * per + more)

        def ready(eng, name):
            u = ends_with(name)
            if u:
                eng.wait_ge(w_used, PIECES * (unit(u) + 1))
            else:
                eng.wait_ge(aux_done, sum(ends_with(n) is None for n in JOBS[:job(name) + 1]))

        def wait_taken(eng, name):
            if readers(name)[0]:
                eng.wait_ge(act_took, taken(name, 0))
            if readers(name)[1]:
                eng.wait_ge(dve_took, taken(name, 1))

        TJOBS = [n for n in JOBS if n[:2] == "T."]

        def turn(name):
            return TJOBS.index("T." + name)

        PARTNER = {"a.h": "a.root", "b.h": "b.root", "m.h": "m.h", "agg": "edges", "agg1": "agg1"}
        BY_DVE = [n[2:] for n in TJOBS if n[2:] not in PARTNER and not n.endswith("qi")]
        GATES = {"a": 0, "b": 1}
        NORMS = ["a", "gat1", "rgat1", "m", "end"]
        RELU_TURNS = {"a", "gat1", "gat2", "rgat1", "m", "agg1"}
        att_names = list(ATT)
        heads_before = {n: sum(ATT[m][1] for m in att_names[:i]) for i, n in enumerate(att_names)}

        @block.sync
        def _(sp):
            sp.dma_start(x[:], d["x"].rearrange("(t p) f -> p t f", p=P)).then_inc(x_here, 16)

            def weights(a, b):
                w = d["weights"].rearrange("(u i k p) f -> (u i) p k f", i=PIECES, k=2, p=P)

                def load(u):
                    for i in range(PIECES):
                        if isinstance(u, int) and u == 0:
                            pass
                        else:
                            sp.wait_ge(w_lo, u * PIECES + (i + 1 - PIECES))
                        sp.dma_start(raw[:, i], w[bass.ds(u * PIECES + i, 1)].rearrange("o p k f -> (o p) k f")
                                     if not isinstance(u, int) else w[u * PIECES + i]).then_inc(raw_here[i], 16)

                if a == 0:
                    load(0)
                    a = 1
                with sp.Fori(a, b) as u:
                    load(u)

            def gate_loads(l):
                hg, qg = d["hg_parts"], d["qg_parts"]
                q = d["L0_gnn_query_embs"].rearrange("b (l a) f -> (b l) a f", a=2)

                def load(b, s):
                    st = stack[:, s].bitcast(F32)
                    for part in range(2):
                        v = hg[part][bass.ds(b * NB, NB), :].rearrange("n (a f) -> n a f", a=1)
                        sp.dma_start(st[32 * part:32 * part + 32], v.to_broadcast([NB, 2, D])).then_inc(stack_here[s], 16)
                        v = qg[part][bass.ds(b * L, L), :].rearrange("(a l) f -> l a f", a=2)
                        sp.dma_start(st[64 + 32 * part:96 + 32 * part], v).then_inc(stack_here[s], 16)
                    for k in range(4):
                        sp.dma_start(qrep[32 * k:32 * k + 32, s], q[bass.ds(b * HL, HL)]).then_inc(qrep_here[s], 16)

                sp.wait_ge(parts_stored, 16 * (2 * 2 + 2 * (l + 1)))
                ready(sp, "ab"[l] + ".root")
                for s in range(2):
                    load(s, s)
                with sp.Fori(1, B // 2) as i:
                    for s in range(2):
                        before = 64 * l - 16 + 8 * (s + 1)
                        sp.wait_ge(add_done[1], i * 16 + before)
                        sp.wait_ge(mul_done[1], i * 16 + before)
                        load(i * 2 + s, s)

            def gate_reload(l):
                for s in range(2):
                    sp.wait_ge(qi_stored[s], 16 * 4 * (l + 1))
                sp.dma_start(tmp[:], d["qi"].rearrange("(t p) f -> p t f", p=P)).then_inc(qi_here, 16)

            weights(0, unit("a.al1") + 1)
            gate_loads(0)
            gate_reload(0)
            weights(unit("a.al2"), unit("b.al1") + 1)
            gate_loads(1)
            gate_reload(1)
            weights(unit("b.al2"), len(UNITS))
            ready(sp, "out")
            sp.wait_ge(rows_here, len(BY_DVE) + 1)
            sp.dma_start(d["out"].rearrange("(t p) f -> p t f", p=P), x[:]).then_inc(out_stored, 16)
            sp.wait_ge(out_stored, 16)

        @block.gpsimd
        def _(pool):
            pool.memset(onec[:], 1.0).then_inc(ones_set, 1)
            pool.wait_ge(ones_set, 1)

            def edge_attributes(i):
                for s in range(2):
                    reached(pool, z_here, i, 2 * GROUP, GROUP * (s - 1))
                    pool.dma_start(ea[0:EA, s, :], d["edge_attr_T"][:, bass.ds((i * 2 + s) * GROUP * P, GROUP * P)]).then_inc(ea_here[s], 16)

            edge_attributes(0)
            with pool.Fori(1, STEPS) as i:
                edge_attributes(i)
            for l in range(2):
                def gate_sums(i):
                    for k in range(2 * PAIRS):
                        s = k % 2
                        pool.wait_ge(mul_done[0], i * 16 + (64 * l + k + 1))
                        pool.wait_ge(mul_done[1], i * 16 + (64 * l + k + 1))
                        reached(pool, sum_used[s], i, 8, 32 * l + k // 2)
                        pool.tensor_tensor(psumm[:, s], prod[:, s, 0], prod[:, s, 1], ALU.add).then_inc(sum_done[s], 1)

                gate_sums(0)
                with pool.Fori(1, B // 2) as i:
                    gate_sums(i)
            for n, name in enumerate(att_names):
                rels, heads = ATT[name]
                pool.wait_ge(rows_here, BY_DVE.index(name) + 1)
                pool.dma_start(vec[:, 0:2 * heads, :], d["att_" + name].rearrange("(o v) f -> o v f", o=1).to_broadcast([P, 2 * heads, D])).then_inc(vec_here, 16)
                pool.wait_ge(sc_here, n + 1)
                pool.dma_start(brow, d["bias_" + name].rearrange("(o f) -> o f", o=1).to_broadcast([P, D])).then_inc(brow_here, 16)
            wait_taken(pool, "rgat2.sum0")
            for row, place in (("L3_gnn_msg_b2", b2row), ("L3_gnn_ln_g", lng), ("L3_gnn_ln_b", lnb)):
                pool.dma_start(place, d[row].rearrange("(o f) -> o f", o=1).to_broadcast([P, D])).then_inc(late_here, 16)
            def edge_indices(i):
                for s in range(2):
                    reached(pool, ohg_here, i, 6, GROUP * (s - 1))
                    pool.dma_start(ixe[:, s], d["edges"][0:2, bass.ds((i * 2 + s) * GROUP * P, GROUP * P)].rearrange("(o a) e -> o a e", o=1).to_broadcast([P, 2, GROUP * P])).then_inc(ixe_here[s], 16)
                    for k in range(GROUP):
                        q = s * GROUP + k
                        m = q % 2
                        reached(pool, msg_here, i, 6, q - 1)
                        pool.tensor_copy(m32[:, m, D:D + 1], ew[:, bass.ds(i * 6 + q, 1)]).then_inc(sew_here, 1)

            edge_indices(0)
            with pool.Fori(1, STEPS) as i:
                edge_indices(i)

        @block.scalar
        def _(act):
            steps = [0]

            def step(ins):
                steps[0] += 1
                ins.then_inc(act_step, 1)
                act.wait_ge(act_step, steps[0])

            made = [0]

            def split_to(u, i):
                while made[0] <= PIECES * u + i and made[0] < PIECES * len(UNITS):
                    p = made[0]
                    act.wait_ge(raw_here[p % PIECES], 16 * (p // PIECES + 1))
                    if p >= PIECES:
                        act.wait_ge(w_used, p - PIECES + 1)
                    act.activation(whi[:, p % PIECES], raw[:, p % PIECES], ACT.Copy).then_inc(w_hi, 1)
                    made[0] += 1

            def columns(name, func=None):
                n = turn(name)
                ready(act, "T." + name)
                f = ACT.Relu if name in RELU_TURNS else ACT.Copy
                j = job("T." + name)
                for i in range(3):
                    src = ps[:, 4 * (j % 2) + i, :].rearrange("p (k n) -> p k n", k=2)
                    ins = act.activation(thi[:, n % 2, 2 * i:2 * i + 2], src, f)
                    ins.then_inc(t_hi, 1)
                act.wait_ge(t_hi, 3 * n + 3)
                act.sem_inc(act_took, 1)

            def take(name, dst, func=ACT.Copy, t=0):
                ready(act, name)
                act.activation(two(dst), rows(job(name), t), func).then_inc(act_took, 1)

            act.dma_start(craw, d["consts"][:, 0:C_ID]).then_inc(cst_here, 16)
            act.dma_start(cst[:], d["consts"][:, C_ID:C_END]).then_inc(cst_here, 16)
            act.dma_start(braw, d["biases"]).then_inc(cst_here, 16)
            act.dma_start(idx[:], d["edges_by_tile"]).then_inc(idx_here, 16)
            act.dma_start(w1e[:], d["edge_w1b"]).then_inc(edge_cst_here, 16)
            act.dma_start(w2e[:], d["L3_gnn_edge_W2"].rearrange("f o -> o f").to_broadcast([P, H4])).then_inc(edge_cst_here, 16)
            act.dma_start(b2e[:], d["L3_gnn_edge_b2"].rearrange("(o f) -> o f", o=1).to_broadcast([P, 1])).then_inc(edge_cst_here, 16)
            act.dma_start(qraw, d["query_T"].rearrange("(k p) n -> p k n", p=P)).then_inc(q_here, 16)
            act.dma_start(types[:], d["node_type_6"].rearrange("(o n) -> o n", o=1).to_broadcast([P, N])).then_inc(ty_here, 16)

            def norm_std(n):
                act.wait_ge(var_here, n + 1)
                act.activation(rstd[:, :, 0], mv[:, :, 1], ACT.Sqrt).then_inc(std_here, 1)

            norm_std(0)
            columns("a")
            act.wait_ge(q_here, 16)
            act.activation(qhi, qraw, ACT.Copy).then_inc(q_split, 1)
            split_to(unit("qg0"), 2)
            take("counts", cT[:, 0])
            act.wait_ge(z_read, TILES)
            act.wait_ge(edge_cst_here, 48)
            act.activation(ew[:], ew[:], ACT.Sigmoid, bias=b2e[:, 0:1]).then_inc(act_step, 1)
            steps[0] += 1
            ready(act, "countT")
            act.activation(cnt[:].rearrange("p t c -> p (t c)")[:, 0:1024], flat(job("countT"), 1024), ACT.Copy).then_inc(act_took, 1)

            def split_parts(name, dram, at):
                ready(act, name)
                if at > 0:
                    act.wait_ge(parts_stored, 16 * 2 * at)
                for t in range(NT):
                    ins = act.activation(two(ghi[:, t]), rows(job(name), t), ACT.Copy)
                ins.then_inc(act_took, 1)
                act.wait_ge(act_took, taken(name, 0))
                act.dma_start(dram[0], ghi.bitcast(F32)).then_inc(parts_stored, 16)
                act.wait_ge(parts_here, at + 1)
                act.dma_start(dram[1], glo.bitcast(F32)).then_inc(parts_stored, 16)

            for i in range(2):
                split_to(unit(f"qg{i}") + 1, 1)
                split_parts(f"qg{i}", [d["qg_parts"][part][i * N:(i + 1) * N].rearrange("(t p) f -> p t f", p=P) for part in range(2)], i)

            for l, L_ in enumerate("ab"):
                if l:
                    columns("b")
                for k in range(NREL):
                    split_to(unit(f"{L_}.rel{k}") + 1, 1)
                    take(f"{L_}.rel{k}", xr[:, k, 0])
                split_to(unit(L_ + ".hg"), 1)
                take(L_ + ".root", nat[:, 0], ACT.Relu)
                columns(L_ + ".h")
                split_to(unit(L_ + ".al1"), 1)
                split_parts(L_ + ".hg", [d["hg_parts"][part].rearrange("(t p) f -> p t f", p=P) for part in range(2)], 2 + l)
                split_to(unit(L_ + ".al1"), 2)

                def store_qi(b, s):
                    i4 = b if isinstance(b, int) else None
                    act.wait_ge(red_done, b + (8 * l + 1))
                    if i4 is None or i4 >= 2:
                        act.wait_ge(qi_stored[s], (b - s) * 8 + 64 * l)
                    elif l:
                        act.wait_ge(qi_stored[s], 64)
                    act.activation(two(qis[0:32, s]), ps[0:32, 4 + 2 * s:6 + 2 * s, 0:HALF], ACT.Copy).then_inc(red_took, 1)
                    act.wait_ge(red_took, b + (8 * l + 1))
                    act.dma_start(d["qi"][bass.ds(b * NB, NB), :], qis[0:32, s]).then_inc(qi_stored[s], 16)

                def gate_steps(i):
                    for k in range(2 * PAIRS):
                        for a in range(2):
                            act.wait_ge(add_done[a], i * 16 + (64 * l + k + 1))
                            act.activation(ps[:, 2 * a:2 * a + 2, 0:HALF], ps[:, 2 * a:2 * a + 2, 0:HALF], ACT.Sigmoid).then_inc(sig_done[a], 1)
                        if k == 4 and not isinstance(i, int):
                            store_qi(i * 2 - 1, 1)
                        if k == 12:
                            store_qi(i * 2, 0)

                gate_steps(0)
                with act.Fori(1, B // 2) as i:
                    gate_steps(i)
                store_qi(B - 1, 1)

                columns(L_ + ".qi")
                split_to(unit(L_ + ".al2") + 1, 1)
                act.wait_ge(qi_here, 16 * (l + 1))
                ready(act, "T." + L_ + ".qi")
                act.activation(tmp[:], tmp[:], ACT.Tanh).then_inc(al_here, 1)
                ready(act, L_ + ".al")
                for t in range(NT):
                    ins = act.activation(two(alpha[:, t]), rows(job(L_ + ".al"), t), ACT.Sigmoid)
                    if t == 0:
                        ins.then_inc(al_here, 1)
                ins.then_inc(act_took, 1)

            for n, name in enumerate(att_names):
                rels, heads = ATT[name]
                w = rels * N
                if name in NORMS:
                    norm_std(NORMS.index(name))
                columns(name)
                for k in range(rels):
                    split_to(unit(f"{name}.{k}") + 1, 1)
                    take(f"{name}.{k}", xr[:, k, 0])
                base = heads_before[name]

                def scores(h):
                    hh = base + h
                    ready(act, f"{name}.row{h}")
                    act.wait_ge(sc_here, n + 1)
                    for t in range(NT):
                        if hh:
                            if h:
                                ready(act, f"{name}.pt{h - 1}")
                        for k in range(rels):
                            ins = act.activation(esc[:, t, k * N:(k + 1) * N], flat(job(f"{name}.row{h}"), w)[:, k * N:(k + 1) * N],
                                                 ACT.Identity, bias=sc[:, t, k, h:h + 1])
                            if k == rels - 1:
                                ins.then_inc(e_here, 1)
                    act.wait_ge(e_here, NT * (hh + 1))
                    act.sem_inc(act_took, 1)

                def exps(h):
                    hh = base + h
                    for t in range(NT):
                        act.wait_ge(max_here, NT * hh + t + 1)
                        act.activation(esc[:, t, 0:w], esc[:, t, 0:w], ACT.Exp, bias=mx[:, t, 0:1]).then_inc(p_here, 1)

                for h in range(heads):
                    hh = base + h
                    scores(h)
                    exps(h)
                    ready(act, f"{name}.pt{h}")
                    if h >= 2:
                        ready(act, f"{name}.sum{h - 2}")
                    act.activation(pt[:, h % 2, 0:2 * rels].rearrange("p a b -> p (a b)"), flat(job(f"{name}.pt{h}"), 2 * rels * N), ACT.Copy).then_inc(act_took, 1)
                if name == "rgat1":
                    for t in range(NT):
                        act.wait_ge(elu_in, t + 1)
                        act.activation(esc[:, t], esc[:, t], ACT.Exp).then_inc(elu_exp, 1)

            norm_std(NORMS.index("m"))
            columns("m")
            for t in range(NTYPE):
                split_to(unit(f"ty{t}") + 1, 1)
            take("m.h", nat[:, 0])
            columns("m.h")
            for a, name in enumerate(("msgA", "msgB")):
                split_to(unit(name) + 1, 1)
                ready(act, name)
                for t in range(NT):
                    ins = act.activation(two(AB[:, a, t, 0]), rows(job(name), t), ACT.Copy)
                    if t == 0:
                        step(ins)
                ins.then_inc(act_took, 1)
            split_to(unit("msg2"), 2)
            other = 4 * ((job("edges") + 1) % 2)
            def messages(i):
                for q in range(2 * GROUP):
                    m = q % 2
                    act.wait_ge(gat_done, i * 6 + (q + 1))
                    reached(act, msg_here, i, 6, q - 1)
                    act.activation(two(m32[:, m, 0:D]), ps[:, other + 2 * m:other + 2 * m + 2, 0:HALF], ACT.Relu,
                                   scale=ew[:, bass.ds(i * 6 + q, 1)]).then_inc(m32_here, 1)

            messages(0)
            with act.Fori(1, STEPS) as i:
                messages(i)
            ready(act, "edges")
            step(act.activation(sew[:, 0:1], rows(job("edges"), 0, HALF + 1)[:, 1, HALF:HALF + 1], ACT.Copy))
            act.activation(two(tmp[:, 0]), rows(job("edges"), 0), ACT.Copy).then_inc(act_took, 1)
            columns("agg")
            split_to(unit("agg1"), 1)
            columns("msg2")
            split_to(unit("agg2"), 1)
            take("agg1", tmp[:, 0])
            columns("agg1")
            split_to(unit("out"), 1)
            columns("agg2")
            split_to(unit("out"), 2)
            norm_std(NORMS.index("end"))

        @block.vector
        def _(dve):
            steps = [0]

            def step(ins):
                steps[0] += 1
                ins.then_inc(dve_step, 1)
                dve.wait_ge(dve_step, steps[0])

            made = [0]

            def split_to(u, i):
                while made[0] <= PIECES * u + i and made[0] < PIECES * len(UNITS):
                    p = made[0]
                    dve.wait_ge(w_hi, p + 1)
                    dve.tensor_tensor(wlo[:, p % PIECES], raw[:, p % PIECES], whi[:, p % PIECES], ALU.subtract).then_inc(w_lo, 1)
                    made[0] += 1

            def columns(name):
                n = turn(name)
                j = job("T." + name)
                for i in range(3):
                    dve.wait_ge(t_hi, 3 * n + i + 1)
                    src = ps[:, 4 * (j % 2) + i, :].rearrange("p (k n) -> p k n", k=2)
                    hi, lo = thi[:, n % 2, 2 * i:2 * i + 2], tlo[:, n % 2, 2 * i:2 * i + 2]
                    if name in RELU_TURNS:
                        ins = dve.scalar_tensor_tensor(lo, src, 0.0, hi, ALU.max, ALU.subtract)
                    else:
                        ins = dve.tensor_tensor(lo, src, hi, ALU.subtract)
                    ins.then_inc(t_lo, 1)
                dve.wait_ge(t_lo, 3 * n + 3)
                dve.sem_inc(dve_took, 1)

            def take(name, dst, relu=False, t=1):
                ready(dve, name)
                if relu:
                    ins = dve.tensor_scalar(two(dst), rows(job(name), t), 0.0, None, ALU.max)
                else:
                    ins = dve.tensor_copy(two(dst), rows(job(name), t))
                ins.then_inc(dve_took, 1)

            def normalise(src, dst, n):
                for t in range(NT):
                    for h in range(2):
                        step(dve.bn_stats(st6[:, t, h, :], src[:, t, h * HALF:(h + 1) * HALF]))
                    step(dve.bn_aggr(mv[:, t, :], st6[:, t].rearrange("p a b -> p (a b)")))
                dve.tensor_scalar(mv[:, :, 1], mv[:, :, 1], LN_EPS, None, ALU.add).then_inc(var_here, 1)
                dve.wait_ge(std_here, n + 1)
                step(dve.reciprocal(rstd[:, :, 1], rstd[:, :, 0]))
                for t in range(NT):
                    ins = dve.tensor_scalar(dst[:, t], src[:, t], mv[:, t, 0:1], rstd[:, t, 1:2], ALU.subtract, ALU.mult)
                    if t == 0:
                        step(ins)
                return ins

            dve.wait_ge(x_here, 16)
            normalise(x, tmp, 0).then_inc(rows_here, 1)
            dve.wait_ge(idx_here, 16)
            step(dve.tensor_copy(idf[:, 0], idx[:, 0]))
            step(dve.tensor_scalar(idf[:, 1], idx[:, 2], float(N), None, ALU.mult))
            step(dve.tensor_tensor(idf[:, 1], idf[:, 1], idx[:, 1], ALU.add))
            dve.wait_ge(cst_here, 48)
            step(dve.tensor_copy(pat.rearrange("p a b -> p (a b)"), craw[:, 0:C_SEL]))
            step(dve.tensor_copy(sel[:].rearrange("p a b -> p (a b)"), craw[:, C_SEL:C_ID]))
            step(dve.tensor_copy(half_bias, braw))
            step(dve.tensor_tensor(bias[:], braw, half_bias, ALU.subtract))
            step(dve.tensor_copy(bias[0:64], braw[0:64]))
            step(dve.memset(ea[EA:EA + 1], 1.0))
            dve.wait_ge(ty_here, 16)
            dve.tensor_scalar(tyhot[:], types[:], type_id, None, ALU.is_equal).then_inc(set_up, 1)
            columns("a")
            dve.wait_ge(edge_cst_here, 48)

            def count_hot(i, q):
                e, k = bass.ds(i * 6 + q, 1), q % GROUP
                reached(dve, oh_used, i, 6, q - 2)
                dve.tensor_scalar(oh[:, k, 0:N], iota[:, 0:N], idf[:, 0, e], None, ALU.is_equal)
                dve.tensor_scalar(oh[:, k, N:], iota, idf[:, 1, e], None, ALU.is_equal).then_inc(oh_here, 1)

            def edge_logit(i, q):
                e, k = bass.ds(i * 6 + q, 1), q % GROUP
                dve.wait_ge(z_here, i * 6 + (q + 1))
                reached(dve, z_read, i, 6, q - 2)
                dve.scalar_tensor_tensor(z1[:, k], ps[:, k, 0:H4], 0.0, w2e[:], ALU.max, ALU.mult,
                                         accum_out=ew[:, e]).then_inc(z_read, 1)

            for q in range(6):
                count_hot(0, q)
                if q >= 2:
                    edge_logit(0, q - 2)
            with dve.Fori(1, STEPS) as i:
                for q in range(6):
                    count_hot(i, q)
                    edge_logit(i, q - 2)
            for q in (4, 5):
                edge_logit(STEPS - 1, q)
            dve.wait_ge(q_split, 1)
            dve.tensor_tensor(qlo, qraw, qhi, ALU.subtract).then_inc(q_split, 1)
            split_to(unit("qg0"), 2)
            take("counts", cT[:, 1])
            ready(dve, "countT")
            dve.tensor_copy(cnt[:].rearrange("p t c -> p (t c)")[:, 1024:1536], flat(job("countT"), 1536)[:, 1024:1536]).then_inc(dve_took, 1)
            ready(dve, "countrow")
            step(dve.tensor_scalar(two(inv), ps[:, 4 * (job("countrow") % 2):4 * (job("countrow") % 2) + 2, 0:HALF], 1.0, None, ALU.max))
            step(dve.reciprocal(inv, inv))
            step(dve.tensor_tensor(norm[:, 0], cT[:, 0], inv, ALU.mult))
            dve.tensor_tensor(norm[:, 1], cT[:, 1], inv, ALU.mult).then_inc(dve_took, 1)

            def split_parts(name, at):
                ready(dve, name)
                dve.wait_ge(act_took, taken(name, 0))
                if at > 0:
                    dve.wait_ge(parts_stored, 16 * 2 * at)
                for t in range(NT):
                    ins = dve.tensor_tensor(two(glo[:, t]), rows(job(name), t), two(ghi[:, t]), ALU.subtract)
                    if t == 0:
                        step(ins)
                ins.then_inc(parts_here, 1)
                dve.wait_ge(parts_here, at + 1)
                dve.sem_inc(dve_took, 1)

            for i in range(2):
                split_to(unit(f"qg{i}") + 1, 1)
                split_parts(f"qg{i}", i)

            for l, L_ in enumerate("ab"):
                if l:
                    columns("b")
                for k in range(NREL):
                    split_to(unit(f"{L_}.rel{k}") + 1, 1)
                    take(f"{L_}.rel{k}", xr[:, k, 1])
                split_to(unit(L_ + ".hg"), 1)
                take(L_ + ".root", nat[:, 1], relu=True)
                columns(L_ + ".h")
                split_to(unit(L_ + ".al1"), 1)
                split_parts(L_ + ".hg", 2 + l)
                split_to(unit(L_ + ".al1"), 2)

                def gate_products(i):
                    for k in range(2 * PAIRS):
                        s = k // PAIRS
                        if k % PAIRS == 0:
                            dve.wait_ge(qrep_here[s], i * 64 + (256 * l + 64))
                        for a in range(2):
                            dve.wait_ge(sig_done[a], i * 16 + (64 * l + k + 1))
                            reached(dve, sum_done[k % 2], i, 8, 32 * l + k // 2)
                            dve.tensor_tensor(two(prod[:, k % 2, a]), ps[:, 2 * a:2 * a + 2, 0:HALF], two(qrep[:, s, a]),
                                              ALU.mult).then_inc(mul_done[a], 1)

                gate_products(0)
                with dve.Fori(1, B // 2) as i:
                    gate_products(i)
                columns(L_ + ".qi")
                split_to(unit(L_ + ".al2") + 1, 1)
                dve.wait_ge(al_here, 2 * l + 1)
                step(dve.tensor_tensor(tmp[:], tmp[:], nat[:], ALU.subtract))
                dve.wait_ge(act_took, taken(L_ + ".al", 0))
                step(dve.tensor_tensor(tmp[:], tmp[:], alpha, ALU.mult))
                dve.sem_inc(dve_took, 1)
                ins = dve.tensor_tensor(tmp[:], tmp[:], nat[:], ALU.add)
                if l == 0:
                    ins.then_inc(rows_here, 1)
                else:
                    step(ins)
                    step(dve.tensor_tensor(x[:], x[:], tmp[:], ALU.add))

            for n, name in enumerate(att_names):
                rels, heads = ATT[name]
                w = rels * N
                gat = rels == 1
                if name == "gat1":
                    c1, m1 = nat[:, :, N:2 * N], nat[:, :, 0:N]
                    step(dve.tensor_tensor(c1, cnt[:, :, 0:N], cnt[:, :, N:2 * N], ALU.add))
                    step(dve.tensor_tensor(c1, c1, cnt[:, :, 2 * N:3 * N], ALU.add))
                    for t in range(NT):
                        step(dve.tensor_tensor(c1[:, t, t * P:(t + 1) * P], c1[:, t, t * P:(t + 1) * P], ident, ALU.add))
                    step(dve.tensor_scalar(m1, c1, 0.0, NO_EDGE, ALU.is_equal, ALU.mult))
                    counts, mask = c1, m1
                if name == "rgat1":
                    step(dve.tensor_scalar(nat[:], cnt[:], 0.0, NO_EDGE, ALU.is_equal, ALU.mult))
                    counts, mask = cnt, nat
                if name in NORMS:
                    normalise(x, tmp, NORMS.index(name)).then_inc(rows_here, 1)
                columns(name)
                for k in range(rels):
                    split_to(unit(f"{name}.{k}") + 1, 1)
                    take(f"{name}.{k}", xr[:, k, 1])
                    dve.wait_ge(vec_here, 16 * (n + 1))
                    wait_taken(dve, f"{name}.{k}")
                    for t in range(NT):
                        for v in range(2 * heads):
                            ins = dve.tensor_tensor_reduce(tmp[:, 0], xr[:, k, t], vec[:, v], 1.0, 0.0,
                                                           ALU.mult, ALU.add, sc[:, t, k, v:v + 1])
                            if (k, t, v) != (rels - 1, NT - 1, 2 * heads - 1):
                                step(ins)
                ins.then_inc(sc_here, 1)
                dve.wait_ge(sc_here, n + 1)
                base = heads_before[name]
                for h in range(heads):
                    hh = base + h
                    for t in range(NT):
                        e = esc[:, t, 0:w]
                        dve.wait_ge(e_here, NT * hh + t + 1)
                        step(dve.scalar_tensor_tensor(e, e, SLOPE, e, ALU.mult, ALU.max))
                        step(dve.tensor_tensor_reduce(e, e, mask[:, t, 0:w], 1.0, NO_EDGE, ALU.add, ALU.max, mx[:, t, 1:2]))
                        dve.tensor_scalar(mx[:, t, 0:1], mx[:, t, 1:2], -1.0, None, ALU.mult).then_inc(max_here, 1)
                    for t in range(NT):
                        e = esc[:, t, 0:w]
                        dve.wait_ge(p_here, NT * hh + t + 1)
                        dve.tensor_tensor_reduce(e, e, counts[:, t, 0:w], 1.0, 0.0, ALU.mult, ALU.add, mx[:, t, 2:3]).then_inc(pw_here, 1)
                    dve.wait_ge(pw_here, NT * (hh + 1))
                    if not gat:
                        step(dve.tensor_scalar(mx[:, :, 2], mx[:, :, 2], Z_EPS, None, ALU.add))
                    step(dve.reciprocal(mx[:, :, 3], mx[:, :, 2]))
                    j = job(f"{name}.sum{h}")
                    c = D // heads
                    dve.wait_ge(brow_here, 16 * (n + 1))
                    ready(dve, f"{name}.sum{h}")
                    for t in range(NT):
                        if heads == 1:
                            o, i, b = two(tmp[:, t]), rows(j, t), two(brow)
                        else:
                            o, i, b = tmp[:, t, h * c:(h + 1) * c], ps[:, 4 * (j % 2) + 2 * t, 0:c], brow[:, h * c:(h + 1) * c]
                        ins = dve.scalar_tensor_tensor(o, i, mx[:, t, 3:4], b, ALU.mult, ALU.add)
                        if t == 0:
                            step(ins)
                    ins.then_inc(dve_took, 1)
                    dve.wait_ge(dve_took, taken(f"{name}.sum{h}", 1))
                if name == "gat1":
                    dve.sem_inc(rows_here, 1)
                elif name == "rgat1":
                    for t in range(NT):
                        dve.tensor_scalar(esc[:, t], tmp[:, t], 0.0, None, ALU.min).then_inc(elu_in, 1)
                    for t in range(NT):
                        dve.wait_ge(elu_exp, t + 1)
                        step(dve.scalar_tensor_tensor(tmp[:, t], tmp[:, t], 0.0, esc[:, t], ALU.max, ALU.add))
                    dve.tensor_scalar(tmp[:], tmp[:], -1.0, None, ALU.add).then_inc(rows_here, 1)
                else:
                    step(dve.tensor_tensor(x[:], x[:], tmp[:], ALU.add))

            normalise(x, tmp, NORMS.index("m")).then_inc(rows_here, 1)
            dve.wait_ge(rows_here, BY_DVE.index("m") + 1)
            step(dve.tensor_scalar(xin, tmp[:], 0.0, None, ALU.max))
            columns("m")
            n = turn("m") % 2
            ty = types[:].rearrange("p (a n) -> p a n", a=1).to_broadcast([P, KB, N])
            for t in range(NTYPE):
                if t >= 2:
                    dve.wait_ge(w_used, PIECES * (unit(f"ty{t - 2}") + 1))
                dve.scalar_tensor_tensor(mhi[:, t % 2], ty, float(t), thi[:, n], ALU.is_equal, ALU.mult).then_inc(m_here, 1)
                dve.scalar_tensor_tensor(mlo[:, t % 2], ty, float(t), tlo[:, n], ALU.is_equal, ALU.mult).then_inc(m_here, 1)
                split_to(unit(f"ty{t}") + 1, 0)
            take("m.h", nat[:, 1])
            columns("m.h")
            for a, name in enumerate(("msgA", "msgB")):
                split_to(unit(name) + 1, 1)
                ready(dve, name)
                dve.wait_ge(act_took, taken(name, 0))
                for t in range(NT):
                    ins = dve.tensor_tensor(two(AB[:, a, t, 1]), rows(job(name), t), two(AB[:, a, t, 0]), ALU.subtract)
                    if t == 0:
                        step(ins)
                ins.then_inc(dve_took, 1)
            split_to(unit("msg2"), 2)
            step(dve.memset(m32[:, :, D + 1:D + 2], 0.0))

            def onehots(i, s, k):
                q = s * GROUP + k
                dve.wait_ge(ixe_here[s], i * 16 + 16)
                reached(dve, scat_done, i, 6, q - 2)
                for c in range(2):
                    for t in range(NT):
                        dve.tensor_scalar(ohg[:, k, 2 * c + t], ixe[:, s, c, k * P:(k + 1) * P], node_id[:, t:t + 1], None, ALU.is_equal)
                dve.tensor_scalar(ohs[:, k], iota[:, 0:N], idf2[:, bass.ds(i * 6 + q, 1)], None, ALU.is_equal).then_inc(ohg_here, 1)

            idf2 = idf[:, 1]
            step(dve.tensor_copy(idf2, idx[:, 1]))

            def split_message(i, q):
                m = q % 2
                dve.wait_ge(m32_here, i * 6 + (q + 1))
                dve.wait_ge(sew_here, i * 6 + (q + 1))
                reached(dve, scat_done, i, 6, q - 1)
                dve.tensor_copy(msg[:, m, 0], m32[:, m]).then_inc(dve_step, 1)
                dve.wait_ge(dve_step, i * 6 + (steps[0] + q + 1))
                dve.tensor_tensor(msg[:, m, 1], m32[:, m], msg[:, m, 0], ALU.subtract).then_inc(msg_here, 1)

            def edge_tiles(i, last):
                for q in range(6):
                    if q < 5:
                        onehots(i, (q + 1) // GROUP, (q + 1) % GROUP)
                    elif not last:
                        onehots(i + 1, 0, 0)
                    split_message(i, q)

            onehots(0, 0, 0)
            edge_tiles(0, False)
            with dve.Fori(1, STEPS - 1) as i:
                edge_tiles(i, False)
            edge_tiles(STEPS - 1, True)
            steps[0] += TILES
            j = job("edges")
            ready(dve, "edges")
            step(dve.tensor_copy(sew[:, 1:2], rows(j, 1, HALF + 1)[:, 1, HALF:HALF + 1]))
            dve.tensor_copy(two(tmp[:, 1]), rows(j, 1)).then_inc(dve_took, 1)
            columns("agg")
            split_to(unit("agg1"), 1)
            dve.wait_ge(late_here, 48)
            ready(dve, "msg2")
            for t in range(NT):
                ins = dve.scalar_tensor_tensor(two(tmp[:, t]), two(b2row), sew[:, t:t + 1], rows(job("msg2"), t), ALU.mult, ALU.add)
                if t == 0:
                    step(ins)
            step(ins)
            dve.sem_inc(dve_took, 1)
            dve.sem_inc(rows_here, 1)
            columns("msg2")
            split_to(unit("agg2"), 1)
            take("agg1", tmp[:, 1])
            columns("agg1")
            split_to(unit("out"), 1)
            ready(dve, "agg2")
            for t in range(NT):
                step(dve.tensor_tensor(two(tmp[:, t]), rows(job("agg2"), t), two(nat[:, t]), ALU.add))
            dve.sem_inc(dve_took, 1)
            dve.sem_inc(rows_here, 1)
            columns("agg2")
            split_to(unit("out"), 2)
            ready(dve, "out")
            for t in range(NT):
                step(dve.tensor_tensor(two(tmp[:, t]), rows(job("out"), t), two(xin[:, t]), ALU.add))
            dve.sem_inc(dve_took, 1)
            step(normalise(tmp, nat, NORMS.index("end")))
            for t in range(NT):
                step(dve.tensor_tensor(nat[:, t], nat[:, t], lng, ALU.mult))
                step(dve.tensor_tensor(nat[:, t], nat[:, t], lnb, ALU.add))
            dve.tensor_tensor(x[:], x[:], nat[:], ALU.add).then_inc(rows_here, 1)

        @block.tensor
        def _(pe):
            def open_job(name):
                j = job(name)
                if j >= 2:
                    wait_upto(j - 2)

            def wait_upto(j):
                a, v = sum(readers(n)[0] for n in JOBS[:j + 1]), sum(readers(n)[1] for n in JOBS[:j + 1])
                if a:
                    pe.wait_ge(act_took, a)
                if v:
                    pe.wait_ge(dve_took, v)

            def product(u, out_job, cols_of, start, stop):
                j = job(out_job)
                for i in range(PIECES):
                    pe.wait_ge(w_lo, PIECES * u + i + 1)
                    for kk in range(2):
                        hi, lo = cols_of(i, kk)
                        k = 2 * i + kk
                        for t in range(NT):
                            o = [rows(j, t)[:, h, :] for h in range(2)]
                            for part, (lhs, ws) in enumerate(((hi, (whi, wlo)), (lo, (whi,)))):
                                for wn, w in enumerate(ws):
                                    for h in range(2):
                                        first = start and k == 0 and part == 0 and wn == 0
                                        last = stop and k == KB - 1 and part == 1
                                        ins = pe.matmul(o[h], lhs[:, t * P:(t + 1) * P], w[:, i, kk, h * HALF:(h + 1) * HALF],
                                                        start=first, stop=last)
                    ins.then_inc(w_used, 1)

            def turned(name):
                n = turn(name)

                def cols_of(i, kk):
                    if kk == 0:
                        pe.wait_ge(t_lo, 3 * n + i + 1)
                    return thi[:, n % 2, 2 * i + kk], tlo[:, n % 2, 2 * i + kk]
                return cols_of

            def add_bias(out_job, lhs):
                for t in range(NT):
                    for h in range(2):
                        pe.matmul(rows(job(out_job), t)[:, h, :], lhs(t), bias[:, h * HALF:(h + 1) * HALF], start=True, stop=False)

            def picked(name):
                return lambda t: sel[:, BIASES.index(name), :]

            def plain(name, turn_name, bias_name=None):
                open_job(name)
                if bias_name:
                    add_bias(name, picked(bias_name))
                product(unit(name), name, turned(turn_name), not bias_name, True)

            def turn_rows(name):
                open_job("T." + name)
                if name in PARTNER:
                    wait_taken(pe, PARTNER[name])
                else:
                    if name.endswith(".qi"):
                        pe.wait_ge(qi_here, 16 * (GATES[name[0]] + 1))
                    else:
                        pe.wait_ge(rows_here, BY_DVE.index(name) + 1)
                src = nat if name in ("a.h", "b.h", "m.h") else tmp
                j = job("T." + name)
                for k in range(KB):
                    for t in range(NT):
                        o = ps[:, 4 * (j % 2) + k // 2, (k % 2) * N + t * P:(k % 2) * N + (t + 1) * P]
                        ins = pe.transpose(o, src[:, t, k * P:(k + 1) * P], ident)
                ins.then_inc(aux_done, 1)

            pe.wait_ge(cst_here, 48)
            turn_rows("a")
            pe.wait_ge(set_up, 1)
            pe.wait_ge(edge_cst_here, 48)
            wait_taken(pe, "T.a")
            j = job("counts")
            def count_tile(k, start, stop):
                for t in range(NT):
                    for h in range(2):
                        ins = pe.matmul(rows(j, t)[:, h, :], oh[:, k, t * P:(t + 1) * P], oh[:, k, N + h * HALF:N + (h + 1) * HALF],
                                        start=start, stop=stop)
                return ins

            def edge_tile(i, q, first=False, last=False):
                s, k = q // GROUP, q % GROUP
                pe.wait_ge(oh_here, i * 6 + (q + 1))
                count_tile(k, first, last).then_inc(aux_done if last else oh_used, 1)
                reached(pe, z_read, i, 6, q - 2)
                if k == 0:
                    pe.wait_ge(ea_here[s], i * 16 + 16)
                pe.matmul(ps[:, k, 0:H4], ea[0:EA + 1, s, k * P:(k + 1) * P], w1e[:], start=True, stop=True).then_inc(z_here, 1)

            for q in range(6):
                edge_tile(0, q, first=q == 0)
            with pe.Fori(1, STEPS - 1) as i:
                for q in range(6):
                    edge_tile(i, q)
            for q in range(6):
                edge_tile(STEPS - 1, q, last=q == 5)
            wait_taken(pe, "counts")
            pe.wait_ge(z_read, TILES)
            for dt in range(NT):
                for k in range(NREL):
                    for st in range(NT):
                        o = flat(job("countT"), 1536)[:, dt * D + k * N + st * P:dt * D + k * N + (st + 1) * P]
                        ins = pe.transpose(o, cT[:, st, k * N + dt * P:k * N + (dt + 1) * P], ident)
            ins.then_inc(aux_done, 1)
            pe.wait_ge(ones_set, 1)
            s = 4 * (job("countrow") % 2)
            for h in range(2):
                for t in range(NT):
                    ins = pe.matmul(ps[:, s + h, 0:HALF], onec[:], cT[:, t, h * HALF:(h + 1) * HALF], start=t == 0, stop=t == NT - 1)
            ins.then_inc(aux_done, 1)
            pe.wait_ge(q_split, 2)
            for i2 in range(2):
                name = f"qg{i2}"
                open_job(name)
                add_bias(name, picked("bg"))
                product(unit(name), name, lambda i, kk: (qhi[:, 2 * i + kk, i2 * N:(i2 + 1) * N], qlo[:, 2 * i + kk, i2 * N:(i2 + 1) * N]), False, True)

            for l, L_ in enumerate("ab"):
                if l:
                    turn_rows("b")
                for k in range(NREL):
                    plain(f"{L_}.rel{k}", L_)
                name = L_ + ".root"
                open_job(name)
                add_bias(name, picked("b1" if l == 0 else "b2"))
                product(unit(name), name, turned(L_), False, False)
                for k in range(NREL):
                    wait_taken(pe, f"{L_}.rel{k}")
                    for st in range(NT):
                        for dt in range(NT):
                            for h in range(2):
                                ins = pe.matmul(rows(job(name), dt)[:, h, :], norm[:, st, k * N + dt * P:k * N + (dt + 1) * P],
                                                xr[:, k, st, h * HALF:(h + 1) * HALF], start=False, stop=k == NREL - 1 and st == NT - 1)
                ins.then_inc(aux_done, 1)
                turn_rows(L_ + ".h")
                plain(L_ + ".hg", L_ + ".h")
                wait_taken(pe, L_ + ".hg")

                def add_pair(i, k):
                    s = k // PAIRS
                    if k % PAIRS == 0:
                        pe.wait_ge(stack_here[s], i * 64 + (256 * l + 64))
                    for a in range(2):
                        reached(pe, mul_done[a], i, 16, 64 * l + k)
                        for h in range(2):
                            ins = pe.matmul(ps[:, 2 * a + h, 0:HALF], pat[:, k % PAIRS, :], stack[:, s, a, h * HALF:(h + 1) * HALF], start=True, stop=True)
                        ins.then_inc(add_done[a], 1)

                def reduce_pair(i, k):
                    s, jj = k // PAIRS, k % PAIRS
                    pe.wait_ge(sum_done[k % 2], i * 8 + (32 * l + k // 2 + 1))
                    if jj == 0:
                        reached(pe, red_took, i, 2, 8 * l + s - 1)
                    for h in range(2):
                        ins = pe.matmul(ps[0:32, 4 + 2 * s + h, 0:HALF], red[:, jj, :], psumm[:, k % 2, h * HALF:(h + 1) * HALF],
                                        start=jj == 0, stop=jj == PAIRS - 1)
                    ins.then_inc(sum_used[k % 2], 1)
                    if jj == PAIRS - 1:
                        pe.wait_ge(sum_used[k % 2], i * 8 + (32 * l + k // 2 + 1))
                        pe.sem_inc(red_done, 1)

                LAG = 2

                def gate_steps(i, last):
                    for k in range(2 * PAIRS):
                        if k + LAG < 2 * PAIRS:
                            add_pair(i, k + LAG)
                        elif not last:
                            add_pair(i + 1, k + LAG - 2 * PAIRS)
                        reduce_pair(i, k)

                for k in range(LAG):
                    add_pair(0, k)
                gate_steps(0, False)
                with pe.Fori(1, B // 2 - 1) as i:
                    gate_steps(i, False)
                gate_steps(B // 2 - 1, True)
                for a in range(2):
                    pe.wait_ge(mul_done[a], 64 * (l + 1))
                pe.wait_ge(red_took, 8 * (l + 1))
                name = L_ + ".al"
                add_bias(name, picked("bq"))
                product(unit(name + "1"), name, turned(L_ + ".h"), False, False)
                turn_rows(L_ + ".qi")
                product(unit(name + "2"), name, turned(L_ + ".qi"), False, True)

            for n, name in enumerate(att_names):
                rels, heads = ATT[name]
                turn_rows(name)
                for k in range(rels):
                    plain(f"{name}.{k}", name)

                def row(h):
                    open_job(f"{name}.row{h}")
                    pe.wait_ge(sc_here, n + 1)
                    for k in range(rels):
                        for t in range(NT):
                            ins = pe.matmul(flat(job(f"{name}.row{h}"), D)[:, k * N + t * P:k * N + (t + 1) * P],
                                            sc[:, t, k, heads + h:heads + h + 1].to_broadcast([P, P]), ident, start=True, stop=True)
                    ins.then_inc(aux_done, 1)

                row(0)
                for h in range(heads):
                    if h + 1 < heads:
                        row(h + 1)
                    open_job(f"{name}.pt{h}")
                    pe.wait_ge(pw_here, NT * (heads_before[name] + h + 1))
                    for k in range(2 * rels):
                        for t in range(NT):
                            o = flat(job(f"{name}.pt{h}"), 2 * rels * N)[:, k * N + t * P:k * N + (t + 1) * P]
                            ins = pe.transpose(o, esc[:, t, k * P:(k + 1) * P], ident)
                    ins.then_inc(aux_done, 1)
                    open_job(f"{name}.sum{h}")
                    wait_taken(pe, f"{name}.pt{h}")
                    j = job(f"{name}.sum{h}")
                    c = D // heads
                    cuts = [(0, HALF), (HALF, HALF)] if heads == 1 else [(h * c, c)]
                    for t in range(NT):
                        for q, (a, m) in enumerate(cuts):
                            for k in range(2 * rels):
                                ins = pe.matmul(ps[:, 4 * (j % 2) + 2 * t + q, 0:m], pt[:, h % 2, k, t * P:(t + 1) * P],
                                                xr[:, k // 2, k % 2, a:a + m], start=k == 0, stop=k == 2 * rels - 1)
                    ins.then_inc(aux_done, 1)

            turn_rows("m")
            open_job("m.h")
            add_bias("m.h", lambda t: tyhot[:, t * P:(t + 1) * P])
            for t in range(NTYPE):
                def of_type(i, kk, t=t):
                    if i == 0 and kk == 0:
                        pe.wait_ge(m_here, 2 * t + 2)
                    return mhi[:, t % 2, 2 * i + kk], mlo[:, t % 2, 2 * i + kk]
                product(unit(f"ty{t}"), "m.h", of_type, False, t == NTYPE - 1)
            turn_rows("m.h")
            plain("msgA", "m.h")
            plain("msgB", "m.h", "msg_b1")
            wait_taken(pe, "msgB")
            j = job("edges")
            other = 4 * ((j + 1) % 2)

            def place(t, h):
                w = HALF + 2 * h
                return ps[:, 4 * (j % 2) + 2 * t + h, 0:w]

            def gather(i, q):
                k, m = q % GROUP, q % 2
                pe.wait_ge(ohg_here, i * 6 + (q + 1))
                reached(pe, m32_here, i, 6, q - 1)
                for c in range(2):
                    for t in range(NT):
                        for part in range(2):
                            for h in range(2):
                                ins = pe.matmul(ps[:, other + 2 * m + h, 0:HALF], ohg[:, k, 2 * c + t, :], AB[:, c, t, part, h * HALF:(h + 1) * HALF],
                                                start=c + t + part == 0, stop=c + t + part == 3)
                ins.then_inc(gat_done, 1)

            def scatter(i, q, first=False, last=False):
                k, m = q % GROUP, q % 2
                pe.wait_ge(msg_here, i * 6 + (q + 1))
                for t in range(NT):
                    for part in range(2):
                        for h in range(2):
                            ins = pe.matmul(place(t, h), ohs[:, k, t * P:(t + 1) * P], msg[:, m, part, h * HALF:(h + 1) * HALF + 2 * h],
                                            start=first and part == 0, stop=last and part == 1)
                ins.then_inc(aux_done if last else scat_done, 1)

            def edge_loop(i, first=False, last=False):
                for q in range(2 * GROUP):
                    if q + 1 < 2 * GROUP:
                        gather(i, q + 1)
                    elif not last:
                        gather(i + 1, 0)
                    scatter(i, q, first and q == 0, last and q == 2 * GROUP - 1)

            gather(0, 0)
            edge_loop(0, first=True)
            with pe.Fori(1, STEPS - 1) as i:
                edge_loop(i)
            edge_loop(STEPS - 1, last=True)
            turn_rows("agg")
            plain("msg2", "agg")
            turn_rows("msg2")
            plain("agg1", "msg2", "agg_b1")
            turn_rows("agg1")
            plain("agg2", "agg1", "agg_b2")
            turn_rows("agg2")
            plain("out", "agg2", "out_b")


def weight_stack(v):
    wg, wq = v["L0_gnn_Wg"], v["L0_gnn_Wq"]
    out = [wg[:, D:].T] * 2
    for k in (1, 2):
        out += list(v[f"L0_gnn_W_rel{k}"]) + [v[f"L0_gnn_W_root{k}"], wg[:, :D].T, wq[:, :D].T, wq[:, D:].T]
    out += [v["L1_gnn_W1"], v["L1_gnn_W2"], *v["L2_gnn_W1"], *v["L2_gnn_W2"], *v["L3_gnn_W_type"]]
    out += [v["L3_gnn_msg_W1"][:D], v["L3_gnn_msg_W1"][D:]]
    out += [v[f"L3_gnn_{n}"] for n in ("msg_W2", "agg_W1", "agg_W2", "out_W")]
    return np.concatenate(out, axis=0)


def lay_out(v):
    a = {"x": v["x"], "node_type_6": v["node_type_6"], "weights": weight_stack(v), "consts": constants()}
    for n in ("L0_gnn_query_embs", "L3_gnn_edge_W2", "L3_gnn_edge_b2", "L3_gnn_msg_b2", "L3_gnn_ln_g", "L3_gnn_ln_b"):
        a[n] = v[n]
    a["edges"] = np.stack([v["src"], v["dst"], v["edge_type_3"]])
    a["edges_by_tile"] = a["edges"].reshape(3, TILES, P).transpose(2, 0, 1)
    a["edge_attr_T"] = v["edge_attr_32"].T
    a["edge_w1b"] = np.concatenate([v["L3_gnn_edge_W1"], v["L3_gnn_edge_b1"][None]])
    q = v["L0_gnn_query_embs"].reshape(B, HL, 2, D).transpose(3, 0, 2, 1)
    a["query_T"] = q.reshape(D, B * L)
    stack = np.zeros((P, D), np.float32)
    names = ["L0_gnn_b1", "L0_gnn_b2", "L0_gnn_bg", "L0_gnn_bq", "L3_gnn_msg_b1", "L3_gnn_agg_b1", "L3_gnn_agg_b2", "L3_gnn_out_b"]
    for half in (0, 64):
        for i, n in enumerate(names):
            stack[half + i] = v[n]
        stack[half + TYPE_ROW:half + TYPE_ROW + NTYPE] = v["L3_gnn_b_type"]
    a["biases"] = stack
    a["att_gat1"] = np.stack([v["L1_gnn_att_dst1"], v["L1_gnn_att_src1"]])
    a["att_gat2"] = np.stack([v["L1_gnn_att_dst2"], v["L1_gnn_att_src2"]])
    a["att_rgat1"] = np.concatenate([v["L2_gnn_q1"].T, v["L2_gnn_k1"].T])
    a["att_rgat2"] = np.concatenate([v["L2_gnn_q2"].T, v["L2_gnn_k2"].T])
    for n, b in (("gat1", "L1_gnn_b1"), ("gat2", "L1_gnn_b2"), ("rgat1", "L2_gnn_b1"), ("rgat2", "L2_gnn_b2")):
        a["bias_" + n] = v[b]
    return {k: np.ascontiguousarray(t) for k, t in a.items()}


def program(nc, arrays):
    d = {}
    for name, a in arrays.items():
        d[name] = nc.dram_tensor("in_" + name, a.shape, mybir.dt.from_np(a.dtype), kind="ExternalInput").ap()
    d["out"] = nc.dram_tensor("out_x", (N, D), F32, kind="ExternalOutput").ap()
    d["hg_parts"] = nc.dram_tensor("hg_parts", (2, N, D), F32).ap()
    d["qg_parts"] = nc.dram_tensor("qg_parts", (2, B * L, D), F32).ap()
    d["qi"] = nc.dram_tensor("qi_rows", (N, D), F32).ap()
    build(nc, d)


def kernel(**inputs):
    import concourse.bacc as bacc
    from concourse.bass_utils import run_bass_kernel_spmd

    v = {k: np.asarray(a) for k, a in inputs.items()}
    arrays = lay_out(v)
    nc = bacc.Bacc("TRN2", target_bir_lowering=False, num_devices=1)
    program(nc, arrays)
    got = run_bass_kernel_spmd(nc, [{"in_" + k: a for k, a in arrays.items()}], core_ids=[0])
    return got.results[0]["out_x"]
```

```python
from contextlib import ExitStack

import numpy as np
import concourse.bass as bass
from concourse import mybir

F32 = mybir.dt.float32
F32R = mybir.dt.float32r
BF16 = mybir.dt.bfloat16
I32 = mybir.dt.int32
ALU = mybir.AluOpType
ACT = mybir.ActivationFunctionType

N, D, E, EA, H4, NREL, NTYPE = 256, 768, 8448, 32, 192, 3, 6
P = 128
NT = N // P
KB = D // P
HALF = D // 2
B, L, NB = 8, 64, N // 8
PAIRS = NB // 4
HL = L // 2
PIECES = 3
TILES = E // P
GROUP = 3
STEPS = TILES // (2 * GROUP)
SLOTS = 3
LAG = 3
AHEAD = 3
HEADS1 = 4
SLOPE = 0.2
LN_EPS = 1e-5
Z_EPS = 1e-16
NO_EDGE = -1e30

UNITS = (["qg0", "qg1"]
         + [f"{l}.{w}" for l in "ab" for w in ("rel0", "rel1", "rel2", "root", "hg", "al1", "al2")]
         + ["gat1.0", "gat2.0", "rgat1.0", "rgat1.1", "rgat1.2", "rgat2.0", "rgat2.1", "rgat2.2"]
         + [f"ty{t}" for t in range(NTYPE)] + ["msgA", "msgB", "msg2", "agg1", "agg2", "out"])


def attention_jobs(name, rels, heads):
    jobs = [f"T.{name}"] + [f"{name}.{r}" for r in range(rels)] + [f"{name}.row0"]
    for h in range(heads):
        jobs += [f"{name}.row{h + 1}"] * (h + 1 < heads) + [f"{name}.pt{h}", f"{name}.sum{h}"]
    return jobs


ATT = {"gat1": (1, 1), "gat2": (1, 1), "rgat1": (NREL, HEADS1), "rgat2": (NREL, 1)}
JOBS = (["T.a", "counts", "countT", "countrow", "qg0", "qg1"]
        + ["a.rel0", "a.rel1", "a.rel2", "a.root", "T.a.h", "a.hg", "a.al1", "T.a.qi", "a.al"]
        + ["T.b", "b.rel0", "b.rel1", "b.rel2", "b.root", "T.b.h", "b.hg", "b.al1", "T.b.qi", "b.al"]
        + [j for n, (r, h) in ATT.items() for j in attention_jobs(n, r, h)]
        + ["T.m", "m.h", "T.m.h", "msgA", "msgB", "edges",
           "T.agg", "msg2", "T.msg2", "agg1", "T.agg1", "agg2", "T.agg2", "out"])


def unit(name):
    return UNITS.index(name)


def job(name):
    return JOBS.index(name)


def ends_with(name):
    if name.endswith(".al"):
        return name + "2"
    return {"m.h": f"ty{NTYPE - 1}"}.get(name, name if name in UNITS and not name.endswith("root") else None)


def readers(name):
    if ".row" in name and name != "countrow" or ".pt" in name:
        return (True, False)
    if ".sum" in name or name in ("countrow", "msg2", "agg2", "out", "a.al", "b.al"):
        return (False, True)
    return (True, True)


def taken(name, who):
    return sum(readers(n)[who] for n in JOBS[:job(name) + 1])


BIASES = ["b1", "b2", "bg", "bq", "msg_b1", "agg_b1", "agg_b2", "out_b"]
TYPE_ROW = 32
ATTVEC = 2 * HEADS1
C_PAT, C_SEL = 0, PAIRS * P
C_ID = C_SEL + len(BIASES) * P
C_RED = C_ID + P
C_IOTA = C_RED + PAIRS * 32
C_NODE = C_IOTA + NREL * N
C_TYPE = C_NODE + NT
C_END = C_TYPE + 1


def constants():
    c = np.zeros((P, C_END), np.float32)
    p = np.arange(P)
    col = np.arange(P)
    for j in range(PAIRS):
        node = (p[:, None] < 64) & (p[:, None] % 32 == 4 * j + col[None] // 32)
        query = (p[:, None] >= 64) & (p[:, None] % 32 == col[None] % 32)
        c[:, C_PAT + j * P:C_PAT + (j + 1) * P] = node | query
        c[:, C_RED + j * 32:C_RED + (j + 1) * 32] = np.arange(32)[None] == 4 * j + p[:, None] // 32
    for i in range(len(BIASES)):
        c[:, C_SEL + i * P:C_SEL + (i + 1) * P] = (p % 64 == i)[:, None]
    c[:, C_ID:C_ID + P] = np.eye(P)
    c[:, C_IOTA:C_IOTA + NREL * N] = np.arange(NREL * N)[None]
    for t in range(NT):
        c[:, C_NODE + t] = p + t * P
    c[:, C_TYPE] = p % 64 - TYPE_ROW
    return c


def build(nc, d):
    with ExitStack() as ctx:
        def sb(name, shape, dt=F32):
            return ctx.enter_context(nc.sbuf_tensor(name, shape, dt))

        def sem(name):
            return ctx.enter_context(nc.semaphore(name))

        raw = sb("raw", [P, PIECES, 2, D])
        whi = sb("whi", [P, PIECES, 2, D], F32R)
        wlo = sb("wlo", [P, PIECES, 2, D], F32R)
        thi = sb("thi", [P, 2, KB, N], F32R)
        tlo = sb("tlo", [P, 2, KB, N], F32R)
        x = sb("x", [P, NT, D])
        nat = sb("nat", [P, NT, D])
        tmp = sb("tmp", [P, NT, D])
        cnt = sb("cnt", [P, NT, NREL * N])
        sel = sb("sel", [P, len(BIASES), P], F32R)
        bias = sb("bias", [P, D], F32R)
        cst = sb("cst", [P, C_END - C_ID])
        ident = cst[:, 0:P]
        red = cst[:, C_RED - C_ID:C_IOTA - C_ID].rearrange("p (j c) -> p j c", c=32)
        iota = cst[:, C_IOTA - C_ID:C_NODE - C_ID]
        node_id = cst[:, C_NODE - C_ID:C_TYPE - C_ID]
        type_id = cst[:, C_TYPE - C_ID:C_END - C_ID]
        idx = sb("idx", [P, 3, TILES], I32)
        idf = sb("idf", [P, 2, TILES])
        ew = sb("ew", [P, TILES])
        st6 = sb("st6", [P, NT, 2, 6])
        mv = sb("mv", [P, NT, 2])
        rstd = sb("rstd", [P, NT, 2])
        sc = sb("sc", [P, NT, NREL, ATTVEC])
        mx = sb("mx", [P, NT, 4])
        b2e = sb("b2e", [P, 1])
        w2e = sb("w2e", [P, H4])
        w1e = sb("w1e", [EA + 1, H4])
        onec = sb("onec", [P, P])
        types = sb("types", [P, N], I32)
        tyhot = sb("tyhot", [P, N], F32R)
        sew = sb("sew", [P, NT])
        src_col = sb("src_col", [P, AHEAD], I32)

        R = sb("R", [P, 11528], F32R)
        G = sb("G", [P, 10752])

        def r(a, *dims):
            return cut(R, a, dims)

        def g(a, *dims):
            return cut(G, a, dims)

        def cut(t, a, dims):
            n = int(np.prod(dims))
            v = t[:, a:a + n]
            if len(dims) == 1:
                return v
            names = "abcd"[:len(dims)]
            kw = {c: dims[i] for i, c in enumerate(names) if i}
            return v.rearrange(f"p ({' '.join(names)}) -> p {' '.join(names)}", **kw)

        pat = r(0, PAIRS, P)
        qhi, qlo = r(1024, KB, B * L), r(4096, KB, B * L)
        stack = r(1024, 2, 2, D)
        ghi, glo = r(7168, NT, D), r(8704, NT, D)
        mhi, mlo = r(0, 2, KB, N), r(3072, 2, KB, N)
        hB = r(0, NT, 2, D)
        ohg = r(3072, 2 * GROUP, NT, P)
        ohs = r(4608, 2 * GROUP, N)
        ewp = r(6144, 2, TILES)
        msg = r(8448, 2, 2, D + 2)
        half_bias = r(7168, D)

        qraw = g(0, KB, B * L)
        cT = g(4608, NT, NREL * N)
        inv = g(6144, NREL * N)
        oh = G[:, 6912:8448].bitcast(BF16).rearrange("p (s c) -> p s c", s=GROUP)
        ea = g(8448, 2, GROUP * P)
        z1 = g(3072, GROUP, H4)
        craw = g(4608, C_ID)
        braw = g(6912, D)
        norm = g(9216, NT, NREL * N)
        xr = g(0, NREL, NT, D)
        qrep = g(0, 2, 2, D)
        prod = g(3072, 4, 2, D)
        psumm = raw[:, 0]
        qis = raw[:, 1, 0]
        qir = g(3072, NT, D)
        vec = g(4608, ATTVEC, D)
        esc = g(4608, 2, NREL * N)
        pt = g(6144, 2, 2 * NREL, N)
        brow = g(9216, D)
        m32 = g(0, 2, D)
        ixe = G[:, 1536:1536 + 2 * GROUP * P].bitcast(I32).rearrange("p (s e) -> p s e", s=2)
        gsum = g(2304, 2, D)
        hA = g(8448, AHEAD, D)
        xin = g(4608, NT, D)
        b2row = g(6144, D)
        lng, lnb = g(6912, D), g(7680, D)

        ps = ctx.enter_context(nc.psum_tensor("ps", [P, 8, 512], F32))

        def flat(j, n):
            s = 4 * (j % 2)
            return ps[:, s:s + 4, :].rearrange("p b c -> p (b c)")[:, 0:n]

        def rows(j, t, w=HALF):
            s = 4 * (j % 2) + 2 * t
            return ps[:, s:s + 2, 0:w]

        def two(ap):
            return ap.rearrange("p (h c) -> p h c", h=2)

        raw_here = [sem(f"raw_here{s}") for s in range(PIECES)]
        w_hi = sem("w_hi")
        w_lo = sem("w_lo")
        w_used = sem("w_used")
        aux_done = sem("aux_done")
        act_took = sem("act_took")
        dve_took = sem("dve_took")
        t_hi = sem("t_hi")
        t_lo = sem("t_lo")
        rows_here = sem("rows_here")
        act_step = sem("act_step")
        dve_step = sem("dve_step")
        x_here = sem("x_here")
        cst_here = sem("cst_here")
        idx_here = sem("idx_here")
        edge_cst_here = sem("edge_cst_here")
        q_here = sem("q_here")
        set_up = sem("set_up")
        ones_set = sem("ones_set")
        ea_here = [sem(f"ea_here{s}") for s in range(2)]
        oh_here = sem("oh_here")
        oh_used = sem("oh_used")
        z_here = sem("z_here")
        z_read = sem("z_read")
        q_split = sem("q_split")
        parts_here = sem("parts_here")
        parts_stored = sem("parts_stored")
        stack_here = [sem(f"stack_here{s}") for s in range(2)]
        qrep_here = [sem(f"qrep_here{s}") for s in range(2)]
        add_done = [sem(f"add_done{s}") for s in range(SLOTS)]
        sig_done = [sem(f"sig_done{s}") for s in range(SLOTS)]
        mul_done = [sem(f"mul_done{s}") for s in range(SLOTS)]
        sum_done = [sem(f"sum_done{s}") for s in range(2)]
        sum_used = [sem(f"sum_used{s}") for s in range(2)]
        red_took = sem("red_took")
        qi_stored = [sem(f"qi_stored{s}") for s in range(2)]
        qi_here = sem("qi_here")
        al_sum = sem("al_sum")
        al_here = sem("al_here")
        std_here = sem("std_here")
        var_here = sem("var_here")
        vec_here = sem("vec_here")
        brow_here = sem("brow_here")
        sc_here = sem("sc_here")
        e_here = sem("e_here")
        max_here = sem("max_here")
        p_here = sem("p_here")
        pw_here = sem("pw_here")
        pt_here = sem("pt_here")
        elu_in = sem("elu_in")
        elu_exp = sem("elu_exp")
        ty_here = sem("ty_here")
        tyhot_here = sem("tyhot_here")
        m_here = sem("m_here")
        AB_here = sem("AB_here")
        ixe_here = [sem(f"ixe_here{s}") for s in range(2)]
        hA_stored = sem("hA_stored")
        src_set = sem("src_set")
        hA_here = [sem(f"hA_here{s}") for s in range(AHEAD)]
        ew_split = sem("ew_split")
        ohg_here = sem("ohg_here")
        gat_done = sem("gat_done")
        gsum_here = sem("gsum_here")
        m32_here = sem("m32_here")
        sew_here = sem("sew_here")
        msg_here = sem("msg_here")
        scat_done = sem("scat_done")
        late_here = sem("late_here")
        out_stored = sem("out_stored")

        block = ctx.enter_context(nc.Block())

        def reached(eng, s, i, per, more):
            if not isinstance(i, int):
                eng.wait_ge(s, i * per + more)
            elif i * per + more > 0:
                eng.wait_ge(s, i * per + more)

        def ready(eng, name):
            u = ends_with(name)
            if u:
                eng.wait_ge(w_used, PIECES * (unit(u) + 1))
            else:
                eng.wait_ge(aux_done, sum(ends_with(n) is None for n in JOBS[:job(name) + 1]))

        def wait_taken(eng, name):
            if readers(name)[0]:
                eng.wait_ge(act_took, taken(name, 0))
            if readers(name)[1]:
                eng.wait_ge(dve_took, taken(name, 1))

        TJOBS = [n for n in JOBS if n[:2] == "T."]

        def turn(name):
            return TJOBS.index("T." + name)

        PARTNER = {"a.h": "a.root", "b.h": "b.root", "m.h": "m.h", "agg": "edges", "agg1": "agg1"}
        BY_DVE = [n[2:] for n in TJOBS if n[2:] not in PARTNER and not n.endswith("qi")]
        GATES = {"a": 0, "b": 1}
        NORMS = ["a", "gat1", "rgat1", "m", "end"]
        RELU_TURNS = {"a", "gat1", "gat2", "rgat1", "m", "agg1"}
        att_names = list(ATT)
        heads_before = {n: sum(ATT[m][1] for m in att_names[:i]) for i, n in enumerate(att_names)}

        def turn_of(k, a):
            n = 2 * k + a
            return n % SLOTS, (4 * PAIRS - n % SLOTS + SLOTS - 1) // SLOTS, n // SLOTS

        def turns_done(eng, sems, i, l, k, a, more):
            s, per, n = turn_of(k, a)
            reached(eng, sems[s], i, per, 4 * per * l + n + more)

        def slot(k, a):
            s = turn_of(k, a)[0]
            return ps[:, 2 * s:2 * s + 2, 0:HALF]

        @block.sync
        def _(sp):
            sp.dma_start(x[:], d["x"].rearrange("(t p) f -> p t f", p=P)).then_inc(x_here, 16)

            def weights(a, b):
                w = d["weights"].rearrange("(u i k p) f -> (u i) p k f", i=PIECES, k=2, p=P)

                def load(u):
                    for i in range(PIECES):
                        if isinstance(u, int) and u == 0:
                            pass
                        else:
                            sp.wait_ge(w_lo, u * PIECES + (i + 1 - PIECES))
                        sp.dma_start(raw[:, i], w[bass.ds(u * PIECES + i, 1)].rearrange("o p k f -> (o p) k f")
                                     if not isinstance(u, int) else w[u * PIECES + i]).then_inc(raw_here[i], 16)

                if a == 0:
                    load(0)
                    a = 1
                with sp.Fori(a, b) as u:
                    load(u)

            def gate_loads(l):
                hg, qg = d["hg_parts"], d["qg_parts"]
                q = d["L0_gnn_query_embs"].rearrange("b (l a) f -> (b l) a f", a=2)

                def load(b, s):
                    st = stack[:, s].bitcast(F32)
                    for part in range(2):
                        v = hg[part][bass.ds(b * NB, NB), :].rearrange("n (a f) -> n a f", a=1)
                        sp.dma_start(st[32 * part:32 * part + 32], v.to_broadcast([NB, 2, D])).then_inc(stack_here[s], 16)
                        v = qg[part][bass.ds(b * L, L), :].rearrange("(a l) f -> l a f", a=2)
                        sp.dma_start(st[64 + 32 * part:96 + 32 * part], v).then_inc(stack_here[s], 16)
                    for k in range(4):
                        sp.dma_start(qrep[32 * k:32 * k + 32, s], q[bass.ds(b * HL, HL)]).then_inc(qrep_here[s], 16)

                sp.wait_ge(parts_stored, 16 * (2 * 2 + 2 * (l + 1)))
                ready(sp, "ab"[l] + ".root")
                for s in range(2):
                    load(s, s)
                with sp.Fori(1, B // 2) as i:
                    for s in range(2):
                        turns_done(sp, add_done, i - 1, l, PAIRS * s + PAIRS - 1, 1, 1)
                        turns_done(sp, mul_done, i - 1, l, PAIRS * s + PAIRS - 1, 1, 1)
                        load(i * 2 + s, s)

            def gate_reload(l):
                for s in range(2):
                    sp.wait_ge(qi_stored[s], 16 * 4 * (l + 1))
                sp.dma_start(qir, d["qi"].rearrange("(t p) f -> p t f", p=P)).then_inc(qi_here, 16)

            weights(0, unit("a.al2") + 1)
            gate_loads(0)
            gate_reload(0)
            weights(unit("b.rel0"), unit("b.al2") + 1)
            gate_loads(1)
            gate_reload(1)
            weights(unit("gat1.0"), len(UNITS))
            ready(sp, "out")
            sp.wait_ge(rows_here, len(BY_DVE) + 1)
            sp.dma_start(d["out"].rearrange("(t p) f -> p t f", p=P), x[:]).then_inc(out_stored, 16)
            sp.wait_ge(out_stored, 16)

        @block.gpsimd
        def _(pool):
            pool.memset(onec[:], 1.0).then_inc(ones_set, 1)
            pool.wait_ge(ones_set, 1)

            def edge_attributes(i):
                for s in range(2):
                    reached(pool, z_here, i, 2 * GROUP, GROUP * (s - 1))
                    pool.dma_start(ea[0:EA, s, :], d["edge_attr_T"][:, bass.ds((i * 2 + s) * GROUP * P, GROUP * P)]).then_inc(ea_here[s], 16)

            edge_attributes(0)
            with pool.Fori(1, STEPS) as i:
                edge_attributes(i)
            for l in range(2):
                def gate_sums(i):
                    for k in range(2 * PAIRS):
                        s = k % 2
                        turns_done(pool, mul_done, i, l, k, 0, 1)
                        turns_done(pool, mul_done, i, l, k, 1, 1)
                        reached(pool, sum_used[s], i, 8, 32 * l + k // 2)
                        pool.tensor_tensor(psumm[:, s], prod[:, k % 4, 0], prod[:, k % 4, 1], ALU.add).then_inc(sum_done[s], 1)

                gate_sums(0)
                with pool.Fori(1, B // 2) as i:
                    gate_sums(i)
            for n, name in enumerate(att_names):
                rels, heads = ATT[name]
                pool.wait_ge(rows_here, BY_DVE.index(name) + 1)
                pool.dma_start(vec[:, 0:2 * heads, :], d["att_" + name].rearrange("(o v) f -> o v f", o=1).to_broadcast([P, 2 * heads, D])).then_inc(vec_here, 16)
                pool.wait_ge(sc_here, n + 1)
                pool.dma_start(brow, d["bias_" + name].rearrange("(o f) -> o f", o=1).to_broadcast([P, D])).then_inc(brow_here, 16)
            wait_taken(pool, "rgat2.sum0")
            for row, place in (("L3_gnn_msg_b2", b2row), ("L3_gnn_ln_g", lng), ("L3_gnn_ln_b", lnb)):
                pool.dma_start(place, d[row].rearrange("(o f) -> o f", o=1).to_broadcast([P, D])).then_inc(late_here, 16)
            wait_taken(pool, "msgA")
            pool.dma_start(d["hA"].rearrange("(t p) f -> p t f", p=P), tmp[:]).then_inc(hA_stored, 16)

            def load_indices(i, s):
                reached(pool, ohg_here, i, 6, GROUP * (s - 1))
                pool.dma_start(ixe[:, s], d["edges"][1:2, bass.ds((i * 2 + s) * GROUP * P, GROUP * P)].to_broadcast([P, GROUP * P])).then_inc(ixe_here[s], 16)

            def set_sources(i, q):
                k = q % AHEAD
                reached(pool, gsum_here, i, 6, q + 1 - AHEAD)
                pool.tensor_copy(src_col[:, k:k + 1], idx[:, 0, bass.ds(i * 6 + q, 1)]).then_inc(src_set, 1)
                pool.wait_ge(src_set, i * 6 + (q + 1))

            def gather_sources(q):
                k = q % AHEAD
                pool.indirect_dma_start(hA[:, k], None, d["hA"], bass.IndirectOffsetOnAxis(ap=src_col[:, k:k + 1], axis=0)).then_inc(hA_here[k], 16)

            def pool_tiles(i, last):
                for q in range(6):
                    if q + 2 < 6:
                        set_sources(i, q + 2)
                    elif not last:
                        set_sources(i + 1, q - 4)
                    reached(pool, scat_done, i, 6, q - 1)
                    pool.tensor_copy(msg[:, q % 2, :, D:D + 1], ewp[:, :, bass.ds(i * 6 + q, 1)]).then_inc(sew_here, 1)
                    if q + 2 < 6 or not last:
                        gather_sources(q + 2)
                    if q in (1, 4) and not last:
                        load_indices(i + 1, q // GROUP)

            for s in range(2):
                load_indices(0, s)
            pool.wait_ge(hA_stored, 16)
            for q in range(2):
                set_sources(0, q)
                gather_sources(q)
            pool.wait_ge(ew_split, 1)
            pool_tiles(0, False)
            with pool.Fori(1, STEPS - 1) as i:
                pool_tiles(i, False)
            pool_tiles(STEPS - 1, True)

        @block.scalar
        def _(act):
            steps = [0]

            def step(ins):
                steps[0] += 1
                ins.then_inc(act_step, 1)
                act.wait_ge(act_step, steps[0])

            made = [0]

            def split_to(u, i):
                while made[0] <= PIECES * u + i and made[0] < PIECES * len(UNITS):
                    p = made[0]
                    act.wait_ge(raw_here[p % PIECES], 16 * (p // PIECES + 1))
                    if p >= PIECES:
                        act.wait_ge(w_used, p - PIECES + 1)
                    act.activation(whi[:, p % PIECES], raw[:, p % PIECES], ACT.Copy).then_inc(w_hi, 1)
                    made[0] += 1

            def columns(name, func=None):
                n = turn(name)
                ready(act, "T." + name)
                f = ACT.Relu if name in RELU_TURNS else ACT.Copy
                j = job("T." + name)
                for i in range(3):
                    src = ps[:, 4 * (j % 2) + i, :].rearrange("p (k n) -> p k n", k=2)
                    ins = act.activation(thi[:, n % 2, 2 * i:2 * i + 2], src, f)
                    ins.then_inc(t_hi, 1)
                act.wait_ge(t_hi, 3 * n + 3)
                act.sem_inc(act_took, 1)

            def take(name, dst, func=ACT.Copy, t=0):
                ready(act, name)
                act.activation(two(dst), rows(job(name), t), func).then_inc(act_took, 1)

            act.dma_start(craw, d["consts"][:, 0:C_ID]).then_inc(cst_here, 16)
            act.dma_start(cst[:], d["consts"][:, C_ID:C_END]).then_inc(cst_here, 16)
            act.dma_start(braw, d["biases"]).then_inc(cst_here, 16)
            act.dma_start(idx[:], d["edges_by_tile"]).then_inc(idx_here, 16)
            act.dma_start(w1e[:], d["edge_w1b"]).then_inc(edge_cst_here, 16)
            act.dma_start(w2e[:], d["L3_gnn_edge_W2"].rearrange("f o -> o f").to_broadcast([P, H4])).then_inc(edge_cst_here, 16)
            act.dma_start(b2e[:], d["L3_gnn_edge_b2"].rearrange("(o f) -> o f", o=1).to_broadcast([P, 1])).then_inc(edge_cst_here, 16)
            act.dma_start(qraw, d["query_T"].rearrange("(k p) n -> p k n", p=P)).then_inc(q_here, 16)
            act.dma_start(types[:], d["node_type_6"].rearrange("(o n) -> o n", o=1).to_broadcast([P, N])).then_inc(ty_here, 16)

            def norm_std(n):
                act.wait_ge(var_here, n + 1)
                act.activation(rstd[:, :, 0], mv[:, :, 1], ACT.Sqrt).then_inc(std_here, 1)

            norm_std(0)
            columns("a")
            act.wait_ge(q_here, 16)
            act.activation(qhi, qraw, ACT.Copy).then_inc(q_split, 1)
            split_to(unit("qg0"), 2)
            take("counts", cT[:, 0])
            act.wait_ge(z_read, TILES)
            act.wait_ge(edge_cst_here, 48)
            act.activation(ew[:], ew[:], ACT.Sigmoid, bias=b2e[:, 0:1]).then_inc(act_step, 1)
            steps[0] += 1
            ready(act, "countT")
            act.activation(cnt[:].rearrange("p t c -> p (t c)")[:, 0:1024], flat(job("countT"), 1024), ACT.Copy).then_inc(act_took, 1)

            def split_parts(name, dram, at):
                ready(act, name)
                if at > 0:
                    act.wait_ge(parts_stored, 16 * 2 * at)
                for t in range(NT):
                    ins = act.activation(two(ghi[:, t]), rows(job(name), t), ACT.Copy)
                ins.then_inc(act_took, 1)
                act.wait_ge(act_took, taken(name, 0))
                act.dma_start(dram[0], ghi.bitcast(F32)).then_inc(parts_stored, 16)
                act.wait_ge(parts_here, at + 1)
                act.dma_start(dram[1], glo.bitcast(F32)).then_inc(parts_stored, 16)

            for i in range(2):
                split_to(unit(f"qg{i}") + 1, 1)
                split_parts(f"qg{i}", [d["qg_parts"][part][i * N:(i + 1) * N].rearrange("(t p) f -> p t f", p=P) for part in range(2)], i)

            for l, L_ in enumerate("ab"):
                if l:
                    columns("b")
                for k in range(NREL):
                    split_to(unit(f"{L_}.rel{k}") + 1, 1)
                    take(f"{L_}.rel{k}", xr[:, k, 0])
                split_to(unit(L_ + ".hg"), 1)
                take(L_ + ".root", nat[:, 0], ACT.Relu)
                columns(L_ + ".h")
                split_to(unit(L_ + ".al1"), 1)
                split_parts(L_ + ".hg", [d["hg_parts"][part].rearrange("(t p) f -> p t f", p=P) for part in range(2)], 2 + l)
                split_to(unit(L_ + ".al2"), 1)
                take(L_ + ".al1", tmp[:, 0])
                split_to(unit(L_ + ".al2"), 2)

                def store_qi(b, s):
                    i4 = b if isinstance(b, int) else None
                    act.wait_ge(sum_used[(PAIRS - 1) % 2], b * (PAIRS // 2) + (32 * l + PAIRS // 2))
                    if i4 is None or i4 >= 2:
                        act.wait_ge(qi_stored[s], (b - s) * 8 + 64 * l)
                    elif l:
                        act.wait_ge(qi_stored[s], 64)
                    act.activation(two(qis[32 * s:32 * s + 32]), ps[32 * s:32 * s + 32, 6:8, 0:HALF], ACT.Copy).then_inc(red_took, 1)
                    act.wait_ge(red_took, b + (8 * l + 1))
                    act.dma_start(d["qi"][bass.ds(b * NB, NB), :], qis[32 * s:32 * s + 32]).then_inc(qi_stored[s], 16)

                def gate_steps(i):
                    for k in range(2 * PAIRS):
                        for a in range(2):
                            turns_done(act, add_done, i, l, k, a, 1)
                            act.activation(slot(k, a), slot(k, a), ACT.Sigmoid).then_inc(sig_done[turn_of(k, a)[0]], 1)
                        if k == 4 and not isinstance(i, int):
                            store_qi(i * 2 - 1, 1)
                        if k == 12:
                            store_qi(i * 2, 0)

                gate_steps(0)
                with act.Fori(1, B // 2) as i:
                    gate_steps(i)
                store_qi(B - 1, 1)

                columns(L_ + ".qi")
                split_to(unit(L_ + ".al2") + 1, 1)
                act.wait_ge(qi_here, 16 * (l + 1))
                ready(act, "T." + L_ + ".qi")
                act.activation(qir, qir, ACT.Tanh).then_inc(al_here, 1)
                for t in range(NT):
                    act.wait_ge(al_sum, NT * l + t + 1)
                    act.activation(tmp[:, t], tmp[:, t], ACT.Sigmoid).then_inc(al_here, 1)

            for n, name in enumerate(att_names):
                rels, heads = ATT[name]
                w = rels * N
                if name in NORMS:
                    norm_std(NORMS.index(name))
                columns(name)
                for k in range(rels):
                    split_to(unit(f"{name}.{k}") + 1, 1)
                    take(f"{name}.{k}", xr[:, k, 0])
                base = heads_before[name]

                def scores(h):
                    hh = base + h
                    ready(act, f"{name}.row{h}")
                    act.wait_ge(sc_here, n + 1)
                    for t in range(NT):
                        if hh:
                            if h:
                                ready(act, f"{name}.pt{h - 1}")
                        for k in range(rels):
                            ins = act.activation(esc[:, t, k * N:(k + 1) * N], flat(job(f"{name}.row{h}"), w)[:, k * N:(k + 1) * N],
                                                 ACT.Identity, bias=sc[:, t, k, h:h + 1])
                            if k == rels - 1:
                                ins.then_inc(e_here, 1)
                    act.wait_ge(e_here, NT * (hh + 1))
                    act.sem_inc(act_took, 1)

                def exps(h):
                    hh = base + h
                    for t in range(NT):
                        act.wait_ge(max_here, NT * hh + t + 1)
                        act.activation(esc[:, t, 0:w], esc[:, t, 0:w], ACT.Exp, bias=mx[:, t, 0:1]).then_inc(p_here, 1)

                for h in range(heads):
                    hh = base + h
                    scores(h)
                    exps(h)
                    ready(act, f"{name}.pt{h}")
                    if h >= 2:
                        ready(act, f"{name}.sum{h - 2}")
                    act.activation(pt[:, h % 2, 0:2 * rels].rearrange("p a b -> p (a b)"), flat(job(f"{name}.pt{h}"), 2 * rels * N), ACT.Copy).then_inc(act_took, 1)
                if name == "rgat1":
                    for t in range(NT):
                        act.wait_ge(elu_in, t + 1)
                        act.activation(esc[:, t], esc[:, t], ACT.Exp).then_inc(elu_exp, 1)

            norm_std(NORMS.index("m"))
            columns("m")
            for t in range(NTYPE):
                split_to(unit(f"ty{t}") + 1, 1)
            take("m.h", nat[:, 0])
            columns("m.h")
            split_to(unit("msgB"), 1)
            take("msgA", tmp[:, 0])
            split_to(unit("msg2"), 1)
            ready(act, "msgB")
            for t in range(NT):
                ins = act.activation(two(hB[:, t, 0]), rows(job("msgB"), t), ACT.Copy)
                if t == 0:
                    step(ins)
            ins.then_inc(act_took, 1)
            split_to(unit("msg2"), 2)

            def messages(i):
                for q in range(2 * GROUP):
                    m = q % 2
                    act.wait_ge(gsum_here, i * 6 + (q + 1))
                    reached(act, msg_here, i, 6, q - 1)
                    reached(act, scat_done, i, 6, q - 1)
                    w = ew[:, bass.ds(i * 6 + q, 1)]
                    act.activation(msg[:, m, 0, 0:D], gsum[:, m], ACT.Relu, scale=w).then_inc(m32_here, 1)
                    act.activation(m32[:, m], gsum[:, m], ACT.Relu, scale=w).then_inc(m32_here, 1)

            messages(0)
            with act.Fori(1, STEPS) as i:
                messages(i)
            ready(act, "edges")
            step(act.activation(sew[:, 0:1], rows(job("edges"), 0, HALF + 1)[:, 1, HALF:HALF + 1], ACT.Copy))
            act.activation(two(tmp[:, 0]), rows(job("edges"), 0), ACT.Copy).then_inc(act_took, 1)
            columns("agg")
            split_to(unit("agg1"), 1)
            columns("msg2")
            split_to(unit("agg2"), 1)
            take("agg1", tmp[:, 0])
            columns("agg1")
            split_to(unit("out"), 1)
            columns("agg2")
            split_to(unit("out"), 2)
            norm_std(NORMS.index("end"))

        @block.vector
        def _(dve):
            steps = [0]

            def step(ins):
                steps[0] += 1
                ins.then_inc(dve_step, 1)
                dve.wait_ge(dve_step, steps[0])

            made = [0]

            def split_to(u, i):
                while made[0] <= PIECES * u + i and made[0] < PIECES * len(UNITS):
                    p = made[0]
                    dve.wait_ge(w_hi, p + 1)
                    dve.tensor_tensor(wlo[:, p % PIECES], raw[:, p % PIECES], whi[:, p % PIECES], ALU.subtract).then_inc(w_lo, 1)
                    made[0] += 1

            def columns(name):
                n = turn(name)
                j = job("T." + name)
                for i in range(3):
                    dve.wait_ge(t_hi, 3 * n + i + 1)
                    src = ps[:, 4 * (j % 2) + i, :].rearrange("p (k n) -> p k n", k=2)
                    hi, lo = thi[:, n % 2, 2 * i:2 * i + 2], tlo[:, n % 2, 2 * i:2 * i + 2]
                    if name in RELU_TURNS:
                        ins = dve.scalar_tensor_tensor(lo, src, 0.0, hi, ALU.max, ALU.subtract)
                    else:
                        ins = dve.tensor_tensor(lo, src, hi, ALU.subtract)
                    ins.then_inc(t_lo, 1)
                dve.wait_ge(t_lo, 3 * n + 3)
                dve.sem_inc(dve_took, 1)

            def take(name, dst, relu=False, t=1):
                ready(dve, name)
                if relu:
                    ins = dve.tensor_scalar(two(dst), rows(job(name), t), 0.0, None, ALU.max)
                else:
                    ins = dve.tensor_copy(two(dst), rows(job(name), t))
                ins.then_inc(dve_took, 1)

            def normalise(src, dst, n):
                for t in range(NT):
                    for h in range(2):
                        step(dve.bn_stats(st6[:, t, h, :], src[:, t, h * HALF:(h + 1) * HALF]))
                    step(dve.bn_aggr(mv[:, t, :], st6[:, t].rearrange("p a b -> p (a b)")))
                dve.tensor_scalar(mv[:, :, 1], mv[:, :, 1], LN_EPS, None, ALU.add).then_inc(var_here, 1)
                dve.wait_ge(std_here, n + 1)
                step(dve.reciprocal(rstd[:, :, 1], rstd[:, :, 0]))
                for t in range(NT):
                    ins = dve.tensor_scalar(dst[:, t], src[:, t], mv[:, t, 0:1], rstd[:, t, 1:2], ALU.subtract, ALU.mult)
                    if t == 0:
                        step(ins)
                return ins

            dve.wait_ge(x_here, 16)
            normalise(x, tmp, 0).then_inc(rows_here, 1)
            dve.wait_ge(idx_here, 16)
            step(dve.tensor_copy(idf[:, 0], idx[:, 0]))
            step(dve.tensor_scalar(idf[:, 1], idx[:, 2], float(N), None, ALU.mult))
            step(dve.tensor_tensor(idf[:, 1], idf[:, 1], idx[:, 1], ALU.add))
            dve.wait_ge(cst_here, 48)
            step(dve.tensor_copy(pat.rearrange("p a b -> p (a b)"), craw[:, 0:C_SEL]))
            step(dve.tensor_copy(sel[:].rearrange("p a b -> p (a b)"), craw[:, C_SEL:C_ID]))
            step(dve.tensor_copy(half_bias, braw))
            step(dve.tensor_tensor(bias[:], braw, half_bias, ALU.subtract))
            step(dve.tensor_copy(bias[0:64], braw[0:64]))
            step(dve.memset(ea[EA:EA + 1], 1.0))
            dve.wait_ge(ty_here, 16)
            dve.tensor_scalar(tyhot[:], types[:], type_id, None, ALU.is_equal).then_inc(set_up, 1)
            columns("a")
            dve.wait_ge(edge_cst_here, 48)

            def count_hot(i, q):
                e, k = bass.ds(i * 6 + q, 1), q % GROUP
                reached(dve, oh_used, i, 6, q - 2)
                dve.tensor_scalar(oh[:, k, 0:N], iota[:, 0:N], idf[:, 0, e], None, ALU.is_equal)
                dve.tensor_scalar(oh[:, k, N:], iota, idf[:, 1, e], None, ALU.is_equal).then_inc(oh_here, 1)

            def edge_logit(i, q):
                e, k = bass.ds(i * 6 + q, 1), q % GROUP
                dve.wait_ge(z_here, i * 6 + (q + 1))
                reached(dve, z_read, i, 6, q - 2)
                dve.scalar_tensor_tensor(z1[:, k], ps[:, k, 0:H4], 0.0, w2e[:], ALU.max, ALU.mult,
                                         accum_out=ew[:, e]).then_inc(z_read, 1)

            for q in range(6):
                count_hot(0, q)
                if q >= 2:
                    edge_logit(0, q - 2)
            with dve.Fori(1, STEPS) as i:
                for q in range(6):
                    count_hot(i, q)
                    edge_logit(i, q - 2)
            for q in (4, 5):
                edge_logit(STEPS - 1, q)
            dve.wait_ge(q_split, 1)
            dve.tensor_tensor(qlo, qraw, qhi, ALU.subtract).then_inc(q_split, 1)
            split_to(unit("qg0"), 2)
            take("counts", cT[:, 1])
            ready(dve, "countT")
            dve.tensor_copy(cnt[:].rearrange("p t c -> p (t c)")[:, 1024:1536], flat(job("countT"), 1536)[:, 1024:1536]).then_inc(dve_took, 1)
            ready(dve, "countrow")
            step(dve.tensor_scalar(two(inv), ps[:, 4 * (job("countrow") % 2):4 * (job("countrow") % 2) + 2, 0:HALF], 1.0, None, ALU.max))
            step(dve.reciprocal(inv, inv))
            step(dve.tensor_tensor(norm[:, 0], cT[:, 0], inv, ALU.mult))
            dve.tensor_tensor(norm[:, 1], cT[:, 1], inv, ALU.mult).then_inc(dve_took, 1)

            def split_parts(name, at):
                ready(dve, name)
                dve.wait_ge(act_took, taken(name, 0))
                if at > 0:
                    dve.wait_ge(parts_stored, 16 * 2 * at)
                for t in range(NT):
                    ins = dve.tensor_tensor(two(glo[:, t]), rows(job(name), t), two(ghi[:, t]), ALU.subtract)
                    if t == 0:
                        step(ins)
                ins.then_inc(parts_here, 1)
                dve.wait_ge(parts_here, at + 1)
                dve.sem_inc(dve_took, 1)

            for i in range(2):
                split_to(unit(f"qg{i}") + 1, 1)
                split_parts(f"qg{i}", i)

            for l, L_ in enumerate("ab"):
                if l:
                    columns("b")
                for k in range(NREL):
                    split_to(unit(f"{L_}.rel{k}") + 1, 1)
                    take(f"{L_}.rel{k}", xr[:, k, 1])
                split_to(unit(L_ + ".hg"), 1)
                take(L_ + ".root", nat[:, 1], relu=True)
                columns(L_ + ".h")
                split_to(unit(L_ + ".al1"), 1)
                split_parts(L_ + ".hg", 2 + l)
                split_to(unit(L_ + ".al2"), 1)
                take(L_ + ".al1", tmp[:, 1])
                split_to(unit(L_ + ".al2"), 2)

                def gate_products(i):
                    for k in range(2 * PAIRS):
                        s = k // PAIRS
                        if k % PAIRS == 0:
                            dve.wait_ge(qrep_here[s], i * 64 + (256 * l + 64))
                        for a in range(2):
                            turns_done(dve, sig_done, i, l, k, a, 1)
                            reached(dve, sum_done[k % 2], i, 8, 32 * l + k // 2 - 1)
                            dve.tensor_tensor(two(prod[:, k % 4, a]), slot(k, a), two(qrep[:, s, a]),
                                              ALU.mult).then_inc(mul_done[turn_of(k, a)[0]], 1)

                gate_products(0)
                with dve.Fori(1, B // 2) as i:
                    gate_products(i)
                columns(L_ + ".qi")
                split_to(unit(L_ + ".al2") + 1, 1)
                dve.wait_ge(al_here, 3 * l + 1)
                step(dve.tensor_tensor(qir, qir, nat[:], ALU.subtract))
                ready(dve, L_ + ".al")
                wait_taken(dve, L_ + ".al1")
                for t in range(NT):
                    ins = dve.tensor_tensor(two(tmp[:, t]), rows(job(L_ + ".al"), t), two(tmp[:, t]), ALU.add)
                    ins.then_inc(al_sum, 1)
                dve.wait_ge(al_here, 3 * l + 3)
                dve.sem_inc(dve_took, 1)
                step(dve.tensor_tensor(qir, qir, tmp[:], ALU.mult))
                ins = dve.tensor_tensor(tmp[:], qir, nat[:], ALU.add)
                if l == 0:
                    ins.then_inc(rows_here, 1)
                else:
                    step(ins)
                    step(dve.tensor_tensor(x[:], x[:], tmp[:], ALU.add))

            for n, name in enumerate(att_names):
                rels, heads = ATT[name]
                w = rels * N
                gat = rels == 1
                if name == "gat1":
                    c1, m1 = nat[:, :, N:2 * N], nat[:, :, 0:N]
                    step(dve.tensor_tensor(c1, cnt[:, :, 0:N], cnt[:, :, N:2 * N], ALU.add))
                    step(dve.tensor_tensor(c1, c1, cnt[:, :, 2 * N:3 * N], ALU.add))
                    for t in range(NT):
                        step(dve.tensor_tensor(c1[:, t, t * P:(t + 1) * P], c1[:, t, t * P:(t + 1) * P], ident, ALU.add))
                    step(dve.tensor_scalar(m1, c1, 0.0, NO_EDGE, ALU.is_equal, ALU.mult))
                    counts, mask = c1, m1
                if name == "rgat1":
                    step(dve.tensor_scalar(nat[:], cnt[:], 0.0, NO_EDGE, ALU.is_equal, ALU.mult))
                    counts, mask = cnt, nat
                if name in NORMS:
                    normalise(x, tmp, NORMS.index(name)).then_inc(rows_here, 1)
                columns(name)
                for k in range(rels):
                    split_to(unit(f"{name}.{k}") + 1, 1)
                    take(f"{name}.{k}", xr[:, k, 1])
                    dve.wait_ge(vec_here, 16 * (n + 1))
                    wait_taken(dve, f"{name}.{k}")
                    for t in range(NT):
                        for v in range(2 * heads):
                            ins = dve.tensor_tensor_reduce(tmp[:, 0], xr[:, k, t], vec[:, v], 1.0, 0.0,
                                                           ALU.mult, ALU.add, sc[:, t, k, v:v + 1])
                            if (k, t, v) != (rels - 1, NT - 1, 2 * heads - 1):
                                step(ins)
                ins.then_inc(sc_here, 1)
                dve.wait_ge(sc_here, n + 1)
                base = heads_before[name]
                for h in range(heads):
                    hh = base + h
                    for t in range(NT):
                        e = esc[:, t, 0:w]
                        dve.wait_ge(e_here, NT * hh + t + 1)
                        step(dve.scalar_tensor_tensor(e, e, SLOPE, e, ALU.mult, ALU.max))
                        step(dve.tensor_tensor_reduce(e, e, mask[:, t, 0:w], 1.0, NO_EDGE, ALU.add, ALU.max, mx[:, t, 1:2]))
                        dve.tensor_scalar(mx[:, t, 0:1], mx[:, t, 1:2], -1.0, None, ALU.mult).then_inc(max_here, 1)
                    for t in range(NT):
                        e = esc[:, t, 0:w]
                        dve.wait_ge(p_here, NT * hh + t + 1)
                        dve.tensor_tensor_reduce(e, e, counts[:, t, 0:w], 1.0, 0.0, ALU.mult, ALU.add, mx[:, t, 2:3]).then_inc(pw_here, 1)
                    dve.wait_ge(pw_here, NT * (hh + 1))
                    if not gat:
                        step(dve.tensor_scalar(mx[:, :, 2], mx[:, :, 2], Z_EPS, None, ALU.add))
                    step(dve.reciprocal(mx[:, :, 3], mx[:, :, 2]))
                    j = job(f"{name}.sum{h}")
                    c = D // heads
                    dve.wait_ge(brow_here, 16 * (n + 1))
                    ready(dve, f"{name}.sum{h}")
                    for t in range(NT):
                        if heads == 1:
                            o, i, b = two(tmp[:, t]), rows(j, t), two(brow)
                        else:
                            o, i, b = tmp[:, t, h * c:(h + 1) * c], ps[:, 4 * (j % 2) + 2 * t, 0:c], brow[:, h * c:(h + 1) * c]
                        ins = dve.scalar_tensor_tensor(o, i, mx[:, t, 3:4], b, ALU.mult, ALU.add)
                        if t == 0:
                            step(ins)
                    ins.then_inc(dve_took, 1)
                    dve.wait_ge(dve_took, taken(f"{name}.sum{h}", 1))
                if name == "gat1":
                    dve.sem_inc(rows_here, 1)
                elif name == "rgat1":
                    for t in range(NT):
                        dve.tensor_scalar(esc[:, t], tmp[:, t], 0.0, None, ALU.min).then_inc(elu_in, 1)
                    for t in range(NT):
                        dve.wait_ge(elu_exp, t + 1)
                        step(dve.scalar_tensor_tensor(tmp[:, t], tmp[:, t], 0.0, esc[:, t], ALU.max, ALU.add))
                    dve.tensor_scalar(tmp[:], tmp[:], -1.0, None, ALU.add).then_inc(rows_here, 1)
                else:
                    step(dve.tensor_tensor(x[:], x[:], tmp[:], ALU.add))

            normalise(x, tmp, NORMS.index("m")).then_inc(rows_here, 1)
            dve.wait_ge(rows_here, BY_DVE.index("m") + 1)
            step(dve.tensor_scalar(xin, tmp[:], 0.0, None, ALU.max))
            columns("m")
            n = turn("m") % 2
            ty = types[:].rearrange("p (a n) -> p a n", a=1).to_broadcast([P, KB, N])
            for t in range(NTYPE):
                if t >= 2:
                    dve.wait_ge(w_used, PIECES * (unit(f"ty{t - 2}") + 1))
                dve.scalar_tensor_tensor(mhi[:, t % 2], ty, float(t), thi[:, n], ALU.is_equal, ALU.mult).then_inc(m_here, 1)
                dve.scalar_tensor_tensor(mlo[:, t % 2], ty, float(t), tlo[:, n], ALU.is_equal, ALU.mult).then_inc(m_here, 1)
                split_to(unit(f"ty{t}") + 1, 0)
            take("m.h", nat[:, 1])
            columns("m.h")
            split_to(unit("msgB"), 1)
            take("msgA", tmp[:, 1])
            step(dve.tensor_copy(ewp[:, 0], ew[:]))
            step(dve.tensor_tensor(ewp[:, 1], ew[:], ewp[:, 0], ALU.subtract))
            step(dve.memset(m32[:, 0, 0:4], 0.0))
            dve.tensor_copy(msg[:, :, :, D + 1:D + 2], m32[:, 0, 0:4].rearrange("p (a b c) -> p a b c", a=2, b=2)).then_inc(ew_split, 1)
            step(dve.tensor_copy(idf[:, 1], idx[:, 1]))

            def onehots(i, q):
                s = q // GROUP
                dve.wait_ge(ixe_here[s], i * 16 + 16)
                reached(dve, scat_done, i, 6, q - 5)
                for t in range(NT):
                    dve.tensor_scalar(ohg[:, q, t], ixe[:, s, (q % GROUP) * P:(q % GROUP + 1) * P], node_id[:, t:t + 1], None, ALU.is_equal)
                dve.tensor_scalar(ohs[:, q], iota[:, 0:N], idf[:, 1, bass.ds(i * 6 + q, 1)], None, ALU.is_equal).then_inc(ohg_here, 1)

            def add_sources(i, q):
                m = q % 2
                dve.wait_ge(gat_done, i * 6 + (q + 1))
                dve.wait_ge(hA_here[q % AHEAD], i * 32 + 16 * (q // AHEAD + 1))
                reached(dve, m32_here, i, 12, 2 * (q - 1))
                dve.tensor_tensor(two(gsum[:, m]), ps[:, other + 2 * m:other + 2 * m + 2, 0:HALF], two(hA[:, q % AHEAD]), ALU.add).then_inc(gsum_here, 1)

            def split_message(i, q):
                m = q % 2
                dve.wait_ge(m32_here, i * 12 + 2 * (q + 1))
                dve.tensor_tensor(msg[:, m, 1, 0:D], m32[:, m], msg[:, m, 0, 0:D], ALU.subtract).then_inc(msg_here, 1)

            other = 4 * ((job("edges") + 1) % 2)
            for q in range(3):
                onehots(0, q)
            split_to(unit("msg2"), 1)
            ready(dve, "msgB")
            dve.wait_ge(act_took, taken("msgB", 0))
            for t in range(NT):
                ins = dve.tensor_tensor(two(hB[:, t, 1]), rows(job("msgB"), t), two(hB[:, t, 0]), ALU.subtract)
                if t == 0:
                    step(ins)
            ins.then_inc(dve_took, 1)
            split_to(unit("msg2"), 2)

            def edge_tiles(i, last):
                for q in range(6):
                    if q < 5:
                        add_sources(i, q + 1)
                    elif not last:
                        add_sources(i + 1, 0)
                    split_message(i, q)
                    if q < 3:
                        onehots(i, q + 3)
                    elif not last:
                        onehots(i + 1, q - 3)

            add_sources(0, 0)
            edge_tiles(0, False)
            with dve.Fori(1, STEPS - 1) as i:
                edge_tiles(i, False)
            edge_tiles(STEPS - 1, True)
            j = job("edges")
            ready(dve, "edges")
            step(dve.tensor_copy(sew[:, 1:2], rows(j, 1, HALF + 1)[:, 1, HALF:HALF + 1]))
            dve.tensor_copy(two(tmp[:, 1]), rows(j, 1)).then_inc(dve_took, 1)
            columns("agg")
            split_to(unit("agg1"), 1)
            dve.wait_ge(late_here, 48)
            ready(dve, "msg2")
            for t in range(NT):
                ins = dve.scalar_tensor_tensor(two(tmp[:, t]), two(b2row), sew[:, t:t + 1], rows(job("msg2"), t), ALU.mult, ALU.add)
                if t == 0:
                    step(ins)
            step(ins)
            dve.sem_inc(dve_took, 1)
            dve.sem_inc(rows_here, 1)
            columns("msg2")
            split_to(unit("agg2"), 1)
            take("agg1", tmp[:, 1])
            columns("agg1")
            split_to(unit("out"), 1)
            ready(dve, "agg2")
            for t in range(NT):
                step(dve.tensor_tensor(two(tmp[:, t]), rows(job("agg2"), t), two(nat[:, t]), ALU.add))
            dve.sem_inc(dve_took, 1)
            dve.sem_inc(rows_here, 1)
            columns("agg2")
            split_to(unit("out"), 2)
            ready(dve, "out")
            for t in range(NT):
                step(dve.tensor_tensor(two(tmp[:, t]), rows(job("out"), t), two(xin[:, t]), ALU.add))
            dve.sem_inc(dve_took, 1)
            step(normalise(tmp, nat, NORMS.index("end")))
            for t in range(NT):
                step(dve.tensor_tensor(nat[:, t], nat[:, t], lng, ALU.mult))
                step(dve.tensor_tensor(nat[:, t], nat[:, t], lnb, ALU.add))
            dve.tensor_tensor(x[:], x[:], nat[:], ALU.add).then_inc(rows_here, 1)

        @block.tensor
        def _(pe):
            def open_job(name):
                j = job(name)
                if j >= 2:
                    wait_upto(j - 2)

            def wait_upto(j):
                a, v = sum(readers(n)[0] for n in JOBS[:j + 1]), sum(readers(n)[1] for n in JOBS[:j + 1])
                if a:
                    pe.wait_ge(act_took, a)
                if v:
                    pe.wait_ge(dve_took, v)

            def product(u, out_job, cols_of, start, stop):
                j = job(out_job)
                for i in range(PIECES):
                    pe.wait_ge(w_lo, PIECES * u + i + 1)
                    for kk in range(2):
                        hi, lo = cols_of(i, kk)
                        k = 2 * i + kk
                        for t in range(NT):
                            o = [rows(j, t)[:, h, :] for h in range(2)]
                            for part, (lhs, ws) in enumerate(((hi, (whi, wlo)), (lo, (whi,)))):
                                for wn, w in enumerate(ws):
                                    for h in range(2):
                                        first = start and k == 0 and part == 0 and wn == 0
                                        last = stop and k == KB - 1 and part == 1
                                        ins = pe.matmul(o[h], lhs[:, t * P:(t + 1) * P], w[:, i, kk, h * HALF:(h + 1) * HALF],
                                                        start=first, stop=last)
                    ins.then_inc(w_used, 1)

            def turned(name):
                n = turn(name)

                def cols_of(i, kk):
                    if kk == 0:
                        pe.wait_ge(t_lo, 3 * n + i + 1)
                    return thi[:, n % 2, 2 * i + kk], tlo[:, n % 2, 2 * i + kk]
                return cols_of

            def add_bias(out_job, lhs):
                for t in range(NT):
                    for h in range(2):
                        pe.matmul(rows(job(out_job), t)[:, h, :], lhs(t), bias[:, h * HALF:(h + 1) * HALF], start=True, stop=False)

            def picked(name):
                return lambda t: sel[:, BIASES.index(name), :]

            def plain(name, turn_name, bias_name=None):
                open_job(name)
                if bias_name:
                    add_bias(name, picked(bias_name))
                product(unit(name), name, turned(turn_name), not bias_name, True)

            def turn_rows(name):
                open_job("T." + name)
                if name in PARTNER:
                    wait_taken(pe, PARTNER[name])
                else:
                    if name.endswith(".qi"):
                        pe.wait_ge(qi_here, 16 * (GATES[name[0]] + 1))
                    else:
                        pe.wait_ge(rows_here, BY_DVE.index(name) + 1)
                src = nat if name in ("a.h", "b.h", "m.h") else qir if name.endswith("qi") else tmp
                j = job("T." + name)
                for k in range(KB):
                    for t in range(NT):
                        o = ps[:, 4 * (j % 2) + k // 2, (k % 2) * N + t * P:(k % 2) * N + (t + 1) * P]
                        ins = pe.transpose(o, src[:, t, k * P:(k + 1) * P], ident)
                ins.then_inc(aux_done, 1)

            pe.wait_ge(cst_here, 48)
            turn_rows("a")
            pe.wait_ge(set_up, 1)
            pe.wait_ge(edge_cst_here, 48)
            wait_taken(pe, "T.a")
            j = job("counts")
            def count_tile(k, start, stop):
                for t in range(NT):
                    for h in range(2):
                        ins = pe.matmul(rows(j, t)[:, h, :], oh[:, k, t * P:(t + 1) * P], oh[:, k, N + h * HALF:N + (h + 1) * HALF],
                                        start=start, stop=stop)
                return ins

            def edge_tile(i, q, first=False, last=False):
                s, k = q // GROUP, q % GROUP
                pe.wait_ge(oh_here, i * 6 + (q + 1))
                count_tile(k, first, last).then_inc(aux_done if last else oh_used, 1)
                reached(pe, z_read, i, 6, q - 2)
                if k == 0:
                    pe.wait_ge(ea_here[s], i * 16 + 16)
                pe.matmul(ps[:, k, 0:H4], ea[0:EA + 1, s, k * P:(k + 1) * P], w1e[:], start=True, stop=True).then_inc(z_here, 1)

            for q in range(6):
                edge_tile(0, q, first=q == 0)
            with pe.Fori(1, STEPS - 1) as i:
                for q in range(6):
                    edge_tile(i, q)
            for q in range(6):
                edge_tile(STEPS - 1, q, last=q == 5)
            wait_taken(pe, "counts")
            pe.wait_ge(z_read, TILES)
            for dt in range(NT):
                for k in range(NREL):
                    for st in range(NT):
                        o = flat(job("countT"), 1536)[:, dt * D + k * N + st * P:dt * D + k * N + (st + 1) * P]
                        ins = pe.transpose(o, cT[:, st, k * N + dt * P:k * N + (dt + 1) * P], ident)
            ins.then_inc(aux_done, 1)
            pe.wait_ge(ones_set, 1)
            s = 4 * (job("countrow") % 2)
            for h in range(2):
                for t in range(NT):
                    ins = pe.matmul(ps[:, s + h, 0:HALF], onec[:], cT[:, t, h * HALF:(h + 1) * HALF], start=t == 0, stop=t == NT - 1)
            ins.then_inc(aux_done, 1)
            pe.wait_ge(q_split, 2)
            for i2 in range(2):
                name = f"qg{i2}"
                open_job(name)
                add_bias(name, picked("bg"))
                product(unit(name), name, lambda i, kk: (qhi[:, 2 * i + kk, i2 * N:(i2 + 1) * N], qlo[:, 2 * i + kk, i2 * N:(i2 + 1) * N]), False, True)

            for l, L_ in enumerate("ab"):
                if l:
                    turn_rows("b")
                for k in range(NREL):
                    plain(f"{L_}.rel{k}", L_)
                name = L_ + ".root"
                open_job(name)
                add_bias(name, picked("b1" if l == 0 else "b2"))
                product(unit(name), name, turned(L_), False, False)
                for k in range(NREL):
                    wait_taken(pe, f"{L_}.rel{k}")
                    for st in range(NT):
                        for dt in range(NT):
                            for h in range(2):
                                ins = pe.matmul(rows(job(name), dt)[:, h, :], norm[:, st, k * N + dt * P:k * N + (dt + 1) * P],
                                                xr[:, k, st, h * HALF:(h + 1) * HALF], start=False, stop=k == NREL - 1 and st == NT - 1)
                ins.then_inc(aux_done, 1)
                turn_rows(L_ + ".h")
                plain(L_ + ".hg", L_ + ".h")
                plain(L_ + ".al1", L_ + ".h", "bq")
                wait_taken(pe, L_ + ".al1")

                def add_turn(i, k, a):
                    s = k // PAIRS
                    if k % PAIRS + a == 0:
                        pe.wait_ge(stack_here[s], i * 64 + (256 * l + 64))
                    turns_done(pe, mul_done, i, l, k, a, 0)
                    for h in range(2):
                        ins = pe.matmul(slot(k, a)[:, h], pat[:, k % PAIRS, :], stack[:, s, a, h * HALF:(h + 1) * HALF], start=True, stop=True)
                    ins.then_inc(add_done[turn_of(k, a)[0]], 1)

                def sum_queries(i, k, h):
                    s, jj = k // PAIRS, k % PAIRS
                    if h == 0:
                        pe.wait_ge(sum_done[k % 2], i * 8 + (32 * l + k // 2 + 1))
                        if jj == 0:
                            reached(pe, red_took, i, 2, 8 * l + s - 1)
                    ins = pe.matmul(ps[32 * s:32 * s + 32, 6 + h, 0:HALF], red[:, jj, :], psumm[:, k % 2, h * HALF:(h + 1) * HALF],
                                    start=jj == 0, stop=jj == PAIRS - 1)
                    if h == 1:
                        ins.then_inc(sum_used[k % 2], 1)

                def gate_steps(i, last):
                    for k in range(2 * PAIRS):
                        for a in range(2):
                            if k + LAG < 2 * PAIRS:
                                add_turn(i, k + LAG, a)
                            elif not last:
                                add_turn(i + 1, k + LAG - 2 * PAIRS, a)
                            sum_queries(i, k, a)

                for k in range(LAG):
                    for a in range(2):
                        add_turn(0, k, a)
                gate_steps(0, False)
                with pe.Fori(1, B // 2 - 1) as i:
                    gate_steps(i, False)
                gate_steps(B // 2 - 1, True)
                for s in range(SLOTS):
                    pe.wait_ge(mul_done[s], 4 * (l + 1) * turn_of(s // 2, s % 2)[1])
                pe.wait_ge(red_took, 8 * (l + 1))
                turn_rows(L_ + ".qi")
                product(unit(L_ + ".al2"), L_ + ".al", turned(L_ + ".qi"), True, True)

            for n, name in enumerate(att_names):
                rels, heads = ATT[name]
                turn_rows(name)
                for k in range(rels):
                    plain(f"{name}.{k}", name)

                def row(h):
                    open_job(f"{name}.row{h}")
                    pe.wait_ge(sc_here, n + 1)
                    for k in range(rels):
                        for t in range(NT):
                            ins = pe.matmul(flat(job(f"{name}.row{h}"), D)[:, k * N + t * P:k * N + (t + 1) * P],
                                            sc[:, t, k, heads + h:heads + h + 1].to_broadcast([P, P]), ident, start=True, stop=True)
                    ins.then_inc(aux_done, 1)

                row(0)
                for h in range(heads):
                    if h + 1 < heads:
                        row(h + 1)
                    open_job(f"{name}.pt{h}")
                    pe.wait_ge(pw_here, NT * (heads_before[name] + h + 1))
                    for k in range(2 * rels):
                        for t in range(NT):
                            o = flat(job(f"{name}.pt{h}"), 2 * rels * N)[:, k * N + t * P:k * N + (t + 1) * P]
                            ins = pe.transpose(o, esc[:, t, k * P:(k + 1) * P], ident)
                    ins.then_inc(aux_done, 1)
                    open_job(f"{name}.sum{h}")
                    wait_taken(pe, f"{name}.pt{h}")
                    j = job(f"{name}.sum{h}")
                    c = D // heads
                    cuts = [(0, HALF), (HALF, HALF)] if heads == 1 else [(h * c, c)]
                    for t in range(NT):
                        for q, (a, m) in enumerate(cuts):
                            for k in range(2 * rels):
                                ins = pe.matmul(ps[:, 4 * (j % 2) + 2 * t + q, 0:m], pt[:, h % 2, k, t * P:(t + 1) * P],
                                                xr[:, k // 2, k % 2, a:a + m], start=k == 0, stop=k == 2 * rels - 1)
                    ins.then_inc(aux_done, 1)

            turn_rows("m")
            open_job("m.h")
            add_bias("m.h", lambda t: tyhot[:, t * P:(t + 1) * P])
            for t in range(NTYPE):
                def of_type(i, kk, t=t):
                    if i == 0 and kk == 0:
                        pe.wait_ge(m_here, 2 * t + 2)
                    return mhi[:, t % 2, 2 * i + kk], mlo[:, t % 2, 2 * i + kk]
                product(unit(f"ty{t}"), "m.h", of_type, False, t == NTYPE - 1)
            turn_rows("m.h")
            plain("msgA", "m.h")
            plain("msgB", "m.h", "msg_b1")
            wait_taken(pe, "msgB")
            j = job("edges")
            other = 4 * ((j + 1) % 2)

            def place(t, h):
                w = HALF + 2 * h
                return ps[:, 4 * (j % 2) + 2 * t + h, 0:w]

            def gather(i, q):
                m = q % 2
                pe.wait_ge(ohg_here, i * 6 + (q + 1))
                reached(pe, gsum_here, i, 6, q - 1)
                for t in range(NT):
                    for part in range(2):
                        for h in range(2):
                            ins = pe.matmul(ps[:, other + 2 * m + h, 0:HALF], ohg[:, q, t, :], hB[:, t, part, h * HALF:(h + 1) * HALF],
                                            start=t + part == 0, stop=t + part == 2)
                ins.then_inc(gat_done, 1)

            def scatter(i, q, first=False, last=False):
                m = q % 2
                pe.wait_ge(msg_here, i * 6 + (q + 1))
                pe.wait_ge(sew_here, i * 6 + (q + 1))
                for t in range(NT):
                    for part in range(2):
                        for h in range(2):
                            ins = pe.matmul(place(t, h), ohs[:, q, t * P:(t + 1) * P], msg[:, m, part, h * HALF:(h + 1) * HALF + 2 * h],
                                            start=first and part == 0, stop=last and part == 1)
                ins.then_inc(aux_done if last else scat_done, 1)

            def edge_loop(i, first=False, last=False):
                for q in range(2 * GROUP):
                    if q + 2 < 2 * GROUP:
                        gather(i, q + 2)
                    elif not last:
                        gather(i + 1, q + 2 - 2 * GROUP)
                    scatter(i, q, first and q == 0, last and q == 2 * GROUP - 1)

            for q in range(2):
                gather(0, q)
            edge_loop(0, first=True)
            with pe.Fori(1, STEPS - 1) as i:
                edge_loop(i)
            edge_loop(STEPS - 1, last=True)
            turn_rows("agg")
            plain("msg2", "agg")
            turn_rows("msg2")
            plain("agg1", "msg2", "agg_b1")
            turn_rows("agg1")
            plain("agg2", "agg1", "agg_b2")
            turn_rows("agg2")
            plain("out", "agg2", "out_b")


def weight_stack(v):
    wg, wq = v["L0_gnn_Wg"], v["L0_gnn_Wq"]
    out = [wg[:, D:].T] * 2
    for k in (1, 2):
        out += list(v[f"L0_gnn_W_rel{k}"]) + [v[f"L0_gnn_W_root{k}"], wg[:, :D].T, wq[:, :D].T, wq[:, D:].T]
    out += [v["L1_gnn_W1"], v["L1_gnn_W2"], *v["L2_gnn_W1"], *v["L2_gnn_W2"], *v["L3_gnn_W_type"]]
    out += [v["L3_gnn_msg_W1"][:D], v["L3_gnn_msg_W1"][D:]]
    out += [v[f"L3_gnn_{n}"] for n in ("msg_W2", "agg_W1", "agg_W2", "out_W")]
    return np.concatenate(out, axis=0)


def lay_out(v):
    a = {"x": v["x"], "node_type_6": v["node_type_6"], "weights": weight_stack(v), "consts": constants()}
    for n in ("L0_gnn_query_embs", "L3_gnn_edge_W2", "L3_gnn_edge_b2", "L3_gnn_msg_b2", "L3_gnn_ln_g", "L3_gnn_ln_b"):
        a[n] = v[n]
    a["edges"] = np.stack([v["src"], v["dst"], v["edge_type_3"]])
    a["edges_by_tile"] = a["edges"].reshape(3, TILES, P).transpose(2, 0, 1)
    a["edge_attr_T"] = v["edge_attr_32"].T
    a["edge_w1b"] = np.concatenate([v["L3_gnn_edge_W1"], v["L3_gnn_edge_b1"][None]])
    q = v["L0_gnn_query_embs"].reshape(B, HL, 2, D).transpose(3, 0, 2, 1)
    a["query_T"] = q.reshape(D, B * L)
    stack = np.zeros((P, D), np.float32)
    names = ["L0_gnn_b1", "L0_gnn_b2", "L0_gnn_bg", "L0_gnn_bq", "L3_gnn_msg_b1", "L3_gnn_agg_b1", "L3_gnn_agg_b2", "L3_gnn_out_b"]
    for half in (0, 64):
        for i, n in enumerate(names):
            stack[half + i] = v[n]
        stack[half + TYPE_ROW:half + TYPE_ROW + NTYPE] = v["L3_gnn_b_type"]
    a["biases"] = stack
    a["att_gat1"] = np.stack([v["L1_gnn_att_dst1"], v["L1_gnn_att_src1"]])
    a["att_gat2"] = np.stack([v["L1_gnn_att_dst2"], v["L1_gnn_att_src2"]])
    a["att_rgat1"] = np.concatenate([v["L2_gnn_q1"].T, v["L2_gnn_k1"].T])
    a["att_rgat2"] = np.concatenate([v["L2_gnn_q2"].T, v["L2_gnn_k2"].T])
    for n, b in (("gat1", "L1_gnn_b1"), ("gat2", "L1_gnn_b2"), ("rgat1", "L2_gnn_b1"), ("rgat2", "L2_gnn_b2")):
        a["bias_" + n] = v[b]
    return {k: np.ascontiguousarray(t) for k, t in a.items()}


def program(nc, arrays):
    d = {}
    for name, a in arrays.items():
        d[name] = nc.dram_tensor("in_" + name, a.shape, mybir.dt.from_np(a.dtype), kind="ExternalInput").ap()
    d["out"] = nc.dram_tensor("out_x", (N, D), F32, kind="ExternalOutput").ap()
    d["hg_parts"] = nc.dram_tensor("hg_parts", (2, N, D), F32).ap()
    d["qg_parts"] = nc.dram_tensor("qg_parts", (2, B * L, D), F32).ap()
    d["hA"] = nc.dram_tensor("hA_rows", (N, D), F32).ap()
    d["qi"] = nc.dram_tensor("qi_rows", (N, D), F32).ap()
    build(nc, d)


def kernel(**inputs):
    import concourse.bacc as bacc
    from concourse.bass_utils import run_bass_kernel_spmd

    v = {k: np.asarray(a) for k, a in inputs.items()}
    arrays = lay_out(v)
    nc = bacc.Bacc("TRN2", target_bir_lowering=False, num_devices=1)
    program(nc, arrays)
    got = run_bass_kernel_spmd(nc, [{"in_" + k: a for k, a in arrays.items()}], core_ids=[0])
    return got.results[0]["out_x"]
```

```python
from contextlib import ExitStack

import numpy as np
import concourse.bass as bass
from concourse import mybir

F32 = mybir.dt.float32
F32R = mybir.dt.float32r
BF16 = mybir.dt.bfloat16
I32 = mybir.dt.int32
ALU = mybir.AluOpType
ACT = mybir.ActivationFunctionType

N, D, E, EA, H4, NREL, NTYPE = 256, 768, 8448, 32, 192, 3, 6
P = 128
NT = N // P
KB = D // P
HALF = D // 2
B, L, NB = 8, 64, N // 8
PAIRS = NB // 4
HL = L // 2
PIECES = 3
TILES = E // P
GROUP = 3
STEPS = TILES // (2 * GROUP)
SLOTS = 3
LAG = 3
AHEAD = 3
HEADS1 = 4
SLOPE = 0.2
LN_EPS = 1e-5
Z_EPS = 1e-16
NO_EDGE = -1e30

UNITS = (["qg0", "qg1"]
         + [f"{l}.{w}" for l in "ab" for w in ("rel0", "rel1", "rel2", "root", "hg", "al1", "al2")]
         + ["gat1.0", "gat2.0", "rgat1.0", "rgat1.1", "rgat1.2", "rgat2.0", "rgat2.1", "rgat2.2"]
         + [f"ty{t}" for t in range(NTYPE)] + ["msgA", "msgB", "msg2", "agg1", "agg2", "out"])


def attention_jobs(name, rels, heads):
    jobs = [f"T.{name}"] + [f"{name}.{r}" for r in range(rels)] + [f"{name}.row0"]
    for h in range(heads):
        jobs += [f"{name}.row{h + 1}"] * (h + 1 < heads) + [f"{name}.pt{h}", f"{name}.sum{h}"]
    return jobs


ATT = {"gat1": (1, 1), "gat2": (1, 1), "rgat1": (NREL, HEADS1), "rgat2": (NREL, 1)}
JOBS = (["counts", "qg0", "qg1", "T.a"]
        + ["a.rel0", "countT", "countrow", "a.rel1", "a.rel2", "a.root", "T.a.h", "a.hg", "a.al1", "T.a.qi", "a.al"]
        + ["T.b", "b.rel0", "b.rel1", "b.rel2", "b.root", "T.b.h", "b.hg", "b.al1", "T.b.qi", "b.al"]
        + [j for n, (r, h) in ATT.items() for j in attention_jobs(n, r, h)]
        + ["T.m", "m.h", "T.m.h", "msgA", "msgB", "edges",
           "T.agg", "msg2", "T.msg2", "agg1", "T.agg1", "agg2", "T.agg2", "out"])


WAITS = {"T.a.qi": 24, "T.b.qi": 24, "T.b": 22, "T.gat1": 54, "T.gat2": 10, "T.rgat1": 38, "T.rgat2": 20, "T.m": 38,
         "T.agg2": 10, "gat1.row0": 18, "gat1.pt0": 15, "gat2.row0": 18, "gat2.pt0": 15, "rgat1.row0": 90,
         "rgat1.pt0": 24, "rgat2.row0": 18, "rgat2.pt0": 34}


def unit(name):
    return UNITS.index(name)


def job(name):
    return JOBS.index(name)


def ends_with(name):
    if name.endswith(".al"):
        return name + "2"
    return {"m.h": f"ty{NTYPE - 1}"}.get(name, name if name in UNITS and not name.endswith("root") else None)


def readers(name):
    if ".row" in name and name != "countrow" or ".pt" in name:
        return (True, False)
    if ".sum" in name or name in ("countrow", "msg2", "agg2", "out", "a.al", "b.al"):
        return (False, True)
    return (True, True)


def taken(name, who):
    return sum(readers(n)[who] for n in JOBS[:job(name) + 1])


BIASES = ["b1", "b2", "bg", "bq", "msg_b1", "agg_b1", "agg_b2", "out_b"]
TYPE_ROW = 32
ATTVEC = 2 * HEADS1
C_PAT, C_SEL = 0, PAIRS * P
C_ID = C_SEL + len(BIASES) * P
C_RED = C_ID + P
C_IOTA = C_RED + PAIRS * 32
C_NODE = C_IOTA + N
C_TYPE = C_NODE + NT
C_LOW = C_TYPE + 1
C_END = C_LOW + 1
CODES = NREL * N
EK = 3 * EA + 2
EW = 256


def constants():
    c = np.zeros((P, C_END), np.float32)
    p = np.arange(P)
    col = np.arange(P)
    for j in range(PAIRS):
        node = (p[:, None] < 64) & (p[:, None] % 32 == 4 * j + col[None] // 32)
        query = (p[:, None] >= 64) & (p[:, None] % 32 == col[None] % 32)
        c[:, C_PAT + j * P:C_PAT + (j + 1) * P] = node | query
        c[:, C_RED + j * 32:C_RED + (j + 1) * 32] = np.arange(32)[None] == 4 * j + p[:, None] // 32
    for i in range(len(BIASES)):
        c[:, C_SEL + i * P:C_SEL + (i + 1) * P] = (p % 64 == i)[:, None]
    c[:, C_ID:C_ID + P] = np.eye(P)
    c[:, C_IOTA:C_IOTA + N] = np.arange(N)[None]
    c[2 * EA:3 * EA, C_LOW] = c[3 * EA + 1, C_LOW] = -1
    for t in range(NT):
        c[:, C_NODE + t] = p + t * P
    c[:, C_TYPE] = p % 64 - TYPE_ROW
    return c


def code_table():
    n = np.arange(N)
    row = np.concatenate([n + 1, -(n + 1), 512 * (n + 1), n]).astype(np.float32)
    return np.broadcast_to(row, (P, CODES + N)).copy()


def build(nc, d):
    with ExitStack() as ctx:
        def sb(name, shape, dt=F32):
            return ctx.enter_context(nc.sbuf_tensor(name, shape, dt))

        def sem(name):
            return ctx.enter_context(nc.semaphore(name))

        raw = sb("raw", [P, PIECES, 2, D])
        whi = sb("whi", [P, PIECES, 2, D], F32R)
        wlo = sb("wlo", [P, PIECES, 2, D], F32R)
        thi = sb("thi", [P, 2, KB, N], F32R)
        tlo = sb("tlo", [P, 2, KB, N], F32R)
        x = sb("x", [P, NT, D])
        nat = sb("nat", [P, NT, D])
        tmp = sb("tmp", [P, NT, D])
        cnt = sb("cnt", [P, NT, NREL * N])
        sel = sb("sel", [P, len(BIASES), P], F32R)
        bias = sb("bias", [P, D], F32R)
        cst = sb("cst", [P, C_END - C_ID])
        ident = cst[:, 0:P]
        red = cst[:, C_RED - C_ID:C_IOTA - C_ID].rearrange("p (j c) -> p j c", c=32)
        iota = cst[:, C_IOTA - C_ID:C_NODE - C_ID]
        node_id = cst[:, C_NODE - C_ID:C_TYPE - C_ID]
        type_id = cst[:, C_TYPE - C_ID:C_LOW - C_ID]
        low_rows = cst[:, C_LOW - C_ID:C_END - C_ID]
        codes = sb("codes", [P, CODES + N], BF16)
        idx = sb("idx", [P, 3, TILES], I32)
        idf = sb("idf", [P, 2, TILES])
        ew = sb("ew", [P, TILES])
        st6 = sb("st6", [P, NT, 2, 6])
        mv = sb("mv", [P, NT, 2])
        rstd = sb("rstd", [P, NT, 2])
        sc = sb("sc", [P, NT, NREL, ATTVEC])
        mxs = sb("mxs", [P, 3, NT, 4])
        b2e = sb("b2e", [P, 1])
        w2e = sb("w2e", [P, H4])
        w1e = sb("w1e", [EK, EW])
        onec = sb("onec", [P, P])
        types = sb("types", [P, N], I32)
        tyhot = sb("tyhot", [P, N], F32R)
        sew = sb("sew", [P, NT])
        src_col = sb("src_col", [P, AHEAD], I32)

        R = sb("R", [P, 11528], F32R)
        G = sb("G", [P, 10752])

        def r(a, *dims):
            return cut(R, a, dims)

        def g(a, *dims):
            return cut(G, a, dims)

        def cut(t, a, dims):
            n = int(np.prod(dims))
            v = t[:, a:a + n]
            if len(dims) == 1:
                return v
            names = "abcd"[:len(dims)]
            kw = {c: dims[i] for i, c in enumerate(names) if i}
            return v.rearrange(f"p ({' '.join(names)}) -> p {' '.join(names)}", **kw)

        pat = r(0, PAIRS, P)
        qhi, qlo = r(1024, KB, B * L), r(4096, KB, B * L)
        stack = r(1024, 2, 2, D)
        ghi, glo = r(7168, NT, D), r(8704, NT, D)
        mhi, mlo = r(0, 2, KB, N), r(3072, 2, KB, N)
        hB = r(0, NT, 2, D)
        ohg = r(3072, 2 * GROUP, NT, P)
        ohs = r(4608, 2 * GROUP, N)
        ewp = r(6144, 2, TILES)
        msg = r(8448, 2, 2, D + 2)
        half_bias = r(7168, D)

        qraw = g(0, KB, B * L)
        cT = g(4608, NT, NREL * N)
        inv = g(6144, NREL * N)
        oh = G[:, 6912:8448].bitcast(BF16).rearrange("p (s c) -> p s c", s=GROUP)
        ea = g(8448, 2, GROUP * P)
        craw_codes = g(9216, CODES + N)
        eap = r(8448, 2, GROUP * P)
        w1p = r(9216, EW)
        z1 = g(3072, GROUP, H4)
        craw = g(4608, C_ID)
        braw = tmp[:, 0]
        norm = g(9216, NT, NREL * N)
        xr = g(0, NREL, NT, D)
        qrep = g(0, 2, 2, D)
        prod = g(3072, 4, 2, D)
        psumm = raw[:, 0]
        qis = raw[:, 1, 0]
        qi_in = raw.rearrange("p s k f -> p (s k) f")[:, 3:3 + NT]
        qir = g(3072, NT, D)
        vec = g(4608, ATTVEC, D)
        escs = g(4608, 2, 2, NREL * N)
        pt = g(7680, 2 * NREL, N)
        dot_prod = r(0, D)
        dot_copy = r(D, D)
        brow = g(9216, D)
        m32 = g(0, 2, D)
        ixe = G[:, 1536:1536 + 2 * GROUP * P].bitcast(I32).rearrange("p (s e) -> p s e", s=2)
        gsum = g(2304, 2, D)
        hA = g(8448, AHEAD, D)
        xin = g(4608, NT, D)
        b2row = g(6144, D)
        lng, lnb = g(6912, D), g(7680, D)

        ps = ctx.enter_context(nc.psum_tensor("ps", [P, 8, 512], F32))

        def flat(j, n):
            s = 4 * (j % 2)
            return ps[:, s:s + 4, :].rearrange("p b c -> p (b c)")[:, 0:n]

        def rows(j, t, w=HALF):
            s = 4 * (j % 2) + 2 * t
            return ps[:, s:s + 2, 0:w]

        def by_tile(ap):
            return ap.rearrange("(t p) f -> p t f", p=P)

        def two(ap):
            return ap.rearrange("p (h c) -> p h c", h=2)

        raw_here = [sem(f"raw_here{s}") for s in range(PIECES)]
        w_hi = sem("w_hi")
        w_lo = sem("w_lo")
        w_used = sem("w_used")
        aux_done = sem("aux_done")
        act_took = sem("act_took")
        dve_took = sem("dve_took")
        t_hi = sem("t_hi")
        t_lo = sem("t_lo")
        rows_here = sem("rows_here")
        act_step = sem("act_step")
        dve_step = sem("dve_step")
        x_here = sem("x_here")
        cst_here = sem("cst_here")
        raw_cst_here = sem("raw_cst_here")
        idx_here = sem("idx_here")
        edge_cst_here = sem("edge_cst_here")
        q_here = sem("q_here")
        set_up = sem("set_up")
        bias_here = sem("bias_here")
        codes_here = sem("codes_here")
        w1_split = sem("w1_split")
        ea_hi = sem("ea_hi")
        ea_split = sem("ea_split")
        ones_set = sem("ones_set")
        ea_here = [sem(f"ea_here{s}") for s in range(2)]
        oh_here = sem("oh_here")
        oh_used = sem("oh_used")
        z_here = sem("z_here")
        z_read = sem("z_read")
        q_hi = sem("q_hi")
        q_lo = sem("q_lo")
        parts_here = sem("parts_here")
        hi_stored = sem("hi_stored")
        lo_stored = sem("lo_stored")
        stack_here = [sem(f"stack_here{s}") for s in range(2)]
        qrep_here = [sem(f"qrep_here{s}") for s in range(2)]
        add_done = [sem(f"add_done{s}") for s in range(SLOTS)]
        sig_done = [sem(f"sig_done{s}") for s in range(SLOTS)]
        mul_done = [sem(f"mul_done{s}") for s in range(SLOTS)]
        sum_done = [sem(f"sum_done{s}") for s in range(2)]
        sum_used = [sem(f"sum_used{s}") for s in range(2)]
        red_took = sem("red_took")
        qi_stored = [sem(f"qi_stored{s}") for s in range(2)]
        qi_here = sem("qi_here")
        al_sum = sem("al_sum")
        al_here = sem("al_here")
        std_here = sem("std_here")
        var_here = sem("var_here")
        x_added = sem("x_added")
        vec_here = sem("vec_here")
        brow_here = sem("brow_here")
        sc_here = sem("sc_here")
        dot_here = sem("dot_here")
        dot_done = sem("dot_done")
        e_here = sem("e_here")
        max_here = sem("max_here")
        p_here = sem("p_here")
        pw_here = sem("pw_here")
        elu_in = sem("elu_in")
        elu_exp = sem("elu_exp")
        ty_here = sem("ty_here")
        m_here = sem("m_here")
        ixe_here = [sem(f"ixe_here{s}") for s in range(2)]
        hA_stored = sem("hA_stored")
        src_set = sem("src_set")
        hA_here = [sem(f"hA_here{s}") for s in range(AHEAD)]
        ew_split = sem("ew_split")
        ohg_here = sem("ohg_here")
        gat_done = sem("gat_done")
        gsum_here = sem("gsum_here")
        m32_here = sem("m32_here")
        sew_here = sem("sew_here")
        msg_here = sem("msg_here")
        scat_done = sem("scat_done")
        late_here = sem("late_here")
        out_stored = sem("out_stored")

        block = ctx.enter_context(nc.Block())

        def reached(eng, s, i, per, more):
            if not isinstance(i, int):
                eng.wait_ge(s, i * per + more)
            elif i * per + more > 0:
                eng.wait_ge(s, i * per + more)

        def aux_count(name):
            return sum(KB // 2 if n[:2] == "T." else 1 for n in JOBS[:job(name) + 1] if ends_with(n) is None)

        def ready(eng, name):
            u = ends_with(name)
            if u:
                eng.wait_ge(w_used, PIECES * (unit(u) + 1))
            else:
                eng.wait_ge(aux_done, aux_count(name))

        def wait_taken(eng, name):
            if readers(name)[0]:
                eng.wait_ge(act_took, taken(name, 0))
            if readers(name)[1]:
                eng.wait_ge(dve_took, taken(name, 1))

        TJOBS = [n for n in JOBS if n[:2] == "T."]

        def dots(name, k):
            rels, heads = ATT[name]
            all_dots = [(t, v) for v in range(2 * heads) for t in range(NT)]
            other = all_dots[1::3] if k == rels - 1 else all_dots[1::2]
            return [x for x in all_dots if x not in other], other

        def shared_dots(name, k):
            done = sum(len(dots(m, r)[1]) for m in att_names[:att_names.index(name)] for r in range(ATT[m][0]))
            return done + sum(len(dots(name, r)[1]) for r in range(k + 1))

        def wait_dots(eng, name):
            eng.wait_ge(sc_here, att_names.index(name) + 1)
            eng.wait_ge(dot_done, shared_dots(name, ATT[name][0] - 1))

        def turn(name):
            return TJOBS.index("T." + name)

        PARTNER = {"a.h": "a.root", "b.h": "b.root", "m.h": "m.h", "agg": "edges", "agg1": "agg1"}
        BY_DVE = [n[2:] for n in TJOBS if n[2:] not in PARTNER and not n.endswith("qi")]
        GATES = {"a": 0, "b": 1}
        NORMS = ["a", "gat1", "rgat1", "m", "end"]
        RELU_TURNS = {"a", "gat1", "gat2", "rgat1", "m", "agg1"}
        ADDED = {"rgat1": 1, "m": 2}
        att_names = list(ATT)
        heads_before = {n: sum(ATT[m][1] for m in att_names[:i]) for i, n in enumerate(att_names)}

        Z_BANK = 4 * ((job("counts") + 1) % 2)

        def turn_of(k, a):
            n = 2 * k + a
            return n % SLOTS, (4 * PAIRS - n % SLOTS + SLOTS - 1) // SLOTS, n // SLOTS

        def turns_done(eng, sems, i, l, k, a, more):
            s, per, n = turn_of(k, a)
            reached(eng, sems[s], i, per, 4 * per * l + n + more)

        def slot(k, a):
            s = turn_of(k, a)[0]
            return ps[:, 2 * s:2 * s + 2, 0:HALF]

        @block.sync
        def _(sp):
            def attributes(i):
                for s in range(2):
                    reached(sp, ea_split, i, 2, s - 1)
                    sp.dma_start(ea[0:EK, s, :], d["edge_attr_T"][:, bass.ds((i * 2 + s) * GROUP * P, GROUP * P)]).then_inc(ea_here[s], 16)

            def weights(a, b):
                w = d["weights"].rearrange("(u i k p) f -> (u i) p k f", i=PIECES, k=2, p=P)

                def load(u):
                    for i in range(PIECES):
                        if isinstance(u, int) and u == 0:
                            attributes(4 + i)
                        else:
                            sp.wait_ge(w_lo, u * PIECES + (i + 1 - PIECES))
                        sp.dma_start(raw[:, i], w[bass.ds(u * PIECES + i, 1)].rearrange("o p k f -> (o p) k f")
                                     if not isinstance(u, int) else w[u * PIECES + i]).then_inc(raw_here[i], 16)

                if a == 0:
                    load(0)
                    with sp.Fori(4 + PIECES, STEPS) as i:
                        attributes(i)
                    a = 1
                with sp.Fori(a, b) as u:
                    load(u)

            def gate_loads(l):
                hg, qg = d["hg_parts"], d["qg_parts"]
                q = d["L0_gnn_query_embs"].rearrange("b (l a) f -> (b l) a f", a=2)

                def load(b, s):
                    st = stack[:, s].bitcast(F32)
                    for part in range(2):
                        if isinstance(b, int):
                            v = (ghi, glo)[part][b * NB:(b + 1) * NB, 0].bitcast(F32)
                        else:
                            v = hg[part][bass.ds(b * NB, NB), :]
                        v = v.rearrange("n (a f) -> n a f", a=1)
                        sp.dma_start(st[32 * part:32 * part + 32], v.to_broadcast([NB, 2, D])).then_inc(stack_here[s], 16)
                        v = qg[part][bass.ds(b * L, L), :].rearrange("(a l) f -> l a f", a=2)
                        sp.dma_start(st[64 + 32 * part:96 + 32 * part], v).then_inc(stack_here[s], 16)
                    for k in range(4):
                        sp.dma_start(qrep[32 * k:32 * k + 32, s], q[bass.ds(b * HL, HL)]).then_inc(qrep_here[s], 16)

                ready(sp, "ab"[l] + ".root")
                sp.wait_ge(hi_stored, 16 * (2 + l))
                sp.wait_ge(lo_stored, 16 * (2 + l))
                sp.wait_ge(act_took, taken("ab"[l] + ".hg", 0))
                sp.wait_ge(parts_here, 3 + l)
                for s in range(2):
                    load(s, s)
                sp.wait_ge(hi_stored, 16 * (3 + l))
                sp.wait_ge(lo_stored, 16 * (3 + l))
                with sp.Fori(1, B // 2) as i:
                    for s in range(2):
                        turns_done(sp, add_done, i - 1, l, PAIRS * s + PAIRS - 1, 1, 1)
                        turns_done(sp, mul_done, i - 1, l, PAIRS * s + PAIRS - 1, 1, 1)
                        load(i * 2 + s, s)

            def gate_reload(l):
                for last, a, b, t in ((3, 0, P, 0), (5, 0, P // 2, 1), (6, P // 2, P // 2 + NB, 1), (7, P - NB, P, 1)):
                    for s in range(2):
                        sp.wait_ge(qi_stored[s], 16 * (4 * l + (last - s) // 2 + 1))
                    sp.dma_start(qi_in[a:b, t], d["qi"][t * P + a:t * P + b, :]).then_inc(qi_here, 16)
                ready(sp, "T." + "ab"[l] + ".qi")
                sp.wait_ge(al_here, 3 * l + 1)

            attributes(0)
            q = d["query_T"].rearrange("(k p) n -> p k n", p=P)
            for h in range(2):
                attributes(h + 1)
                sp.dma_start(qraw[:, 3 * h:3 * h + 3], q[:, 3 * h:3 * h + 3]).then_inc(q_here, 16)
            attributes(3)
            sp.dma_start(x[:], d["x"].rearrange("(t p) f -> p t f", p=P)).then_inc(x_here, 16)
            weights(0, unit("a.al2") + 1)
            gate_loads(0)
            gate_reload(0)
            weights(unit("b.rel0"), unit("b.al2") + 1)
            gate_loads(1)
            gate_reload(1)
            weights(unit("gat1.0"), len(UNITS))
            ready(sp, "out")
            for t in range(NT):
                sp.wait_ge(rows_here, NT * len(BY_DVE) + t + 1)
                sp.dma_start(d["out"][t * P:(t + 1) * P, :], x[:, t]).then_inc(out_stored, 16)
            sp.wait_ge(out_stored, 16 * NT)

        @block.gpsimd
        def _(pool):
            pool.memset(onec[:], 1.0).then_inc(ones_set, 1)
            pool.wait_ge(ones_set, 1)

            def split_attributes(i):
                for s in range(2):
                    pool.wait_ge(ea_hi, i * 2 + (s + 1))
                    low = slice(EA, 2 * EA)
                    pool.tensor_tensor(eap[low, s], ea[low, s], eap[low, s], ALU.subtract).then_inc(ea_split, 1)

            split_attributes(0)
            split_attributes(1)
            pool.wait_ge(set_up, 4)
            pool.wait_ge(ea_split, 4)
            pool.tensor_tensor(bias[64:P], braw[64:P], half_bias[64:P], ALU.subtract).then_inc(bias_here, 1)
            pool.wait_ge(bias_here, 1)
            with pool.Fori(2, STEPS - KB) as i:
                split_attributes(i)

            def split_queries(k):
                pool.wait_ge(q_hi, k + 1)
                pool.wait_ge(ea_split, 2 * k + 2 * (STEPS - KB + 1))
                block = slice(k, k + 1) if isinstance(k, int) else bass.ds(k, 1)
                pool.tensor_tensor(qlo[:, block], qraw[:, block], qhi[:, block], ALU.subtract).then_inc(q_lo, 1)
                pool.wait_ge(q_lo, k + 1)

            with pool.Fori(STEPS - KB, STEPS - 1) as i:
                split_attributes(i)
                split_queries(i - (STEPS - KB))
            split_attributes(STEPS - 1)
            split_queries(KB - 1)
            def store_low_parts(at, dram):
                pool.wait_ge(parts_here, at + 1)
                pool.dma_start(by_tile(dram), glo.bitcast(F32)).then_inc(lo_stored, 16)

            for i in range(2):
                store_low_parts(i, d["qg_parts"][1][i * N:(i + 1) * N])
            for l in range(2):
                store_low_parts(2 + l, d["hg_parts"][1])

                def gate_sums(i):
                    for k in range(2 * PAIRS):
                        s = k % 2
                        turns_done(pool, mul_done, i, l, k, 0, 1)
                        turns_done(pool, mul_done, i, l, k, 1, 1)
                        reached(pool, sum_used[s], i, 8, 32 * l + k // 2)
                        pool.tensor_tensor(psumm[:, s], prod[:, k % 4, 0], prod[:, k % 4, 1], ALU.add).then_inc(sum_done[s], 1)

                gate_sums(0)
                with pool.Fori(1, B // 2) as i:
                    gate_sums(i)
            for n, name in enumerate(att_names):
                rels, heads = ATT[name]
                pool.wait_ge(rows_here, NT * (BY_DVE.index(name) + 1))
                vectors = d["att_" + name].rearrange("(o v) f -> o v f", o=1)
                pool.dma_start(vec[:, 0:2 * heads, :], vectors.to_broadcast([P, 2 * heads, D])).then_inc(vec_here, 16)
                pool.wait_ge(vec_here, 16 * (n + 1))
                for k in range(rels):
                    wait_taken(pool, f"{name}.{k}")
                    for o, (t, v) in enumerate(dots(name, k)[1]):
                        at = shared_dots(name, k - 1) + o
                        if at >= 2:
                            pool.wait_ge(dot_done, at - 1)
                        pool.tensor_tensor(tmp[:, at % 2], xr[:, k, t], vec[:, v], ALU.mult).then_inc(dot_here, 1)
                wait_dots(pool, name)
                pool.dma_start(brow, d["bias_" + name].rearrange("(o f) -> o f", o=1).to_broadcast([P, D])).then_inc(brow_here, 16)
                if name in ("gat2", "rgat2"):
                    wait_taken(pool, f"{name}.sum0")
                    pool.tensor_tensor(x[:, 1], x[:, 1], tmp[:, 1], ALU.add).then_inc(x_added, 1)
            for row, place in (("L3_gnn_msg_b2", b2row), ("L3_gnn_ln_g", lng), ("L3_gnn_ln_b", lnb)):
                pool.dma_start(place, d[row].rearrange("(o f) -> o f", o=1).to_broadcast([P, D])).then_inc(late_here, 16)
            wait_taken(pool, "msgA")
            pool.dma_start(d["hA"].rearrange("(t p) f -> p t f", p=P), tmp[:]).then_inc(hA_stored, 16)

            def load_indices(i, s):
                reached(pool, ohg_here, i, 6, GROUP * (s - 1))
                dst = d["edges"][1:2, bass.ds((i * 2 + s) * GROUP * P, GROUP * P)]
                pool.dma_start(ixe[:, s], dst.to_broadcast([P, GROUP * P])).then_inc(ixe_here[s], 16)

            def set_sources(i, q):
                k = q % AHEAD
                reached(pool, gsum_here, i, 6, q + 1 - AHEAD)
                pool.tensor_copy(src_col[:, k:k + 1], idx[:, 0, bass.ds(i * 6 + q, 1)]).then_inc(src_set, 1)
                pool.wait_ge(src_set, i * 6 + (q + 1))

            def gather_sources(q):
                k = q % AHEAD
                pool.indirect_dma_start(hA[:, k], None, d["hA"], bass.IndirectOffsetOnAxis(ap=src_col[:, k:k + 1], axis=0)).then_inc(hA_here[k], 16)

            def pool_tiles(i, last):
                for q in range(6):
                    if q + 2 < 6:
                        set_sources(i, q + 2)
                    elif not last:
                        set_sources(i + 1, q - 4)
                    reached(pool, scat_done, i, 6, q - 1)
                    pool.tensor_copy(msg[:, q % 2, :, D:D + 1], ewp[:, :, bass.ds(i * 6 + q, 1)]).then_inc(sew_here, 1)
                    if q + 2 < 6 or not last:
                        gather_sources(q + 2)
                    if q in (1, 4) and not last:
                        load_indices(i + 1, q // GROUP)

            for s in range(2):
                load_indices(0, s)
            pool.wait_ge(hA_stored, 16)
            for q in range(2):
                set_sources(0, q)
                gather_sources(q)
            pool.wait_ge(ew_split, 1)
            pool_tiles(0, False)
            with pool.Fori(1, STEPS - 1) as i:
                pool_tiles(i, False)
            pool_tiles(STEPS - 1, True)

        @block.scalar
        def _(act):
            steps = [0]

            def step(ins):
                steps[0] += 1
                ins.then_inc(act_step, 1)
                act.wait_ge(act_step, steps[0])

            made = [0]

            def split_to(u, i):
                while made[0] <= PIECES * u + i and made[0] < PIECES * len(UNITS):
                    p = made[0]
                    act.wait_ge(raw_here[p % PIECES], 16 * (p // PIECES + 1))
                    if p >= PIECES:
                        act.wait_ge(w_used, p - PIECES + 1)
                    act.activation(whi[:, p % PIECES], raw[:, p % PIECES], ACT.Copy).then_inc(w_hi, 1)
                    made[0] += 1

            def columns(name, func=None):
                n = turn(name)
                f = ACT.Relu if name in RELU_TURNS else ACT.Copy
                j = job("T." + name)
                for i in range(3):
                    act.wait_ge(aux_done, aux_count("T." + name) - 2 + i)
                    src = ps[:, 4 * (j % 2) + i, :].rearrange("p (k n) -> p k n", k=2)
                    ins = act.activation(thi[:, n % 2, 2 * i:2 * i + 2], src, f)
                    ins.then_inc(t_hi, 1)
                act.wait_ge(t_hi, 3 * n + 3)
                act.sem_inc(act_took, 1)

            def take(name, dst, func=ACT.Copy, t=0):
                ready(act, name)
                act.activation(two(dst), rows(job(name), t), func).then_inc(act_took, 1)

            act.dma_start(idx[:], d["edges_by_tile"]).then_inc(idx_here, 16)
            act.dma_start(craw_codes, d["codes"]).then_inc(codes_here, 16)
            act.dma_start(cst[:], d["consts"][:, C_ID:C_END]).then_inc(cst_here, 16)
            act.dma_start(w1e[:], d["edge_w1b"]).then_inc(edge_cst_here, 16)
            act.dma_start(w2e[:], d["L3_gnn_edge_W2"].rearrange("f o -> o f").to_broadcast([P, H4])).then_inc(edge_cst_here, 16)
            act.dma_start(b2e[:], d["L3_gnn_edge_b2"].rearrange("(o f) -> o f", o=1).to_broadcast([P, 1])).then_inc(edge_cst_here, 16)
            act.dma_start(craw, d["consts"][:, 0:C_ID]).then_inc(raw_cst_here, 16)
            act.dma_start(braw, d["biases"]).then_inc(raw_cst_here, 16)
            act.dma_start(types[:], d["node_type_6"].rearrange("(o n) -> o n", o=1).to_broadcast([P, N])).then_inc(ty_here, 16)

            def norm_std(n):
                for t in range(NT):
                    act.wait_ge(var_here, NT * n + t + 1)
                    act.activation(rstd[:, t, 0:1], mv[:, t, 1:2], ACT.Sqrt).then_inc(std_here, 1)

            def attributes(i):
                for s in range(2):
                    act.wait_ge(ea_here[s], i * 16 + 16)
                    reached(act, z_here, i, 2 * GROUP, GROUP * (s - 1))
                    act.activation(eap[0:EK, s], ea[0:EK, s], ACT.Copy).then_inc(ea_hi, 1)

            attributes(0)
            act.wait_ge(raw_cst_here, 32)
            act.activation(sel[:].rearrange("p a b -> p (a b)"), craw[:, C_SEL:C_ID], ACT.Copy).then_inc(set_up, 1)
            act.activation(bias[0:64], braw[0:64], ACT.Copy).then_inc(set_up, 1)
            act.activation(half_bias, braw, ACT.Copy).then_inc(set_up, 1)
            act.activation(pat.rearrange("p a b -> p (a b)"), craw[:, 0:C_SEL], ACT.Copy).then_inc(set_up, 1)
            with act.Fori(1, STEPS - KB - 1) as i:
                attributes(i)
            act.wait_ge(q_here, 32)
            with act.Fori(STEPS - KB - 1, STEPS - 1) as i:
                attributes(i)
                k = bass.ds(i - (STEPS - KB - 1), 1)
                act.activation(qhi[:, k], qraw[:, k], ACT.Copy).then_inc(q_hi, 1)
            attributes(STEPS - 1)
            split_to(unit("qg0"), 2)
            take("counts", cT[:, 0])
            split_to(unit("qg1"), 0)
            norm_std(0)
            act.wait_ge(z_read, TILES)
            act.wait_ge(edge_cst_here, 48)
            act.activation(ew[:], ew[:], ACT.Sigmoid, bias=b2e[:, 0:1]).then_inc(act_step, 1)
            steps[0] += 1
            def split_parts(name, dram, at):
                ready(act, name)
                if at > 0:
                    act.wait_ge(hi_stored, 16 * at)
                for t in range(NT):
                    ins = act.activation(two(ghi[:, t]), rows(job(name), t), ACT.Copy)
                ins.then_inc(act_took, 1)
                act.wait_ge(act_took, taken(name, 0))
                act.dma_start(dram, ghi.bitcast(F32)).then_inc(hi_stored, 16)

            for i in range(2):
                split_to(unit(f"qg{i}") + 1, 1)
                split_parts(f"qg{i}", by_tile(d["qg_parts"][0][i * N:(i + 1) * N]), i)
            columns("a")

            for l, L_ in enumerate("ab"):
                if l:
                    columns("b")
                for k in range(NREL):
                    split_to(unit(f"{L_}.rel{k}") + 1, 1)
                    take(f"{L_}.rel{k}", xr[:, k, 0])
                    if (L_, k) == ("a", 0):
                        split_to(unit("a.rel1"), 2)
                        ready(act, "countT")
                        act.activation(cnt[:].rearrange("p t c -> p (t c)")[:, 0:1024], flat(job("countT"), 1024), ACT.Copy).then_inc(act_took, 1)
                split_to(unit(L_ + ".hg"), 1)
                take(L_ + ".root", nat[:, 0], ACT.Relu)
                columns(L_ + ".h")
                split_to(unit(L_ + ".al1"), 1)
                split_parts(L_ + ".hg", by_tile(d["hg_parts"][0]), 2 + l)
                split_to(unit(L_ + ".al2"), 1)
                take(L_ + ".al1", tmp[:, 0])
                split_to(unit(L_ + ".al2"), 2)

                def store_qi(b, s):
                    act.wait_ge(sum_used[(PAIRS - 1) % 2], b * (PAIRS // 2) + (32 * l + PAIRS // 2))
                    if not isinstance(b, int) or b >= 2:
                        act.wait_ge(qi_stored[s], (b - s) * 8 + 64 * l)
                    elif l:
                        act.wait_ge(qi_stored[s], 64)
                    act.activation(two(qis[32 * s:32 * s + 32]), ps[32 * s:32 * s + 32, 6:8, 0:HALF], ACT.Copy).then_inc(red_took, 1)
                    act.wait_ge(red_took, b + (8 * l + 1))
                    act.dma_start(d["qi"][bass.ds(b * NB, NB), :], qis[32 * s:32 * s + 32]).then_inc(qi_stored[s], 16)

                def gate_steps(i):
                    for k in range(2 * PAIRS):
                        for a in range(2):
                            turns_done(act, add_done, i, l, k, a, 1)
                            act.activation(slot(k, a), slot(k, a), ACT.Sigmoid).then_inc(sig_done[turn_of(k, a)[0]], 1)
                        if k == 4 and not isinstance(i, int):
                            store_qi(i * 2 - 1, 1)
                        if k == 12:
                            store_qi(i * 2, 0)

                gate_steps(0)
                with act.Fori(1, B // 2) as i:
                    gate_steps(i)
                store_qi(B - 1, 1)

                columns(L_ + ".qi")
                act.activation(qir, qi_in, ACT.Tanh).then_inc(al_here, 1)
                split_to(unit(L_ + ".al2") + 1, 1)
                for t in range(NT):
                    act.wait_ge(al_sum, NT * l + t + 1)
                    act.activation(tmp[:, t], tmp[:, t], ACT.Sigmoid).then_inc(al_here, 1)

            for n, name in enumerate(att_names):
                rels, heads = ATT[name]
                w = rels * N
                if name in NORMS:
                    norm_std(NORMS.index(name))
                columns(name)
                for k in range(rels):
                    u = unit(f"{name}.{k}")
                    split_to(u + 1, 1)
                    take(f"{name}.{k}", xr[:, k, 0])
                    for o, (t, v) in enumerate(dots(name, k)[1]):
                        at = shared_dots(name, k - 1) + o
                        if o in (0, 2, 5) and k < rels - 1:
                            split_to(*divmod(min(made[0], PIECES * (u + 2) + 1), PIECES))
                        act.wait_ge(dot_here, at + 1)
                        if at:
                            act.wait_ge(dot_done, at)
                        act.activation(dot_copy, tmp[:, at % 2], ACT.Copy, accum_out=sc[:, t, k, v:v + 1]).then_inc(dot_done, 1)
                base = heads_before[name]

                def scores(h):
                    hh = base + h
                    esc = escs[:, h % 2]
                    ready(act, f"{name}.row{h}")
                    if h == 0:
                        wait_dots(act, name)
                    if h >= 2:
                        ready(act, f"{name}.pt{h - 2}")
                    for t in range(NT):
                        for k in range(rels):
                            ins = act.activation(esc[:, t, k * N:(k + 1) * N], flat(job(f"{name}.row{h}"), w)[:, k * N:(k + 1) * N],
                                                 ACT.Identity, bias=sc[:, t, k, h:h + 1])
                        ins.then_inc(e_here, 1)
                    act.wait_ge(e_here, NT * (hh + 1))
                    act.sem_inc(act_took, 1)

                def exps(h):
                    hh = base + h
                    for t in range(NT):
                        e = escs[:, h % 2, t, 0:w]
                        act.wait_ge(max_here, NT * hh + t + 1)
                        act.activation(e, e, ACT.Exp, bias=mxs[:, hh % 3, t, 0:1]).then_inc(p_here, 1)

                scores(0)
                exps(0)
                if heads > 1:
                    scores(1)
                for h in range(heads):
                    ready(act, f"{name}.pt{h}")
                    if h:
                        ready(act, f"{name}.sum{h - 1}")
                    act.activation(pt[:, 0:2 * rels].rearrange("p a b -> p (a b)"),
                                   flat(job(f"{name}.pt{h}"), 2 * rels * N), ACT.Copy).then_inc(act_took, 1)
                    if h + 1 < heads:
                        exps(h + 1)
                    if h + 2 < heads:
                        scores(h + 2)
                if name == "rgat1":
                    for t in range(NT):
                        act.wait_ge(elu_in, t + 1)
                        act.activation(escs[:, 0, t], escs[:, 0, t], ACT.Exp).then_inc(elu_exp, 1)

            norm_std(NORMS.index("m"))
            columns("m")
            for t in range(NTYPE):
                split_to(unit(f"ty{t}") + 1, 1)
            take("m.h", nat[:, 0])
            columns("m.h")
            split_to(unit("msgB"), 1)
            take("msgA", tmp[:, 0])
            split_to(unit("msg2"), 1)
            ready(act, "msgB")
            for t in range(NT):
                ins = act.activation(two(hB[:, t, 0]), rows(job("msgB"), t), ACT.Copy)
                if t == 0:
                    step(ins)
            ins.then_inc(act_took, 1)
            split_to(unit("msg2"), 2)

            def messages(i):
                for q in range(2 * GROUP):
                    m = q % 2
                    act.wait_ge(gsum_here, i * 6 + (q + 1))
                    reached(act, msg_here, i, 6, q - 1)
                    reached(act, scat_done, i, 6, q - 1)
                    w = ew[:, bass.ds(i * 6 + q, 1)]
                    act.activation(msg[:, m, 0, 0:D], gsum[:, m], ACT.Relu, scale=w).then_inc(m32_here, 1)
                    act.activation(m32[:, m], gsum[:, m], ACT.Relu, scale=w).then_inc(m32_here, 1)

            messages(0)
            with act.Fori(1, STEPS) as i:
                messages(i)
            ready(act, "edges")
            step(act.activation(sew[:, 0:1], rows(job("edges"), 0, HALF + 1)[:, 1, HALF:HALF + 1], ACT.Copy))
            act.activation(two(tmp[:, 0]), rows(job("edges"), 0), ACT.Copy).then_inc(act_took, 1)
            columns("agg")
            split_to(unit("agg1"), 1)
            columns("msg2")
            split_to(unit("agg2"), 1)
            take("agg1", tmp[:, 0])
            columns("agg1")
            split_to(unit("out"), 1)
            columns("agg2")
            split_to(unit("out"), 2)
            norm_std(NORMS.index("end"))

        @block.vector
        def _(dve):
            steps = [0]

            def step(ins):
                steps[0] += 1
                ins.then_inc(dve_step, 1)
                dve.wait_ge(dve_step, steps[0])

            made = [0]

            def split_to(u, i):
                while made[0] <= PIECES * u + i and made[0] < PIECES * len(UNITS):
                    p = made[0]
                    dve.wait_ge(w_hi, p + 1)
                    dve.tensor_tensor(wlo[:, p % PIECES], raw[:, p % PIECES], whi[:, p % PIECES], ALU.subtract).then_inc(w_lo, 1)
                    made[0] += 1

            def columns(name):
                n = turn(name)
                j = job("T." + name)
                for i in range(3):
                    dve.wait_ge(t_hi, 3 * n + i + 1)
                    src = ps[:, 4 * (j % 2) + i, :].rearrange("p (k n) -> p k n", k=2)
                    hi, lo = thi[:, n % 2, 2 * i:2 * i + 2], tlo[:, n % 2, 2 * i:2 * i + 2]
                    if name in RELU_TURNS:
                        ins = dve.scalar_tensor_tensor(lo, src, 0.0, hi, ALU.max, ALU.subtract)
                    else:
                        ins = dve.tensor_tensor(lo, src, hi, ALU.subtract)
                    ins.then_inc(t_lo, 1)
                dve.wait_ge(t_lo, 3 * n + 3)
                dve.sem_inc(dve_took, 1)

            def take(name, dst, relu=False, t=1):
                ready(dve, name)
                if relu:
                    ins = dve.tensor_scalar(two(dst), rows(job(name), t), 0.0, None, ALU.max)
                else:
                    ins = dve.tensor_copy(two(dst), rows(job(name), t))
                ins.then_inc(dve_took, 1)

            def moments(src, added=None):
                for t in range(NT):
                    if t and added:
                        dve.wait_ge(x_added, added)
                    dve.bn_stats(st6[:, t, 0, :], src[:, t, 0:HALF])
                    step(dve.bn_stats(st6[:, t, 1, :], src[:, t, HALF:D]))
                    step(dve.bn_aggr(mv[:, t, :], st6[:, t].rearrange("p a b -> p (a b)")))
                    dve.tensor_scalar(mv[:, t, 1:2], mv[:, t, 1:2], LN_EPS, None, ALU.add).then_inc(var_here, 1)

            def inverse_std(n, t):
                dve.wait_ge(std_here, NT * n + t + 1)
                step(dve.reciprocal(rstd[:, t, 1:2], rstd[:, t, 0:1]))

            def normalise(name, added=None):
                moments(x, added)
                for t in range(NT):
                    inverse_std(NORMS.index(name), t)
                    dve.tensor_scalar(tmp[:, t], x[:, t], mv[:, t, 0:1], rstd[:, t, 1:2], ALU.subtract, ALU.mult).then_inc(rows_here, 1)

            dve.wait_ge(idx_here, 16)
            step(dve.tensor_copy(idf[:, 0], idx[:, 0]))
            step(dve.tensor_scalar(idf[:, 1], idx[:, 2], 257.5, -259.5, ALU.mult, ALU.add))
            step(dve.tensor_tensor(idf[:, 1], idf[:, 1], idx[:, 2], ALU.mult))
            step(dve.tensor_scalar(idf[:, 1], idf[:, 1], 1.0, None, ALU.add))
            step(dve.scalar_tensor_tensor(idf[:, 1], idx[:, 1], 1.0, idf[:, 1], ALU.add, ALU.mult))
            dve.wait_ge(codes_here, 16)
            step(dve.tensor_copy(codes[:], craw_codes))
            def count_hot(i, q):
                e, k = bass.ds(i * 6 + q, 1), q % GROUP
                reached(dve, oh_used, i, 6, q - 2)
                dve.tensor_scalar(oh[:, k, 0:N], codes[:, CODES:], idf[:, 0, e], None, ALU.is_equal)
                dve.tensor_scalar(oh[:, k, N:], codes[:, 0:CODES], idf[:, 1, e], None, ALU.is_equal).then_inc(oh_here, 1)

            def edge_logit(i, q):
                e, k = bass.ds(i * 6 + q, 1), q % GROUP
                dve.wait_ge(z_here, i * 6 + (q + 1))
                reached(dve, z_read, i, 6, q - 2)
                dve.scalar_tensor_tensor(z1[:, k], ps[:, Z_BANK + k, 0:H4], 0.0, w2e[:], ALU.max, ALU.mult,
                                         accum_out=ew[:, e]).then_inc(z_read, 1)

            for q in range(6):
                count_hot(0, q)
                if q == 0:
                    dve.wait_ge(edge_cst_here, 48)
                    dve.wait_ge(cst_here, 16)
                    step(dve.tensor_copy(w1p[0:EK], w1e[:]))
                    dve.scalar_tensor_tensor(w1p[0:EK], w1p[0:EK], low_rows[0:EK], w1e[:], ALU.mult, ALU.add).then_inc(w1_split, 1)
                if q >= 2:
                    edge_logit(0, q - 2)
            with dve.Fori(1, STEPS) as i:
                for q in range(6):
                    count_hot(i, q)
                    edge_logit(i, q - 2)
            for q in (4, 5):
                edge_logit(STEPS - 1, q)
            split_to(unit("qg0"), 2)
            take("counts", cT[:, 1])
            dve.wait_ge(ty_here, 16)
            step(dve.tensor_scalar(tyhot[:], types[:], type_id, None, ALU.is_equal))
            dve.wait_ge(x_here, 16)
            dve.wait_ge(bias_here, 1)
            normalise("a")

            def split_parts(name, at):
                ready(dve, name)
                dve.wait_ge(act_took, taken(name, 0))
                if at > 0:
                    dve.wait_ge(lo_stored, 16 * at)
                for t in range(NT):
                    ins = dve.tensor_tensor(two(glo[:, t]), rows(job(name), t), two(ghi[:, t]), ALU.subtract)
                    if t == 0:
                        step(ins)
                ins.then_inc(parts_here, 1)
                dve.wait_ge(parts_here, at + 1)
                dve.sem_inc(dve_took, 1)

            for i in range(2):
                split_to(unit(f"qg{i}") + 1, 1)
                split_parts(f"qg{i}", i)
            columns("a")
            for l, L_ in enumerate("ab"):
                if l:
                    columns("b")
                for k in range(NREL):
                    split_to(unit(f"{L_}.rel{k}") + 1, 1)
                    take(f"{L_}.rel{k}", xr[:, k, 1])
                    if (L_, k) == ("a", 0):
                        split_to(unit("a.rel1"), 2)
                        ready(dve, "countT")
                        dve.tensor_copy(cnt[:].rearrange("p t c -> p (t c)")[:, 1024:1536],
                                        flat(job("countT"), 1536)[:, 1024:1536]).then_inc(dve_took, 1)
                        ready(dve, "countrow")
                        dve.tensor_scalar(two(inv), rows(job("countrow"), 0), 1.0, None, ALU.max).then_inc(dve_took, 1)
                        dve.wait_ge(dve_took, taken("countrow", 1))
                        step(dve.reciprocal(inv, inv))
                        step(dve.tensor_tensor(norm[:, 0], cT[:, 0], inv, ALU.mult))
                        step(dve.tensor_tensor(norm[:, 1], cT[:, 1], inv, ALU.mult))
                split_to(unit(L_ + ".hg"), 1)
                take(L_ + ".root", nat[:, 1], relu=True)
                columns(L_ + ".h")
                split_to(unit(L_ + ".al1"), 1)
                split_parts(L_ + ".hg", 2 + l)
                split_to(unit(L_ + ".al2"), 1)
                take(L_ + ".al1", tmp[:, 1])
                split_to(unit(L_ + ".al2"), 2)

                def gate_products(i):
                    for k in range(2 * PAIRS):
                        s = k // PAIRS
                        if k % PAIRS == 0:
                            dve.wait_ge(qrep_here[s], i * 64 + (256 * l + 64))
                        for a in range(2):
                            turns_done(dve, sig_done, i, l, k, a, 1)
                            reached(dve, sum_done[k % 2], i, 8, 32 * l + k // 2 - 1)
                            dve.tensor_tensor(two(prod[:, k % 4, a]), slot(k, a), two(qrep[:, s, a]),
                                              ALU.mult).then_inc(mul_done[turn_of(k, a)[0]], 1)

                gate_products(0)
                with dve.Fori(1, B // 2) as i:
                    gate_products(i)
                columns(L_ + ".qi")
                dve.wait_ge(al_here, 3 * l + 1)
                step(dve.tensor_tensor(qir, qir, nat[:], ALU.subtract))
                if l:
                    step(dve.tensor_tensor(x[:], x[:], nat[:], ALU.add))
                split_to(unit(L_ + ".al2") + 1, 1)
                ready(dve, L_ + ".al")
                wait_taken(dve, L_ + ".al1")
                for t in range(NT):
                    ins = dve.tensor_tensor(two(tmp[:, t]), rows(job(L_ + ".al"), t), two(tmp[:, t]), ALU.add)
                    ins.then_inc(al_sum, 1)
                for t in range(NT):
                    dve.wait_ge(al_here, 3 * l + 2 + t)
                    step(dve.tensor_tensor(qir[:, t], qir[:, t], tmp[:, t], ALU.mult))
                    if l == 0:
                        ins = dve.tensor_tensor(tmp[:, t], qir[:, t], nat[:, t], ALU.add)
                    else:
                        ins = dve.tensor_tensor(x[:, t], qir[:, t], x[:, t], ALU.add)
                    if l == 0:
                        ins.then_inc(rows_here, 1)
                    else:
                        step(ins)
                dve.sem_inc(dve_took, 1)

            for n, name in enumerate(att_names):
                rels, heads = ATT[name]
                w = rels * N
                gat = rels == 1
                if name in NORMS:
                    normalise(name, ADDED.get(name))
                columns(name)
                split_to(unit(f"{name}.0"), 2)
                if name == "gat1":
                    c1, m1 = nat[:, :, N:2 * N], nat[:, :, 0:N]
                    step(dve.tensor_tensor(c1, cnt[:, :, 0:N], cnt[:, :, N:2 * N], ALU.add))
                    step(dve.tensor_tensor(c1, c1, cnt[:, :, 2 * N:3 * N], ALU.add))
                    for t in range(NT):
                        step(dve.tensor_tensor(c1[:, t, t * P:(t + 1) * P], c1[:, t, t * P:(t + 1) * P], ident, ALU.add))
                    step(dve.tensor_scalar(m1, c1, 0.0, NO_EDGE, ALU.is_equal, ALU.mult))
                    counts, mask = c1, m1
                if name == "rgat1":
                    step(dve.tensor_scalar(nat[:], cnt[:], 0.0, NO_EDGE, ALU.is_equal, ALU.mult))
                    counts, mask = cnt, nat
                for k in range(rels):
                    u = unit(f"{name}.{k}")
                    split_to(u + 1, 1)
                    take(f"{name}.{k}", xr[:, k, 1])
                    dve.wait_ge(vec_here, 16 * (n + 1))
                    wait_taken(dve, f"{name}.{k}")
                    own = dots(name, k)[0]
                    for o, (t, v) in enumerate(own):
                        if o in (2, 5, 8) and k < rels - 1:
                            split_to(*divmod(min(made[0], PIECES * (u + 2) + 1), PIECES))
                        ins = dve.tensor_tensor_reduce(dot_prod, xr[:, k, t], vec[:, v], 1.0, 0.0,
                                                       ALU.mult, ALU.add, sc[:, t, k, v:v + 1])
                        if k < rels - 1 or o < len(own) - 1:
                            step(ins)
                ins.then_inc(sc_here, 1)
                base = heads_before[name]

                def maxima(h):
                    hh = base + h
                    mx = mxs[:, hh % 3]
                    for t in range(NT):
                        e = escs[:, h % 2, t, 0:w]
                        dve.wait_ge(e_here, NT * hh + t + 1)
                        step(dve.scalar_tensor_tensor(e, e, SLOPE, e, ALU.mult, ALU.max))
                        step(dve.tensor_tensor_reduce(e, e, mask[:, t, 0:w], 1.0, NO_EDGE, ALU.add, ALU.max, mx[:, t, 1:2]))
                        dve.tensor_scalar(mx[:, t, 0:1], mx[:, t, 1:2], -1.0, None, ALU.mult).then_inc(max_here, 1)

                def weigh(h):
                    hh = base + h
                    mx = mxs[:, hh % 3]
                    for t in range(NT):
                        e = escs[:, h % 2, t, 0:w]
                        dve.wait_ge(p_here, NT * hh + t + 1)
                        dve.tensor_tensor_reduce(e, e, counts[:, t, 0:w], 1.0, 0.0, ALU.mult, ALU.add, mx[:, t, 2:3]).then_inc(pw_here, 1)
                    dve.wait_ge(pw_here, NT * (hh + 1))
                    if not gat:
                        step(dve.tensor_scalar(mx[:, :, 2], mx[:, :, 2], Z_EPS, None, ALU.add))
                    step(dve.reciprocal(mx[:, :, 3], mx[:, :, 2]))

                def sums(h):
                    mx = mxs[:, (base + h) % 3]
                    j = job(f"{name}.sum{h}")
                    c = D // heads
                    dve.wait_ge(brow_here, 16 * (n + 1))
                    ready(dve, f"{name}.sum{h}")
                    for t in range(NT):
                        if heads == 1:
                            o, i, b = two(tmp[:, t]), rows(j, t), two(brow)
                        else:
                            o, i, b = tmp[:, t, h * c:(h + 1) * c], ps[:, 4 * (j % 2) + 2 * t, 0:c], brow[:, h * c:(h + 1) * c]
                        ins = dve.scalar_tensor_tensor(o, i, mx[:, t, 3:4], b, ALU.mult, ALU.add)
                        if t == 0:
                            step(ins)
                    ins.then_inc(dve_took, 1)
                    dve.wait_ge(dve_took, taken(f"{name}.sum{h}", 1))

                maxima(0)
                weigh(0)
                if heads > 1:
                    maxima(1)
                for h in range(heads):
                    if h + 1 < heads:
                        weigh(h + 1)
                    sums(h)
                    if h + 2 < heads:
                        maxima(h + 2)
                if name == "gat1":
                    dve.sem_inc(rows_here, NT)
                elif name == "rgat1":
                    for t in range(NT):
                        dve.tensor_scalar(escs[:, 0, t], tmp[:, t], 0.0, None, ALU.min).then_inc(elu_in, 1)
                    for t in range(NT):
                        dve.wait_ge(elu_exp, t + 1)
                        step(dve.scalar_tensor_tensor(tmp[:, t], tmp[:, t], 0.0, escs[:, 0, t], ALU.max, ALU.add))
                        dve.tensor_scalar(tmp[:, t], tmp[:, t], -1.0, None, ALU.add).then_inc(rows_here, 1)
                else:
                    step(dve.tensor_tensor(x[:, 0], x[:, 0], tmp[:, 0], ALU.add))

            normalise("m", ADDED["m"])
            columns("m")
            n = turn("m") % 2
            ty = types[:].rearrange("p (a n) -> p a n", a=1).to_broadcast([P, 2, N])
            for t in range(NTYPE):
                if t >= 2:
                    dve.wait_ge(w_used, PIECES * (unit(f"ty{t - 2}") + 1))
                for i in range(PIECES):
                    for part, of in ((mhi, thi), (mlo, tlo)):
                        dve.scalar_tensor_tensor(part[:, t % 2, 2 * i:2 * i + 2], ty, float(t), of[:, n, 2 * i:2 * i + 2],
                                                 ALU.is_equal, ALU.mult).then_inc(m_here, 1)
                split_to(unit(f"ty{t}") + 1, 0)
                if t == 1:
                    dve.wait_ge(rows_here, NT * (BY_DVE.index("m") + 1))
                    step(dve.tensor_scalar(xin, tmp[:], 0.0, None, ALU.max))
            take("m.h", nat[:, 1])
            columns("m.h")
            split_to(unit("msgB"), 1)
            take("msgA", tmp[:, 1])
            split_to(unit("msgB"), 2)
            step(dve.tensor_copy(ewp[:, 0], ew[:]))
            step(dve.tensor_tensor(ewp[:, 1], ew[:], ewp[:, 0], ALU.subtract))
            step(dve.memset(m32[:, 0, 0:4], 0.0))
            dve.tensor_copy(msg[:, :, :, D + 1:D + 2], m32[:, 0, 0:4].rearrange("p (a b c) -> p a b c", a=2, b=2)).then_inc(ew_split, 1)
            step(dve.tensor_copy(idf[:, 1], idx[:, 1]))

            def onehots(i, q):
                s = q // GROUP
                dve.wait_ge(ixe_here[s], i * 16 + 16)
                reached(dve, scat_done, i, 6, q - 5)
                for t in range(NT):
                    dve.tensor_scalar(ohg[:, q, t], ixe[:, s, (q % GROUP) * P:(q % GROUP + 1) * P], node_id[:, t:t + 1], None, ALU.is_equal)
                dve.tensor_scalar(ohs[:, q], iota[:, 0:N], idf[:, 1, bass.ds(i * 6 + q, 1)], None, ALU.is_equal).then_inc(ohg_here, 1)

            def add_sources(i, q):
                m = q % 2
                dve.wait_ge(gat_done, i * 6 + (q + 1))
                dve.wait_ge(hA_here[q % AHEAD], i * 32 + 16 * (q // AHEAD + 1))
                reached(dve, m32_here, i, 12, 2 * (q - 1))
                dve.tensor_tensor(two(gsum[:, m]), ps[:, other + 2 * m:other + 2 * m + 2, 0:HALF], two(hA[:, q % AHEAD]),
                                  ALU.add).then_inc(gsum_here, 1)

            def split_message(i, q):
                m = q % 2
                dve.wait_ge(m32_here, i * 12 + 2 * (q + 1))
                dve.tensor_tensor(msg[:, m, 1, 0:D], m32[:, m], msg[:, m, 0, 0:D], ALU.subtract).then_inc(msg_here, 1)

            other = 4 * ((job("edges") + 1) % 2)
            for q in range(3):
                onehots(0, q)
            split_to(unit("msg2"), 1)
            ready(dve, "msgB")
            dve.wait_ge(act_took, taken("msgB", 0))
            for t in range(NT):
                ins = dve.tensor_tensor(two(hB[:, t, 1]), rows(job("msgB"), t), two(hB[:, t, 0]), ALU.subtract)
                if t == 0:
                    step(ins)
            ins.then_inc(dve_took, 1)
            split_to(unit("msg2"), 2)

            def edge_tiles(i, last):
                for q in range(6):
                    if q < 5:
                        add_sources(i, q + 1)
                    elif not last:
                        add_sources(i + 1, 0)
                    split_message(i, q)
                    if q < 3:
                        onehots(i, q + 3)
                    elif not last:
                        onehots(i + 1, q - 3)

            add_sources(0, 0)
            edge_tiles(0, False)
            with dve.Fori(1, STEPS - 1) as i:
                edge_tiles(i, False)
            edge_tiles(STEPS - 1, True)
            j = job("edges")
            ready(dve, "edges")
            step(dve.tensor_copy(sew[:, 1:2], rows(j, 1, HALF + 1)[:, 1, HALF:HALF + 1]))
            dve.tensor_copy(two(tmp[:, 1]), rows(j, 1)).then_inc(dve_took, 1)
            columns("agg")
            split_to(unit("agg1"), 1)
            dve.wait_ge(late_here, 48)
            ready(dve, "msg2")
            for t in range(NT):
                dve.scalar_tensor_tensor(two(tmp[:, t]), two(b2row), sew[:, t:t + 1], rows(job("msg2"), t), ALU.mult, ALU.add).then_inc(rows_here, 1)
            dve.wait_ge(rows_here, NT * (BY_DVE.index("msg2") + 1))
            dve.sem_inc(dve_took, 1)
            columns("msg2")
            split_to(unit("agg2"), 1)
            take("agg1", tmp[:, 1])
            columns("agg1")
            split_to(unit("out"), 1)
            step(dve.tensor_tensor(x[:], x[:], lnb.rearrange("p (o f) -> p o f", o=1).to_broadcast([P, NT, D]), ALU.add))
            ready(dve, "agg2")
            for t in range(NT):
                dve.tensor_tensor(two(tmp[:, t]), rows(job("agg2"), t), two(nat[:, t]), ALU.add).then_inc(rows_here, 1)
            dve.wait_ge(rows_here, NT * (BY_DVE.index("agg2") + 1))
            dve.sem_inc(dve_took, 1)
            columns("agg2")
            split_to(unit("out"), 2)
            ready(dve, "out")
            for t in range(NT):
                ins = dve.tensor_tensor(two(tmp[:, t]), rows(job("out"), t), two(xin[:, t]), ALU.add)
                step(ins)
            dve.sem_inc(dve_took, 1)
            moments(tmp)
            for t in range(NT):
                inverse_std(NORMS.index("end"), t)
                step(dve.scalar_tensor_tensor(nat[:, t], tmp[:, t], mv[:, t, 0:1], lng, ALU.subtract, ALU.mult))
                dve.scalar_tensor_tensor(x[:, t], nat[:, t], rstd[:, t, 1:2], x[:, t], ALU.mult, ALU.add).then_inc(rows_here, 1)

        @block.tensor
        def _(pe):
            def open_job(name):
                j = job(name)
                if j >= 2:
                    wait_upto(j - 2)

            def wait_upto(j):
                a, v = sum(readers(n)[0] for n in JOBS[:j + 1]), sum(readers(n)[1] for n in JOBS[:j + 1])
                if a:
                    pe.wait_ge(act_took, a)
                if v:
                    pe.wait_ge(dve_took, v)

            def product(u, out_job, cols_of, start, stop):
                j = job(out_job)
                for i in range(PIECES):
                    pe.wait_ge(w_lo, PIECES * u + i + 1)
                    for kk in range(2):
                        hi, lo = cols_of(i, kk)
                        k = 2 * i + kk
                        for t in range(NT):
                            o = [rows(j, t)[:, h, :] for h in range(2)]
                            for part, (lhs, ws) in enumerate(((hi, (whi, wlo)), (lo, (whi,)))):
                                for wn, w in enumerate(ws):
                                    for h in range(2):
                                        first = start and k == 0 and part == 0 and wn == 0
                                        last = stop and k == KB - 1 and part == 1
                                        ins = pe.matmul(o[h], lhs[:, t * P:(t + 1) * P], w[:, i, kk, h * HALF:(h + 1) * HALF],
                                                        start=first, stop=last)
                    ins.then_inc(w_used, 1)

            def turned(name):
                n = turn(name)

                def cols_of(i, kk):
                    if kk == 0:
                        pe.wait_ge(t_lo, 3 * n + i + 1)
                    return thi[:, n % 2, 2 * i + kk], tlo[:, n % 2, 2 * i + kk]
                return cols_of

            def add_bias(out_job, lhs):
                for t in range(NT):
                    for h in range(2):
                        pe.matmul(rows(job(out_job), t)[:, h, :], lhs(t), bias[:, h * HALF:(h + 1) * HALF], start=True, stop=False)

            def picked(name):
                return lambda t: sel[:, BIASES.index(name), :]

            def plain(name, turn_name, bias_name=None):
                open_job(name)
                if bias_name:
                    add_bias(name, picked(bias_name))
                product(unit(name), name, turned(turn_name), not bias_name, True)

            def keep_clock(name):
                for _ in range(WAITS.get(name, 0)):
                    pe.matmul(flat(job(name), HALF), sel[:, 0, :], bias[:, 0:HALF], start=True, stop=True)

            def turn_rows(name):
                open_job("T." + name)
                keep_clock("T." + name)
                src = nat if name in ("a.h", "b.h", "m.h") else qi_in if name.endswith("qi") else tmp
                j = job("T." + name)
                for t in range(NT):
                    if name in PARTNER:
                        pe.wait_ge((act_took, dve_took)[t], taken(PARTNER[name], t))
                    elif name.endswith(".qi"):
                        pe.wait_ge(qi_here, 64 * (GATES[name[0]] + 1))
                    else:
                        pe.wait_ge(rows_here, NT * BY_DVE.index(name) + t + 1)
                    for k in range(KB):
                        o = ps[:, 4 * (j % 2) + k // 2, (k % 2) * N + t * P:(k % 2) * N + (t + 1) * P]
                        ins = pe.transpose(o, src[:, t, k * P:(k + 1) * P], ident)
                        if t == NT - 1 and k % 2:
                            ins.then_inc(aux_done, 1)

            j = job("counts")
            def count_tile(k, start, stop):
                for t in range(NT):
                    for h in range(2):
                        ins = pe.matmul(rows(j, t)[:, h, :], oh[:, k, t * P:(t + 1) * P], oh[:, k, N + h * HALF:N + (h + 1) * HALF],
                                        start=start, stop=stop)
                return ins

            def edge_tile(i, q, first=False, last=False):
                s, k = q // GROUP, q % GROUP
                pe.wait_ge(oh_here, i * 6 + (q + 1))
                count_tile(k, first, last).then_inc(aux_done if last else oh_used, 1)
                reached(pe, z_read, i, 6, q - 2)
                if first:
                    pe.wait_ge(w1_split, 1)
                if k == 0:
                    pe.wait_ge(ea_split, i * 2 + (s + 1))
                pe.matmul(ps[:, Z_BANK + k, 0:EW], eap[0:EK, s, k * P:(k + 1) * P], w1p[0:EK], start=True, stop=True).then_inc(z_here, 1)

            for q in range(6):
                edge_tile(0, q, first=q == 0)
            with pe.Fori(1, STEPS - 1) as i:
                for q in range(6):
                    edge_tile(i, q)
            for q in range(6):
                edge_tile(STEPS - 1, q, last=q == 5)
            def queries(i2):
                name = f"qg{i2}"
                open_job(name)
                add_bias(name, picked("bg"))
                batch = slice(i2 * N, (i2 + 1) * N)
                product(unit(name), name, lambda i, kk: (qhi[:, 2 * i + kk, batch], qlo[:, 2 * i + kk, batch]), False, True)

            pe.wait_ge(z_read, TILES)
            pe.wait_ge(set_up, 4)
            pe.wait_ge(bias_here, 1)
            pe.wait_ge(q_lo, KB)
            queries(0)
            queries(1)
            turn_rows("a")

            def turn_counts():
                open_job("countT")
                for dt in range(NT):
                    for k in range(NREL):
                        for st in range(NT):
                            o = flat(job("countT"), 1536)[:, dt * D + k * N + st * P:dt * D + k * N + (st + 1) * P]
                            ins = pe.transpose(o, cT[:, st, k * N + dt * P:k * N + (dt + 1) * P], ident)
                ins.then_inc(aux_done, 1)
                open_job("countrow")
                pe.wait_ge(ones_set, 1)
                s = 4 * (job("countrow") % 2)
                for h in range(2):
                    for t in range(NT):
                        ins = pe.matmul(ps[:, s + h, 0:HALF], onec[:], cT[:, t, h * HALF:(h + 1) * HALF], start=t == 0, stop=t == NT - 1)
                ins.then_inc(aux_done, 1)

            for l, L_ in enumerate("ab"):
                if l:
                    turn_rows("b")
                for k in range(NREL):
                    plain(f"{L_}.rel{k}", L_)
                    if (L_, k) == ("a", 0):
                        turn_counts()
                name = L_ + ".root"
                open_job(name)
                add_bias(name, picked("b1" if l == 0 else "b2"))
                product(unit(name), name, turned(L_), False, False)
                for k in range(NREL):
                    wait_taken(pe, f"{L_}.rel{k}")
                    for st in range(NT):
                        for dt in range(NT):
                            for h in range(2):
                                ins = pe.matmul(rows(job(name), dt)[:, h, :], norm[:, st, k * N + dt * P:k * N + (dt + 1) * P],
                                                xr[:, k, st, h * HALF:(h + 1) * HALF], start=False, stop=k == NREL - 1 and st == NT - 1)
                ins.then_inc(aux_done, 1)
                turn_rows(L_ + ".h")
                plain(L_ + ".hg", L_ + ".h")
                plain(L_ + ".al1", L_ + ".h", "bq")
                wait_taken(pe, L_ + ".al1")

                def add_turn(i, k, a):
                    s = k // PAIRS
                    if k % PAIRS + a == 0:
                        pe.wait_ge(stack_here[s], i * 64 + (256 * l + 64))
                    turns_done(pe, mul_done, i, l, k, a, 0)
                    for h in range(2):
                        ins = pe.matmul(slot(k, a)[:, h], pat[:, k % PAIRS, :], stack[:, s, a, h * HALF:(h + 1) * HALF], start=True, stop=True)
                    ins.then_inc(add_done[turn_of(k, a)[0]], 1)

                def sum_queries(i, k, h):
                    s, jj = k // PAIRS, k % PAIRS
                    if h == 0:
                        pe.wait_ge(sum_done[k % 2], i * 8 + (32 * l + k // 2 + 1))
                        if jj == 0:
                            reached(pe, red_took, i, 2, 8 * l + s - 1)
                    ins = pe.matmul(ps[32 * s:32 * s + 32, 6 + h, 0:HALF], red[:, jj, :], psumm[:, k % 2, h * HALF:(h + 1) * HALF],
                                    start=jj == 0, stop=jj == PAIRS - 1)
                    if h == 1:
                        ins.then_inc(sum_used[k % 2], 1)

                def gate_steps(i, last):
                    for k in range(2 * PAIRS):
                        for a in range(2):
                            if k + LAG < 2 * PAIRS:
                                add_turn(i, k + LAG, a)
                            elif not last:
                                add_turn(i + 1, k + LAG - 2 * PAIRS, a)
                            sum_queries(i, k, a)

                for k in range(LAG):
                    for a in range(2):
                        add_turn(0, k, a)
                gate_steps(0, False)
                with pe.Fori(1, B // 2 - 1) as i:
                    gate_steps(i, False)
                gate_steps(B // 2 - 1, True)
                for s in range(SLOTS):
                    pe.wait_ge(mul_done[s], 4 * (l + 1) * turn_of(s // 2, s % 2)[1])
                pe.wait_ge(red_took, 8 * (l + 1))
                turn_rows(L_ + ".qi")
                product(unit(L_ + ".al2"), L_ + ".al", turned(L_ + ".qi"), True, True)

            for n, name in enumerate(att_names):
                rels, heads = ATT[name]
                turn_rows(name)
                for k in range(rels):
                    plain(f"{name}.{k}", name)

                def row(h):
                    open_job(f"{name}.row{h}")
                    keep_clock(f"{name}.row{h}")
                    if h == 0:
                        wait_dots(pe, name)
                    for k in range(rels):
                        for t in range(NT):
                            ins = pe.matmul(flat(job(f"{name}.row{h}"), D)[:, k * N + t * P:k * N + (t + 1) * P],
                                            sc[:, t, k, heads + h:heads + h + 1].to_broadcast([P, P]), ident, start=True, stop=True)
                    ins.then_inc(aux_done, 1)

                row(0)
                for h in range(heads):
                    if h + 1 < heads:
                        row(h + 1)
                    open_job(f"{name}.pt{h}")
                    keep_clock(f"{name}.pt{h}")
                    pe.wait_ge(pw_here, NT * (heads_before[name] + h + 1))
                    for k in range(2 * rels):
                        for t in range(NT):
                            o = flat(job(f"{name}.pt{h}"), 2 * rels * N)[:, k * N + t * P:k * N + (t + 1) * P]
                            ins = pe.transpose(o, escs[:, h % 2, t, k * P:(k + 1) * P], ident)
                    ins.then_inc(aux_done, 1)
                    open_job(f"{name}.sum{h}")
                    wait_taken(pe, f"{name}.pt{h}")
                    j = job(f"{name}.sum{h}")
                    c = D // heads
                    cuts = [(0, HALF), (HALF, HALF)] if heads == 1 else [(h * c, c)]
                    for t in range(NT):
                        for q, (a, m) in enumerate(cuts):
                            for k in range(2 * rels):
                                ins = pe.matmul(ps[:, 4 * (j % 2) + 2 * t + q, 0:m], pt[:, k, t * P:(t + 1) * P],
                                                xr[:, k // 2, k % 2, a:a + m], start=k == 0, stop=k == 2 * rels - 1)
                    ins.then_inc(aux_done, 1)

            turn_rows("m")
            open_job("m.h")
            add_bias("m.h", lambda t: tyhot[:, t * P:(t + 1) * P])
            for t in range(NTYPE):
                def of_type(i, kk, t=t):
                    if kk == 0:
                        pe.wait_ge(m_here, 2 * PIECES * t + 2 * i + 2)
                    return mhi[:, t % 2, 2 * i + kk], mlo[:, t % 2, 2 * i + kk]
                product(unit(f"ty{t}"), "m.h", of_type, False, t == NTYPE - 1)
            turn_rows("m.h")
            plain("msgA", "m.h")
            plain("msgB", "m.h", "msg_b1")
            wait_taken(pe, "msgB")
            j = job("edges")
            other = 4 * ((j + 1) % 2)

            def place(t, h):
                w = HALF + 2 * h
                return ps[:, 4 * (j % 2) + 2 * t + h, 0:w]

            def gather(i, q):
                m = q % 2
                pe.wait_ge(ohg_here, i * 6 + (q + 1))
                reached(pe, gsum_here, i, 6, q - 1)
                for t in range(NT):
                    for part in range(2):
                        for h in range(2):
                            ins = pe.matmul(ps[:, other + 2 * m + h, 0:HALF], ohg[:, q, t, :], hB[:, t, part, h * HALF:(h + 1) * HALF],
                                            start=t + part == 0, stop=t + part == 2)
                ins.then_inc(gat_done, 1)

            def scatter(i, q, first=False, last=False):
                m = q % 2
                pe.wait_ge(msg_here, i * 6 + (q + 1))
                pe.wait_ge(sew_here, i * 6 + (q + 1))
                for t in range(NT):
                    for part in range(2):
                        for h in range(2):
                            ins = pe.matmul(place(t, h), ohs[:, q, t * P:(t + 1) * P], msg[:, m, part, h * HALF:(h + 1) * HALF + 2 * h],
                                            start=first and part == 0, stop=last and part == 1)
                ins.then_inc(aux_done if last else scat_done, 1)

            def edge_loop(i, first=False, last=False):
                for q in range(2 * GROUP):
                    if q + 2 < 2 * GROUP:
                        gather(i, q + 2)
                    elif not last:
                        gather(i + 1, q + 2 - 2 * GROUP)
                    scatter(i, q, first and q == 0, last and q == 2 * GROUP - 1)

            for q in range(2):
                gather(0, q)
            edge_loop(0, first=True)
            with pe.Fori(1, STEPS - 1) as i:
                edge_loop(i)
            edge_loop(STEPS - 1, last=True)
            turn_rows("agg")
            plain("msg2", "agg")
            turn_rows("msg2")
            plain("agg1", "msg2", "agg_b1")
            turn_rows("agg1")
            plain("agg2", "agg1", "agg_b2")
            turn_rows("agg2")
            plain("out", "agg2", "out_b")


def weight_stack(v):
    wg, wq = v["L0_gnn_Wg"], v["L0_gnn_Wq"]
    out = [wg[:, D:].T] * 2
    for k in (1, 2):
        out += list(v[f"L0_gnn_W_rel{k}"]) + [v[f"L0_gnn_W_root{k}"], wg[:, :D].T, wq[:, :D].T, wq[:, D:].T]
    out += [v["L1_gnn_W1"], v["L1_gnn_W2"], *v["L2_gnn_W1"], *v["L2_gnn_W2"], *v["L3_gnn_W_type"]]
    out += [v["L3_gnn_msg_W1"][:D], v["L3_gnn_msg_W1"][D:]]
    out += [v[f"L3_gnn_{n}"] for n in ("msg_W2", "agg_W1", "agg_W2", "out_W")]
    return np.concatenate(out, axis=0)


def lay_out(v):
    a = {"x": v["x"], "node_type_6": v["node_type_6"], "weights": weight_stack(v), "consts": constants()}
    for n in ("L0_gnn_query_embs", "L3_gnn_edge_W2", "L3_gnn_edge_b2", "L3_gnn_msg_b2", "L3_gnn_ln_g", "L3_gnn_ln_b"):
        a[n] = v[n]
    a["edges"] = np.stack([v["src"], v["dst"], v["edge_type_3"]])
    a["edges_by_tile"] = a["edges"].reshape(3, TILES, P).transpose(2, 0, 1)
    a["codes"] = code_table()
    a["edge_attr_T"] = np.concatenate([v["edge_attr_32"].T] * 3 + [np.ones((2, E), np.float32)])
    w1b = np.concatenate([v["L3_gnn_edge_W1"]] * 3 + [v["L3_gnn_edge_b1"][None]] * 2)
    a["edge_w1b"] = np.concatenate([w1b, np.zeros((EK, EW - H4), np.float32)], axis=1)
    q = v["L0_gnn_query_embs"].reshape(B, HL, 2, D).transpose(3, 0, 2, 1)
    a["query_T"] = q.reshape(D, B * L)
    stack = np.zeros((P, D), np.float32)
    names = ["L0_gnn_b1", "L0_gnn_b2", "L0_gnn_bg", "L0_gnn_bq", "L3_gnn_msg_b1", "L3_gnn_agg_b1", "L3_gnn_agg_b2", "L3_gnn_out_b"]
    for half in (0, 64):
        for i, n in enumerate(names):
            stack[half + i] = v[n]
        stack[half + TYPE_ROW:half + TYPE_ROW + NTYPE] = v["L3_gnn_b_type"]
    a["biases"] = stack
    a["att_gat1"] = np.stack([v["L1_gnn_att_dst1"], v["L1_gnn_att_src1"]])
    a["att_gat2"] = np.stack([v["L1_gnn_att_dst2"], v["L1_gnn_att_src2"]])
    a["att_rgat1"] = np.concatenate([v["L2_gnn_q1"].T, v["L2_gnn_k1"].T])
    a["att_rgat2"] = np.concatenate([v["L2_gnn_q2"].T, v["L2_gnn_k2"].T])
    for n, b in (("gat1", "L1_gnn_b1"), ("gat2", "L1_gnn_b2"), ("rgat1", "L2_gnn_b1"), ("rgat2", "L2_gnn_b2")):
        a["bias_" + n] = v[b]
    return {k: np.ascontiguousarray(t) for k, t in a.items()}


def program(nc, arrays):
    d = {}
    for name, a in arrays.items():
        d[name] = nc.dram_tensor("in_" + name, a.shape, mybir.dt.from_np(a.dtype), kind="ExternalInput").ap()
    d["out"] = nc.dram_tensor("out_x", (N, D), F32, kind="ExternalOutput").ap()
    d["hg_parts"] = nc.dram_tensor("hg_parts", (2, N, D), F32).ap()
    d["qg_parts"] = nc.dram_tensor("qg_parts", (2, B * L, D), F32).ap()
    d["hA"] = nc.dram_tensor("hA_rows", (N, D), F32).ap()
    d["qi"] = nc.dram_tensor("qi_rows", (N, D), F32).ap()
    build(nc, d)


def kernel(**inputs):
    import concourse.bacc as bacc
    from concourse.bass_utils import run_bass_kernel_spmd

    v = {k: np.asarray(a) for k, a in inputs.items()}
    arrays = lay_out(v)
    nc = bacc.Bacc("TRN2", target_bir_lowering=False, num_devices=1)
    program(nc, arrays)
    got = run_bass_kernel_spmd(nc, [{"in_" + k: a for k, a in arrays.items()}], core_ids=[0])
    return got.results[0]["out_x"]
```
